# Optimizing a Trainium2 kernel written in Bass

```python
import numpy as np
import jax
import jax.numpy as jnp

def _softmax(x, axis=-1):
    return jax.nn.softmax(x, axis=axis)

def _gelu(x):
    return jax.nn.gelu(x, approximate=True)

def _silu(x):
    return jax.nn.silu(x)

def _sigmoid(x):
    return jax.nn.sigmoid(x)

def _layernorm(x, axis=-1, eps=1e-05):
    m = jnp.mean(x, axis=axis, keepdims=True)
    v = jnp.var(x, axis=axis, keepdims=True)
    return (x - m) / jnp.sqrt(v + eps)

def _scatter_add(tgt, idx, src, axis=0):
    return tgt.at[idx].add(src)

def _segment_sum(src, seg, n):
    return jax.ops.segment_sum(src, seg, n)
kernel_name = 'mk_gps_d1_gnn_r8_a27c6f'

def setup_inputs(seed: int=0):
    np.random.seed(seed)
    _w = jnp.asarray

    def _rec_inputs():
        import jax
        import jax.numpy as jnp
        _gk = jax.random.key(seed)
        x = -0.0002117 + 1 * jax.random.normal(jax.random.fold_in(_gk, 1), (12500, 256), jnp.float32)
        _s = jax.random.randint(jax.random.fold_in(_gk, 2), (100000,), 0, 12500, jnp.int32)
        _d = jax.random.randint(jax.random.fold_in(_gk, 3), (100000,), 0, 12500, jnp.int32)
        _loop = jnp.arange(12500, dtype=jnp.int32)
        src = jnp.concatenate([_s, _d, _loop])
        dst = jnp.concatenate([_d, _s, _loop])
        _o = jnp.argsort(dst, stable=True)
        src = src[_o]
        dst = dst[_o]
        edge_weight = jax.random.uniform(jax.random.fold_in(_gk, 12), (212500,), jnp.float32, 0.0, 1)
        return (x, src, dst, edge_weight)
    x, src, dst, edge_weight = _rec_inputs()

    def _L0_gnn_setup():
        import jax, jax.numpy as jnp
        import numpy as np
        N_NODES = 12500
        N_EDGES = 400000
        NFEAT = 256
        NHID = 256

        def _gcn_layer(x, W, b, edge_weight, edge_src, edge_dst):
            support = x @ W
            msgs = support[edge_src] * edge_weight[:, None]
            agg = jax.ops.segment_sum(msgs, edge_dst, num_segments=N_NODES)
            return agg + b
        key = jax.random.key(seed)
        ks = jax.random.split(key, 8)
        x = jax.random.normal(ks[0], (N_NODES, NFEAT), dtype=jnp.float32)
        W1 = jax.random.normal(ks[1], (NFEAT, NHID), dtype=jnp.float32) / np.sqrt(NFEAT)
        b1 = jax.random.normal(ks[2], (NHID,), dtype=jnp.float32) * 0.01
        W2 = jax.random.normal(ks[3], (NHID, NHID), dtype=jnp.float32) / np.sqrt(NHID)
        b2 = jax.random.normal(ks[4], (NHID,), dtype=jnp.float32) * 0.01
        edge_weight = jax.random.uniform(ks[5], (N_EDGES,), dtype=jnp.float32)
        edge_src = jax.random.randint(ks[6], (N_EDGES,), 0, N_NODES, dtype=jnp.int32)
        edge_dst = jax.random.randint(ks[7], (N_EDGES,), 0, N_NODES, dtype=jnp.int32)
        return {'x': x, 'W1': W1, 'b1': b1, 'W2': W2, 'b2': b2, 'edge_weight': edge_weight, 'edge_src': edge_src, 'edge_dst': edge_dst}
    _L0_gnn_all = _L0_gnn_setup()
    _L0_gnn_in = {k: v for k, v in _L0_gnn_all.items() if k in ('W1', 'b1', 'W2', 'b2')}
    del _L0_gnn_all

    def _L0_mix_setup():
        import jax, jax.numpy as jnp
        import numpy as np
        NHEAD = 8
        ATT_EPS = 1e-06
        LN_EPS = 1e-05

        def _layernorm(x, g, b):
            mu = jnp.mean(x, axis=-1, keepdims=True)
            var = jnp.mean(jnp.square(x - mu), axis=-1, keepdims=True)
            return (x - mu) * jax.lax.rsqrt(var + LN_EPS) * g + b
        key = jax.random.key(seed)
        ks = jax.random.split(key, 7)
        N, L, C = (4, 2048, 256)
        s = 1.0 / np.sqrt(C)
        return {'x': jax.random.normal(ks[0], (N, L, C), jnp.float32), 'Wq': jax.random.normal(ks[1], (C, C), jnp.float32) * s, 'Wk': jax.random.normal(ks[2], (C, C), jnp.float32) * s, 'Wv': jax.random.normal(ks[3], (C, C), jnp.float32) * s, 'Wm': jax.random.normal(ks[4], (C, C), jnp.float32) * s, 'W1': jax.random.normal(ks[5], (2 * C, 2 * C), jnp.float32) * (1.0 / np.sqrt(2 * C)), 'W2': jax.random.normal(ks[6], (2 * C, C), jnp.float32) * (1.0 / np.sqrt(2 * C)), 'g1': jnp.ones((C,), jnp.float32), 'b1': jnp.zeros((C,), jnp.float32), 'g2': jnp.ones((C,), jnp.float32), 'b2': jnp.zeros((C,), jnp.float32)}
    _L0_mix_all = _L0_mix_setup()
    _L0_mix_in = {k: v for k, v in _L0_mix_all.items() if k in ('Wq', 'Wk', 'Wv', 'Wm', 'W1', 'W2', 'g1', 'b1', 'g2', 'b2')}
    del _L0_mix_all

    def _L0_ffn_setup():
        import math
        import jax, jax.numpy as jnp
        import numpy as np
        CAPACITY_FACTOR = 1.25
        key = jax.random.key(seed)
        ks = jax.random.split(key, 5)
        B, L, D, F, E = (8, 1024, 256, 1024, 8)
        h = jax.random.normal(ks[0], (B, L, D), dtype=jnp.float32)
        gate_w = jax.random.normal(ks[1], (D, E), dtype=jnp.float32) * 0.02
        gate_b = jnp.zeros((E,), dtype=jnp.float32)
        w1 = jax.random.normal(ks[2], (E, D, F), dtype=jnp.float32) * (1.0 / math.sqrt(D))
        b1 = jnp.zeros((E, F), dtype=jnp.float32)
        w2 = jax.random.normal(ks[3], (E, F, D), dtype=jnp.float32) * (1.0 / math.sqrt(F))
        b2 = jnp.zeros((E, D), dtype=jnp.float32)
        return {'h': h, 'gate_w': gate_w, 'gate_b': gate_b, 'w1': w1, 'b1': b1, 'w2': w2, 'b2': b2}
    _L0_ffn_all = _L0_ffn_setup()
    _L0_ffn_in = {k: v for k, v in _L0_ffn_all.items() if k in ('gate_w', 'gate_b', 'w1', 'b1', 'w2', 'b2')}
    del _L0_ffn_all
    return {'x': x, 'src': src, 'dst': dst, 'edge_weight': edge_weight, 'L0_gnn_W1': _L0_gnn_in['W1'], 'L0_gnn_b1': _L0_gnn_in['b1'], 'L0_gnn_W2': _L0_gnn_in['W2'], 'L0_gnn_b2': _L0_gnn_in['b2'], 'L0_mix_Wq': _L0_mix_in['Wq'], 'L0_mix_Wk': _L0_mix_in['Wk'], 'L0_mix_Wv': _L0_mix_in['Wv'], 'L0_mix_Wm': _L0_mix_in['Wm'], 'L0_mix_W1': _L0_mix_in['W1'], 'L0_mix_W2': _L0_mix_in['W2'], 'L0_mix_g1': _L0_mix_in['g1'], 'L0_mix_b1': _L0_mix_in['b1'], 'L0_mix_g2': _L0_mix_in['g2'], 'L0_mix_b2': _L0_mix_in['b2'], 'L0_ffn_gate_w': _L0_ffn_in['gate_w'], 'L0_ffn_gate_b': _L0_ffn_in['gate_b'], 'L0_ffn_w1': _L0_ffn_in['w1'], 'L0_ffn_b1': _L0_ffn_in['b1'], 'L0_ffn_w2': _L0_ffn_in['w2'], 'L0_ffn_b2': _L0_ffn_in['b2']}

def reference(x, src, dst, edge_weight, L0_gnn_W1, L0_gnn_b1, L0_gnn_W2, L0_gnn_b2, L0_mix_Wq, L0_mix_Wk, L0_mix_Wv, L0_mix_Wm, L0_mix_W1, L0_mix_W2, L0_mix_g1, L0_mix_b1, L0_mix_g2, L0_mix_b2, L0_ffn_gate_w, L0_ffn_gate_b, L0_ffn_w1, L0_ffn_b1, L0_ffn_w2, L0_ffn_b2):
    import jax
    import jax.numpy as jnp

    def _L0_gnn_ref(x, W1, b1, W2, b2, edge_weight, edge_src, edge_dst):
        import jax, jax.numpy as jnp
        import numpy as np
        N_NODES = 12500
        N_EDGES = 400000
        NFEAT = 256
        NHID = 256

        def _gcn_layer(x, W, b, edge_weight, edge_src, edge_dst):
            support = x @ W
            msgs = support[edge_src] * edge_weight[:, None]
            agg = jax.ops.segment_sum(msgs, edge_dst, num_segments=N_NODES)
            return agg + b
        h = jax.nn.elu(_gcn_layer(x, W1, b1, edge_weight, edge_src, edge_dst))
        h = jax.nn.elu(_gcn_layer(h, W2, b2, edge_weight, edge_src, edge_dst))
        return h

    def _L0_mix_ref(x, Wq, Wk, Wv, Wm, W1, W2, g1, b1, g2, b2):
        import jax, jax.numpy as jnp
        import numpy as np
        NHEAD = 8
        ATT_EPS = 1e-06
        LN_EPS = 1e-05

        def _layernorm(x, g, b):
            mu = jnp.mean(x, axis=-1, keepdims=True)
            var = jnp.mean(jnp.square(x - mu), axis=-1, keepdims=True)
            return (x - mu) * jax.lax.rsqrt(var + LN_EPS) * g + b
        N, L, C = x.shape
        H = NHEAD
        D = C // H
        q = (x @ Wq).reshape(N, L, H, D)
        k = (x @ Wk).reshape(N, L, H, D)
        v = (x @ Wv).reshape(N, L, H, D)
        Q = jax.nn.elu(q) + 1.0
        K = jax.nn.elu(k) + 1.0
        v = v / L
        KV = jnp.einsum('nshd,nshv->nhdv', K, v)
        Z = 1.0 / (jnp.einsum('nlhd,nhd->nlh', Q, K.sum(axis=1)) + ATT_EPS)
        msg = jnp.einsum('nlhd,nhdv,nlh->nlhv', Q, KV, Z) * L
        msg = msg.reshape(N, L, C) @ Wm
        msg = _layernorm(msg, g1, b1)
        h = jnp.concatenate([x, msg], axis=-1) @ W1
        h = jax.nn.relu(h) @ W2
        msg = _layernorm(h, g2, b2)
        return x + msg

    def _L0_ffn_ref(h, gate_w, gate_b, w1, b1, w2, b2):
        import math
        import jax, jax.numpy as jnp
        import numpy as np
        CAPACITY_FACTOR = 1.25
        B, L, D = h.shape
        E = gate_w.shape[1]
        T = B * L
        C = max(1, math.ceil(CAPACITY_FACTOR * T / E))
        x = h.reshape(T, D)
        logits = x @ gate_w + gate_b
        probs = jax.nn.softmax(logits, axis=-1)
        idx = jnp.argmax(probs, axis=-1)
        prb = jnp.take_along_axis(probs, idx[:, None], axis=1)[:, 0]
        one_hot = jax.nn.one_hot(idx, E, dtype=jnp.float32)
        pos = (jnp.cumsum(one_hot, axis=0) * one_hot).sum(-1).astype(jnp.int32) - 1
        kept = pos < C
        pos_safe = jnp.where(kept, pos, C)
        buf = jnp.zeros((E, C, D), dtype=h.dtype).at[idx, pos_safe].set(x, mode='drop')
        hmid = jax.nn.relu(jnp.einsum('ecd,edf->ecf', buf, w1) + b1[:, None, :])
        ybuf = jnp.einsum('ecf,efd->ecd', hmid, w2) + b2[:, None, :]
        pos_g = jnp.minimum(pos, C - 1)
        y_tok = ybuf[idx, pos_g] * (prb * kept)[:, None]
        y = y_tok.reshape(B, L, D)
        y = jnp.nan_to_num(y, nan=0.0, posinf=10000.0, neginf=-10000.0)
        return y
    xn = _layernorm(x, axis=-1)
    x = x + _L0_gnn_ref(xn, L0_gnn_W1, L0_gnn_b1, L0_gnn_W2, L0_gnn_b2, edge_weight, src, dst) + _L0_mix_ref(xn[None], L0_mix_Wq, L0_mix_Wk, L0_mix_Wv, L0_mix_Wm, L0_mix_W1, L0_mix_W2, L0_mix_g1, L0_mix_b1, L0_mix_g2, L0_mix_b2)[0]
    x = x + _L0_ffn_ref(_layernorm(x, axis=-1)[None], L0_ffn_gate_w, L0_ffn_gate_b, L0_ffn_w1, L0_ffn_b1, L0_ffn_w2, L0_ffn_b2)[0]
    return x

_drawn_inputs = setup_inputs


def setup_inputs(seed=0):
    import zlib

    import numpy as np

    out = dict(_drawn_inputs(seed))
    spreads = {'L0_mix_g1': (1.0, 0.596),
     'L0_mix_b1': (0.0, 0.616),
     'L0_mix_g2': (1.0, 0.2),
     'L0_mix_b2': (0.0, 0.449),
     'L0_ffn_gate_b': (0.0, 0.491),
     'L0_ffn_b1': (0.0, 0.8),
     'L0_ffn_b2': (0.0, 0.8)}
    factors = {'L0_gnn_b1': 7.97,
     'L0_gnn_b2': 8.0,
     'L0_ffn_gate_w': 2.994,
     'L0_ffn_w1': 3.305,
     'L0_ffn_w2': 2.732}
    for name, (base, spread) in spreads.items():
        noise = np.random.default_rng([zlib.crc32(name.encode()), seed]).standard_normal(out[name].shape)
        drawn = base * np.exp(spread * noise) if base else spread * noise
        out[name] = jnp.asarray(drawn.astype(out[name].dtype))
    for name, factor in factors.items():
        out[name] = (out[name] * factor).astype(out[name].dtype)
    return out
```

```python
import concourse.bass as bass
from concourse import mybir
from contextlib import ExitStack
import numpy as np

F32 = mybir.dt.float32
I32 = mybir.dt.int32
U32 = mybir.dt.uint32
U8 = mybir.dt.uint8
ALU = mybir.AluOpType
ACT = mybir.ActivationFunctionType
AX = mybir.AxisListType

P = 128
N = 12500
D = 256
KD = D // P
E = 212500
GROUP = 8
TURN = 2
SLOTS = GROUP * TURN
TURNS = -(-E // (P * SLOTS))
NCH = TURNS * SLOTS
NT = TURNS
NP = NT * P
WIN = 128
AGG = NP + WIN
LN_EPS = 1e-5
ATT_EPS = 1e-6
H = 8
HC = P // (D // H)
HD = D // H
KVW = P + HC
BANK = 512
KVS = P + 1
F1 = 512
NE = 8
F = 1024
FC = F // P
CAP = -(-5 * N // (4 * NE))
ROWS = -(-CAP // P) * P
TB = 256
TRASH = NE * ROWS
PB = 4
PSLOTS = 2
DT = 4
TABLES = "natural_log_exp_and_others"
LOG_WIN = 7
LOG_TB = 8
assert 1 << LOG_WIN == WIN and 1 << LOG_TB == TB and NP >= N and TURNS % 2 == 0 and NT % (PB * PSLOTS) == 0 and NT % DT == 0


def wait_apart(engine, semaphore, value, passed):
    engine.wait_ge(semaphore, value)
    engine.sem_inc(passed, 1)


def semaphores(nc, ctx, suffix=""):
    taken = []

    def sem(name):
        taken.append(nc.alloc_semaphore(name=f"{name}{suffix}"))
        return taken[-1]

    def clear():
        nc.clear_and_free_semaphores(taken)
        nc.all_engine_barrier()

    ctx.callback(clear)
    return sem


class Memory:
    pass


def prepare(nc, m):
    with ExitStack() as ctx:
        def sb(name, shape, dt):
            return ctx.enter_context(nc.sbuf_tensor(name, shape, dt))

        sem = semaphores(nc, ctx)

        rows = sb("ln_rows", [P, PSLOTS, PB, D], F32)
        normed = sb("ln_normed", [P, PSLOTS, PB, D], F32)
        stats = sb("ln_stats", [P, PSLOTS, PB, 6], F32)
        mv = sb("ln_mean_var", [P, PSLOTS, PB, 2], F32)
        sd = sb("ln_sd", [P, PSLOTS, PB], F32)
        rstd = sb("ln_rstd", [P, PSLOTS, PB], F32)
        dst_rows = sb("dst_rows", [TURNS, TURN, GROUP * P], I32)
        low = sb("low", [TURNS, TURN], I32)
        high = sb("high", [TURNS, TURN], I32)
        span = sb("span", [TURNS, TURN], I32)
        more = sb("more", [TURNS, 1], I32)
        dst_i = sb("dst_i", [P, NCH], I32)
        dst_f = sb("dst_f", [P, NCH], F32)
        low_all = sb("low_all", [P, TURNS * TURN], I32)
        low_f = sb("low_f", [P, TURNS * TURN], F32)
        more_row = sb("more_row", [1, TURNS], I32)
        more_f = sb("more_f", [1, TURNS], F32)
        more_sum = sb("more_sum", [1, TURNS], F32)
        more_one = sb("more_one", [1, TURNS], F32)
        iota_i = sb("iota_i", [P, WIN], I32)
        node_i = sb("node_i", [P, NT], I32)

        consts_loaded = sem("consts_loaded")
        edges_loaded = sem("edges_loaded")
        x_loaded = [sem(f"x_loaded{s}") for s in range(PSLOTS)]
        mv_done = sem("mean_var_done")
        sd_done = sem("sd_done")
        eps_set = sem("eps_set")
        rstd_done = sem("rstd_done")
        xn_done = sem("xn_done")
        xn_stored = [sem(f"xn_stored{s}") for s in range(PSLOTS)]
        step = sem("prepare_step")
        spans_done = sem("spans_done")
        spans_stored = sem("spans_stored")
        spans_back = sem("spans_back")
        iotas_done = sem("iotas_done")
        tables_done = sem("tables_done")
        zero_set = sem("zero_set")
        pad_stored = sem("pad_stored")

        x_blocks = m.x.rearrange("(b p j) f -> b p j f", p=P, j=PB)
        xn_blocks = m.xn[0:NP, :].rearrange("(b p j) f -> b p j f", p=P, j=PB)
        n_blocks = NT // PB
        loops = n_blocks // PSLOTS
        consts = [
            (m.w_q[:, :, :], m.in_w_q.rearrange("(k p) n -> p k n", p=P)),
            (m.w_m[:, :, :], m.in_w_m.rearrange("(k p) n -> p k n", p=P)),
            (m.w_g2[:, :, :], m.in_w_g2.rearrange("(k p) n -> p k n", p=P)),
            (m.w_1[:, :, :], m.in_w_1.rearrange("(k p) n -> p k n", p=P)),
            (m.w_2[:, :, :], m.in_w_2.rearrange("(k p) n -> p k n", p=P)),
            (m.b_g1[:, :], m.in_b_g1.rearrange("(o n) -> o n", o=1)),
            (m.b_g2[:, :], m.in_b_g2.rearrange("(o n) -> o n", o=1)),
            (m.ln1_gh[:, :], m.in_ln1_g),
            (m.ln1_b[:, :], m.in_ln1_b),
            (m.ln2_gh[:, :], m.in_ln2_g.rearrange("(o n) -> o n", o=1).to_broadcast([P, D])),
            (m.ln2_b[:, :], m.in_ln2_b.rearrange("(o n) -> o n", o=1).to_broadcast([P, D])),
            (m.gate_w[:, :, :], m.in_gate_w.rearrange("(k p) n -> p k n", p=P)),
            (m.gate_b[:, :], m.in_gate_b.rearrange("(o n) -> o n", o=1).to_broadcast([P, NE])),
            (m.wgt[:, 0:NCH], m.in_wgt),
        ]

        with nc.Block("prepare") as block:
            @block.sync
            def _(sp):
                sp.dma_start(dst_rows[:, :, :],
                             m.in_dst_rows.rearrange("t (g e) -> t g e", g=TURN)).then_inc(edges_loaded, 16)
                sp.dma_start(dst_i[:, :], m.in_dst).then_inc(edges_loaded, 16)
                for s in range(PSLOTS):
                    sp.dma_start(rows[:, s, :, :], x_blocks[s]).then_inc(x_loaded[s], 16)
                with sp.Fori(1, loops) as i:
                    for s in range(PSLOTS):
                        sp.wait_ge(xn_done, i * PSLOTS + (s + 1 - PSLOTS))
                        sp.dma_start(rows[:, s, :, :],
                                     x_blocks[bass.ds(i * PSLOTS + s, 1)].rearrange("b p j f -> (b p) j f")
                                     ).then_inc(x_loaded[s], 16)
                for to, of in consts:
                    sp.dma_start(to, of).then_inc(consts_loaded, 16)
                sp.wait_ge(spans_done, 2)
                sp.dma_start(m.low_dram[:, :], low[:, :]).then_inc(spans_stored, 16)
                sp.dma_start(m.more_dram[:, :], more[:, :]).then_inc(spans_stored, 16)
                sp.wait_ge(spans_stored, 32)
                sp.dma_start(low_all[:, :],
                             m.low_dram.rearrange("(o t) g -> o (t g)", o=1).to_broadcast([P, TURNS * TURN])
                             ).then_inc(spans_back, 16)
                sp.dma_start(m.table[0:1, :, 0:TURN],
                             m.low_dram.rearrange("(o t) g -> o t g", o=1)).then_inc(spans_back, 16)
                sp.dma_start(more_row[:, :],
                             m.more_dram.rearrange("(o t) g -> o (t g)", o=1)).then_inc(spans_back, 16)
                sp.wait_ge(consts_loaded, 16 * len(consts))

            @block.scalar
            def _(act):
                def store(i, s):
                    act.wait_ge(xn_done, i * PSLOTS + s + 1)
                    act.dma_start(xn_blocks[bass.ds(i * PSLOTS + s, 1)].rearrange("b p j f -> (b p) j f"),
                                  normed[:, s, :, :]).then_inc(xn_stored[s], 16)

                act.wait_ge(eps_set, 1)
                with act.Fori(0, loops) as i:
                    for s in range(PSLOTS):
                        act.wait_ge(mv_done, i * PSLOTS + s + 1)
                        nc.scalar.activation(sd[:, s, :], mv[:, s, :, 1], ACT.Sqrt,
                                             bias=m.eps[:, 0:1]).then_inc(sd_done, 1)
                        if s:
                            store(i, s - 1)
                    store(i, PSLOTS - 1)
                act.wait_ge(zero_set, 1)
                act.dma_start(m.xn[NP:NP + P, :], m.zeros[:, 0:D]).then_inc(pad_stored, 16)
                for buffer in (m.xe, m.ye):
                    act.dma_start(buffer.rearrange("(p n) f -> p n f", p=P),
                                  m.zeros[:, 0:D].rearrange("p (o f) -> p o f", o=1)
                                  .to_broadcast([P, buffer.shape[0] // P, D])).then_inc(m.buffers_zeroed, 16)
                act.wait_ge(pad_stored, 16)
                for s in range(PSLOTS):
                    act.wait_ge(xn_stored[s], 16 * loops)

            @block.gpsimd
            def _(pool):
                nc.gpsimd.memset(m.zeros[:, :], 0.0).then_inc(zero_set, 1)
                nc.gpsimd.memset(m.ones[:, :], 1.0).then_inc(zero_set, 1)
                nc.gpsimd.iota(iota_i[:, :], [[1, WIN]], base=0, channel_multiplier=0).then_inc(iotas_done, 1)
                nc.gpsimd.iota(node_i[:, :], [[P, NT]], base=0, channel_multiplier=1).then_inc(iotas_done, 1)
                pool.wait_ge(zero_set, 2)
                nc.gpsimd.affine_select(out=m.ident[:, :], in_=m.zeros[:, 0:P], compare_op=ALU.not_equal, fill=1.0,
                                        base=0, pattern=[[-1, P]], channel_multiplier=1).then_inc(iotas_done, 1)
                nc.gpsimd.affine_select(out=m.upto[:, :], in_=m.ones[:, :], compare_op=ALU.is_ge, fill=0.0,
                                        base=0, pattern=[[1, P]], channel_multiplier=-1).then_inc(iotas_done, 1)

            @block.vector
            def _(dve):
                nc.vector.memset(m.eps[:, :], LN_EPS).then_inc(eps_set, 1)
                dve.wait_ge(edges_loaded, 32)
                nc.vector.tensor_reduce(low[:, :], dst_rows[:, :, :], AX.X, ALU.min).then_inc(spans_done, 1)
                nc.vector.tensor_reduce(high[:, :], dst_rows[:, :, :], AX.X, ALU.max).then_inc(step, 1)
                nc.vector.tensor_copy(dst_f[:, :], dst_i[:, :]).then_inc(step, 1)
                dve.wait_ge(step, 2)
                nc.vector.tensor_tensor(span[:, :], high[:, :], low[:, :], ALU.subtract).then_inc(step, 1)
                dve.wait_ge(step, 3)
                nc.vector.tensor_scalar(high[:, :], span[:, :], LOG_WIN, None,
                                        ALU.arith_shift_right).then_inc(step, 1)
                dve.wait_ge(step, 4)
                nc.vector.tensor_reduce(more[:, :], high[:, :], AX.X, ALU.max).then_inc(spans_done, 1)
                stat_steps = 5

                def turn(i, s, first):
                    dve.wait_ge(x_loaded[s], 16 * i + 16)
                    for j in range(PB):
                        last = nc.vector.bn_stats(stats[:, s, j, :], rows[:, s, j, :])
                    last.then_inc(step, 1)
                    wait_apart(dve, step, i * PSLOTS + (s + stat_steps), m.passed)
                    for j in range(PB):
                        last = nc.vector.bn_aggr(mv[:, s, j, :], stats[:, s, j, :])
                    last.then_inc(mv_done, 1)
                    dve.wait_ge(sd_done, i * PSLOTS + s + 1)
                    nc.vector.reciprocal(rstd[:, s, :], sd[:, s, :]).then_inc(rstd_done, 1)
                    dve.wait_ge(rstd_done, i * PSLOTS + s + 1)
                    if not first:
                        dve.wait_ge(xn_stored[s], 16 * i)
                    for j in range(PB):
                        last = nc.vector.tensor_scalar(normed[:, s, j, :], rows[:, s, j, :], mv[:, s, j, 0:1],
                                                       rstd[:, s, j:j + 1], ALU.subtract, ALU.mult)
                    last.then_inc(xn_done, 1)

                for s in range(PSLOTS):
                    turn(0, s, True)
                with dve.Fori(1, loops) as i:
                    for s in range(PSLOTS):
                        turn(i, s, False)
                dve.wait_ge(iotas_done, 4)
                nc.vector.tensor_copy(m.cols[:, :], iota_i[:, :]).then_inc(tables_done, 1)
                nc.vector.tensor_scalar(m.valid[:, :], node_i[:, :], float(N), None, ALU.is_lt).then_inc(tables_done, 1)
                dve.wait_ge(spans_back, 48)
                nc.vector.tensor_copy(low_f[:, :], low_all[:, :]).then_inc(tables_done, 1)
                nc.vector.tensor_copy(more_f[:, :], more_row[:, :]).then_inc(tables_done, 1)
                nc.vector.memset(more_one[:, :], 1.0).then_inc(tables_done, 1)
                dve.wait_ge(tables_done, 5)
                nc.vector.tensor_tensor(m.dst_rel[:, 0:NCH].rearrange("p (g c) -> p g c", c=GROUP),
                                        dst_f[:, :].rearrange("p (g c) -> p g c", c=GROUP),
                                        low_f[:, :].rearrange("p (g o) -> p g o", o=1)
                                        .to_broadcast([P, TURNS * TURN, GROUP]), ALU.subtract).then_inc(tables_done, 1)
                nc.vector.tensor_tensor_scan(more_sum[:, :], more_one[:, :], more_f[:, :], 0.0,
                                             ALU.mult, ALU.add).then_inc(tables_done, 1)
                dve.wait_ge(tables_done, 7)
                nc.vector.tensor_copy(m.table[0:1, :, TURN + 1], more_sum[:, :]).then_inc(tables_done, 1)
                nc.vector.tensor_tensor(m.table[0:1, :, TURN], more_sum[:, :], more_f[:, :],
                                        ALU.subtract).then_inc(tables_done, 1)
                nc.vector.memset(m.dst_rel[:, NCH:NCH + SLOTS], 0.0).then_inc(tables_done, 1)
                nc.vector.memset(m.wgt[:, NCH:NCH + SLOTS], 0.0).then_inc(tables_done, 1)
                dve.wait_ge(consts_loaded, 16 * len(consts))
                nc.vector.tensor_scalar(m.ln1_gh[:, :], m.ln1_gh[:, :], -0.5, None, ALU.mult).then_inc(tables_done, 1)
                nc.vector.tensor_scalar(m.ln2_gh[:, :], m.ln2_gh[:, :], -0.5, None, ALU.mult).then_inc(tables_done, 1)
                dve.wait_ge(tables_done, 13)


def gather(nc, m, layer, source, mixer):
    with ExitStack() as ctx:
        def sb(name, shape, dt=F32):
            return ctx.enter_context(nc.sbuf_tensor(f"{name}{layer}", shape, dt))

        sem = semaphores(nc, ctx, layer)

        def ps(name, a, b):
            bank = ctx.enter_context(nc.psum_tensor(f"{name}{layer}", [P, BANK], F32))
            return bank[:, 0:a * b].rearrange("p (a b) -> p a b", a=a)

        rows = sb("rows", [P, 2, SLOTS, D])
        sel = sb("sel", [P, SLOTS, WIN])
        idx = sb("idx", [P, 2, SLOTS], I32)
        rel_now = sb("rel_now", [P, SLOTS])
        wgt_now = sb("wgt_now", [P, SLOTS])
        sums = [ps(f"sums{g}_", KD, WIN) for g in range(TURN)]

        idx_loaded = [sem(f"idx_loaded{u}_") for u in range(2)]
        rows_loaded = [[sem(f"rows_loaded{u}{g}_") for g in range(TURN)] for u in range(2)]
        rows_used = [sem(f"rows_used{u}_") for u in range(2)]
        sel_ready = [sem(f"sel_ready{g}_") for g in range(TURN)]
        summed = [sem(f"summed{g}_") for g in range(TURN)]
        now_ready = sem("now_ready")
        added = sem("added")
        agg_zeroed = sem("agg_zeroed")
        further_sel = sem("further_sel")
        further_sum = sem("further_sum")
        further_step = sem("further_step")

        mix = mixer(nc, m, sb, sem, ps)
        loops = TURNS // 2

        def window_products(g, h, u, before):
            for c in range(GROUP):
                k = g * GROUP + c
                last = nc.tensor.matmul(sums[g][:, h, :], rows[:, u, k, h * P:(h + 1) * P], sel[:, k, :],
                                        start=(c == 0), stop=(c == GROUP - 1))
                if c == 0 and before is not None:
                    last.then_inc(before, 1)
            return last

        def selection(g):
            for c in range(GROUP):
                k = g * GROUP + c
                last = nc.vector.tensor_scalar(sel[:, k, :], m.cols[:, :], rel_now[:, k:k + 1], wgt_now[:, k:k + 1],
                                               ALU.is_equal, ALU.mult)
            return last

        def add_window(g, at):
            window = m.agg[:, :, bass.ds(at, WIN)]
            return nc.vector.tensor_tensor(window, window, sums[g][:, :, :], ALU.add)

        def turns(engine, body):
            for u in range(2):
                body(0, u)
            with engine.Fori(1, loops) as i:
                for u in range(2):
                    body(i, u)

        with nc.Block(f"gather{layer}") as block:
            @block.sync
            def _(sp):
                for u in range(2):
                    sp.dma_start(idx[:, u, :], m.in_src[u]).then_inc(idx_loaded[u], 16)
                    mix.load(sp, u, u)
                mix.load_weights(sp)
                with sp.Fori(1, loops) as i:
                    for u in range(2):
                        sp.wait_ge(rows_loaded[u][TURN - 1], 16 * GROUP * i)
                        sp.dma_start(idx[:, u, :], m.in_src[bass.ds(2 * i + u, 1)].rearrange("o p c -> (o p) c")
                                     ).then_inc(idx_loaded[u], 16)
                        mix.free(sp, i - 1, u)
                        mix.load(sp, 2 * i + u, u)
                        mix.store(sp, i - 1, u)
                mix.load_past(sp)
                mix.stored(sp)
                sp.wait_ge(m.buffers_zeroed, 32)

            @block.gpsimd
            def _(pool):
                with pool.Fori(0, loops) as i:
                    for u in range(2):
                        pool.wait_ge(idx_loaded[u], 16 * i + 16)
                        wait_apart(pool, rows_used[u], i + 1, m.pool_passed)
                        for k in range(SLOTS):
                            nc.gpsimd.indirect_dma_start(
                                out=rows[:, u, k, :], out_offset=None, in_=source,
                                in_offset=bass.IndirectOffsetOnAxis(ap=idx[:, u, k:k + 1], axis=0)
                            ).then_inc(rows_loaded[u][k // GROUP], 16)

            @block.vector
            def _(dve):
                def take(t):
                    nc.vector.tensor_copy(rel_now[:, :], m.dst_rel[:, bass.ds(t * SLOTS, SLOTS)]).then_inc(now_ready, 1)
                    nc.vector.tensor_copy(wgt_now[:, :], m.wgt[:, bass.ds(t * SLOTS, SLOTS)]).then_inc(now_ready, 1)
                    dve.wait_ge(now_ready, 2 * t + 2)
                    selection(0).then_inc(sel_ready[0], 1)

                nc.vector.memset(m.agg[:, :, :], 0.0).then_inc(agg_zeroed, 1)
                mix.dve_begin(dve)
                dve.wait_ge(agg_zeroed, 1)
                take(0)
                def turn(i, u):
                    t = 2 * i + u
                    mix.dve(dve, i, u, 0)
                    selection(1).then_inc(sel_ready[1], 1)
                    mix.dve(dve, i, u, 1)
                    low = [dve.value_load(m.table[0:1, bass.ds(t, 1), g], min_val=0, max_val=N - 1)
                           for g in range(TURN)]
                    dve.wait_ge(summed[0], t + 1)
                    add_window(0, low[0]).then_inc(added, 1)
                    mix.dve(dve, i, u, 2)
                    first = dve.value_load(m.table[0:1, bass.ds(t, 1), TURN], min_val=0, max_val=NP)
                    end = dve.value_load(m.table[0:1, bass.ds(t, 1), TURN + 1], min_val=0, max_val=NP)
                    dve.wait_ge(summed[1], t + 1)
                    wait_apart(dve, added, 2 * t + 1, m.passed)
                    add_window(1, low[1]).then_inc(added, 1)
                    wait_apart(dve, added, 2 * t + 2, m.passed)
                    with dve.If(first < end):
                        with dve.Fori(first, end) as w:
                            nc.vector.tensor_scalar(rel_now[:, :], rel_now[:, :], float(-WIN), None,
                                                    ALU.add).then_inc(further_step, 1)
                            dve.wait_ge(further_step, 3 * w + 1)
                            for g in range(TURN):
                                last = selection(g)
                            last.then_inc(further_sel, 1)
                            dve.wait_ge(further_sum, w + 1)
                            for g in range(TURN):
                                at = low[g] + (w - first + 1) * WIN
                                inside = at <= NP
                                at = dve.snap(inside * at + (1 - inside) * NP).with_bounds(min_val=0, max_val=NP)
                                add_window(g, at).then_inc(further_step, 1)
                                wait_apart(dve, further_step, 3 * w + g + 2, m.passed)
                    take(t + 1)
                    mix.dve(dve, i, u, 3)

                turns(dve, turn)
                mix.dve_end(dve)

            @block.scalar
            def _(act):
                mix.act_begin(act)
                turns(act, lambda i, u: mix.act(act, i, u))
                mix.act_end(act)

            @block.tensor
            def _(pe):
                pe.sem_inc(rows_used[0], 1)
                mix.pe_begin(pe)

                def turn(i, u):
                    t = 2 * i + u
                    first = pe.value_load(m.table[0:1, bass.ds(t, 1), TURN], min_val=0, max_val=NP)
                    end = pe.value_load(m.table[0:1, bass.ds(t, 1), TURN + 1], min_val=0, max_val=NP)
                    mix.pe(pe, i, u, 0)
                    for g in range(TURN):
                        for h in range(KD):
                            if h == 0:
                                pe.wait_ge(sel_ready[g], t + 1)
                                pe.wait_ge(rows_loaded[u][g], 16 * GROUP * (i + 1))
                            last = window_products(g, h, u, rows_used[1 - u] if g == 0 and h == 0 else None)
                            if h == KD - 1:
                                last.then_inc(summed[g], 1)
                            if g * KD + h < TURN * KD - 1:
                                mix.pe(pe, i, u, 1 + g * KD + h)
                    with pe.If(first < end):
                        with pe.Fori(first, end) as w:
                            pe.wait_ge(further_sel, w + 1)
                            for g in range(TURN):
                                for h in range(KD):
                                    last = window_products(g, h, u, None)
                            last.then_inc(further_sum, 1)
                    mix.pe(pe, i, u, TURN * KD)

                turns(pe, turn)
                mix.pe_end(pe)
        mix.after()


def keys_values(nc, m, sb, sem, ps):
    mix = Memory()
    w_k = sb("w_k", [P, KD, D])
    w_v = sb("w_v", [P, KD, D])
    tile = sb("kv_tile", [P, 2, D])
    xt = sb("kv_xt", [P, KD, P])
    k_min = sb("k_min", [P, D])
    k_exp = sb("k_exp", [P, D])
    keys = sb("keys", [P, D])
    values = sb("values", [P, KD, KVS])
    turned = ps("kv_turned", KD, P)
    proj = [ps(f"kv_proj{n}_", 1, D) for n in range(2)]
    total = ps("kv_total", KD, KVS)

    weights_loaded = sem("kv_weights_loaded")
    tile_loaded = [sem(f"kv_tile_loaded{u}_") for u in range(2)]
    tile_turned = sem("kv_tile_turned")
    xt_ready = sem("kv_xt_ready")
    projected = sem("kv_projected")
    k_min_ready = sem("k_min_ready")
    k_exp_ready = sem("k_exp_ready")
    keys_ready = sem("keys_ready")
    values_ready = sem("values_ready")
    total_opened = sem("kv_total_opened")
    total_done = sem("kv_total_done")
    kv_zeroed = sem("kv_zeroed")
    kv_done = sem("kv_done")

    def load(sp, t, u):
        sp.dma_start(tile[:, u, :], m.xn[bass.ds(t * P, P), :]).then_inc(tile_loaded[u], 16)

    def load_weights(sp):
        for to, of in ((w_k, m.in_w_k), (w_v, m.in_w_v)):
            sp.dma_start(to[:, :, :], of.rearrange("(k p) n -> p k n", p=P)).then_inc(weights_loaded, 16)

    def free(sp, i, u):
        sp.wait_ge(tile_turned, 2 * i + (u + 1))

    def pe_begin(pe):
        pe.wait_ge(weights_loaded, 32)
        nc.tensor.matmul(total[:, :, :], m.ident[:, :], m.zeros[:, :].rearrange("p (k n) -> p k n", k=KD),
                         start=True, stop=False)

    def pe(pe, i, u, place):
        t = 2 * i + u
        if place == 0:
            pe.wait_ge(tile_loaded[u], 16 * i + 16)
            for h in range(KD):
                last = nc.tensor.transpose(turned[:, h, :], tile[:, u, h * P:(h + 1) * P], m.ident[:, :])
            last.then_inc(tile_turned, 1)
        if place == 1:
            pe.wait_ge(xt_ready, t + 1)
            for n, w in enumerate((w_k, w_v)):
                for k in range(KD):
                    last = nc.tensor.matmul(proj[n][:, 0, :], xt[:, k, :], w[:, k, :], start=(k == 0), stop=(k == KD - 1))
            last.then_inc(projected, 1)
        if place == 3:
            pe.wait_ge(keys_ready, t + 1)
            pe.wait_ge(values_ready, 2 * t + 2)
            for h in range(KD):
                nc.tensor.matmul(total[:, h, :], keys[:, h * P:(h + 1) * P], values[:, h, :], start=False, stop=False)

    def pe_end(pe):
        nc.tensor.matmul(total[:, :, :], m.ident[:, :], m.zeros[:, :].rearrange("p (k n) -> p k n", k=KD),
                         start=False, stop=True).then_inc(total_done, 1)

    def dve(dve, i, u, place):
        t = 2 * i + u
        if place == 1:
            dve.wait_ge(projected, t + 1)
            nc.vector.tensor_scalar(k_min[:, :], proj[0][:, 0, :], 0.0, None, ALU.min).then_inc(k_min_ready, 1)
        if place == 2:
            dve.wait_ge(k_exp_ready, t + 1)
            nc.vector.scalar_tensor_tensor(keys[:, :], proj[0][:, 0, :], 0.0, k_exp[:, :],
                                           ALU.max, ALU.add).then_inc(keys_ready, 1)

    def act(act, i, u):
        t = 2 * i + u
        act.wait_ge(tile_turned, t + 1)
        nc.scalar.copy(xt[:, :, :], turned[:, :, :]).then_inc(xt_ready, 1)
        act.wait_ge(projected, t + 1)
        nc.scalar.copy(values[:, :, 0:P], proj[1][:, 0, :].rearrange("p (k n) -> p k n", k=KD)).then_inc(values_ready, 1)
        nc.scalar.copy(values[:, :, P:KVS],
                       m.valid[:, bass.ds(t, 1)].rearrange("p (o n) -> p o n", o=1).to_broadcast([P, KD, 1])
                       ).then_inc(values_ready, 1)
        act.wait_ge(k_min_ready, t + 1)
        nc.scalar.activation(k_exp[:, :], k_min[:, :], ACT.Exp).then_inc(k_exp_ready, 1)

    def after():
        with nc.Block("kv") as block:
            @block.vector
            def _(dve):
                dve.wait_ge(total_done, 1)
                nc.vector.memset(m.kv[:, :, :], 0.0).then_inc(kv_zeroed, 1)
                dve.wait_ge(kv_zeroed, 1)
                for j in range(HC):
                    head = slice(j * HD, (j + 1) * HD)
                    nc.vector.tensor_scalar(m.kv[head, :, head], total[head, :, head], 1.0 / N, None, ALU.mult)
                    nc.vector.tensor_copy(m.kv[head, :, P + j:P + j + 1], total[head, :, P:KVS]).then_inc(kv_done, 1)
                dve.wait_ge(kv_done, HC)

    mix.load, mix.free, mix.pe_begin, mix.pe, mix.pe_end = load, free, pe_begin, pe, pe_end
    mix.dve, mix.act, mix.after = dve, act, after
    mix.store = lambda sp, i, u: None
    mix.load_weights = load_weights
    mix.load_past = mix.stored = mix.dve_begin = mix.act_begin = mix.dve_end = mix.act_end = lambda engine: None
    return mix


def attend(nc, m, sb, sem, ps):
    mix = Memory()
    tile = sb("tile", [P, 2, D])
    xt = sb("xt", [P, 2, KD, P])
    q_min = sb("q_min", [P, KD, P])
    queries = sb("queries", [P, KD, P])
    den = sb("den", [P, KD, HC])
    inv = sb("inv", [P, KD, HC])
    msg = sb("msg", [P, D])
    msg_t = sb("msg_t", [P, KD, P])
    norm_t = sb("norm_t", [P, KD, P])
    hidden = sb("hidden", [P, F1 // P, P])
    scaled = sb("scaled", [P, D])
    result = sb("result", [P, 2, D])
    stats = sb("stats", [P, 2, 6])
    mv = sb("mv", [P, 2, 2])
    var = sb("var", [P, 2, 1])
    ln_var = sb("ln_var", [P, 2, 1])
    guess = sb("guess", [P, 2, 1])
    square = sb("square", [P, 2, 1])
    inv_sd = sb("inv_sd", [P, 2, 1])

    tile_ps = ps("tile_ps", KD, P)
    query_ps = tile_ps
    num_ps = ps("num_ps", KD, KVW)
    turn_ps = ps("turn_ps", KD, P)
    row_ps = [ps(f"row_ps{n}_", 1, D)[:, 0, :] for n in range(2)]
    hidden_ps = ps("hidden_ps", F1 // P, P)

    tile_loaded = [sem(f"tile_loaded{u}_") for u in range(2)]
    tile_turned = sem("tile_turned")
    xt_ready = sem("xt_ready")
    query_projected = sem("query_projected")
    q_min_ready = sem("q_min_ready")
    q_exp_ready = sem("q_exp_ready")
    queries_ready = sem("queries_ready")
    num_ready = sem("num_ready")
    den_ready = sem("den_ready")
    inv_ready = sem("inv_ready")
    msg_ready = sem("msg_ready")
    msg_turned = sem("msg_turned")
    msg_t_ready = sem("msg_t_ready")
    msg_projected = sem("msg_projected")
    normed_ready = sem("normed_ready")
    norm_turned = sem("norm_turned")
    norm_t_ready = sem("norm_t_ready")
    hidden_done = sem("hidden_done")
    hidden_ready = sem("hidden_ready")
    mlp_done = sem("mlp_done")
    base_ready = sem("base_ready")
    scaled_ready = sem("scaled_ready")
    mixed = sem("mixed")
    stored = [sem(f"mix_stored{u}_") for u in range(2)]
    result_free = [sem(f"result_free{u}_") for u in range(2)]
    ln_step = [sem(f"ln_step{n}_") for n in range(2)]
    var_ready = [sem(f"var_ready{n}_") for n in range(2)]
    log_ready = [sem(f"log_ready{n}_") for n in range(2)]
    guess_ready = [sem(f"guess_ready{n}_") for n in range(2)]
    inv_sd_ready = [sem(f"inv_sd_ready{n}_") for n in range(2)]

    def is_first(i, u):
        return isinstance(i, int) and i == 0 and u == 0

    def load(sp, t, u):
        sp.dma_start(tile[:, u, :], m.xn[bass.ds(t * P, P), :]).then_inc(tile_loaded[u], 16)

    def free(sp, i, u):
        sp.wait_ge(base_ready, 2 * i + (u + 1))

    def store(sp, i, u):
        t = 2 * i + u
        sp.wait_ge(mixed, t + 1)
        sp.dma_start(m.mix[bass.ds(t * P, P), :], result[:, u, :]).then_inc(stored[u], 16)
        sp.wait_ge(stored[u], 16 * i + 16)
        sp.sem_inc(result_free[u], 1)

    def load_past(sp):
        free(sp, TURNS // 2 - 1, 0)
        load(sp, TURNS, 0)

    def all_stored(sp):
        for u in range(2):
            store(sp, TURNS // 2 - 1, u)

    def turn_tile(pe, t, u, i):
        pe.wait_ge(tile_loaded[u], 16 * i + 16)
        for h in range(KD):
            last = nc.tensor.transpose(tile_ps[:, h, :], tile[:, u, h * P:(h + 1) * P], m.ident[:, :])
        last.then_inc(tile_turned, 1)

    def project_queries(pe, t, u):
        pe.wait_ge(xt_ready, t + 1)
        for h in range(KD):
            for k in range(KD):
                last = nc.tensor.matmul(query_ps[:, h, :], m.w_q[:, k, h * P:(h + 1) * P], xt[:, u, k, :],
                                        start=(k == 0), stop=(k == KD - 1))
        last.then_inc(query_projected, 1)

    def mlp_output(pe, t):
        pe.wait_ge(hidden_ready, t + 1)
        for o in range(F1 // P):
            last = nc.tensor.matmul(row_ps[1], hidden[:, o, :], m.w_2[:, o, :], start=(o == 0),
                                    stop=(o == F1 // P - 1))
        last.then_inc(mlp_done, 1)

    def pe_begin(pe):
        turn_tile(pe, 0, 0, 0)
        project_queries(pe, 0, 0)

    def pe(pe, i, u, place):
        t = 2 * i + u
        if place == 1:
            pe.wait_ge(queries_ready, t + 1)
            for h in range(KD):
                last = nc.tensor.matmul(num_ps[:, h, :], queries[:, h, :], m.kv[:, h, :], start=True, stop=True)
            last.then_inc(num_ready, 1)
            if not is_first(i, u):
                mlp_output(pe, t - 1)
        if place == 2:
            pe.wait_ge(msg_ready, t + 1)
            for h in range(KD):
                last = nc.tensor.transpose(turn_ps[:, h, :], msg[:, h * P:(h + 1) * P], m.ident[:, :])
            last.then_inc(msg_turned, 1)
            turn_tile(pe, t + 1, 1 - u, i + u)
            pe.wait_ge(msg_t_ready, t + 1)
            for k in range(KD):
                last = nc.tensor.matmul(row_ps[0], msg_t[:, k, :], m.w_m[:, k, :], start=(k == 0), stop=(k == KD - 1))
            last.then_inc(msg_projected, 1)
        if place == 4:
            pe.wait_ge(normed_ready, t + 1)
            for h in range(KD):
                last = nc.tensor.transpose(turn_ps[:, h, :], msg[:, h * P:(h + 1) * P], m.ident[:, :])
            last.then_inc(norm_turned, 1)
            project_queries(pe, t + 1, 1 - u)
            pe.wait_ge(norm_t_ready, 2 * t + 2)
            for o in range(F1 // P):
                for k in range(2 * KD):
                    of = xt[:, u, k, :] if k < KD else norm_t[:, k - KD, :]
                    last = nc.tensor.matmul(hidden_ps[:, o, :], m.w_1[:, k, o * P:(o + 1) * P], of,
                                            start=(k == 0), stop=(k == 2 * KD - 1))
            last.then_inc(hidden_done, 1)

    def pe_end(pe):
        mlp_output(pe, TURNS - 1)

    def variance(dve, t, n):
        nc.vector.bn_stats(stats[:, n, :], row_ps[n]).then_inc(ln_step[n], 1)
        wait_apart(dve, ln_step[n], 3 * t + 1, m.passed)
        nc.vector.bn_aggr(mv[:, n, :], stats[:, n, :]).then_inc(ln_step[n], 1)
        dve.wait_ge(ln_step[n], 3 * t + 2)
        nc.vector.tensor_scalar(var[:, n, :], mv[:, n, 1:2], LN_EPS, None, ALU.add).then_inc(var_ready[n], 1)

    def inverse_sd(dve, t, n):
        dve.wait_ge(guess_ready[n], t + 1)
        nc.vector.scalar_tensor_tensor(square[:, n, :], guess[:, n, :], var[:, n, :], guess[:, n, :],
                                       ALU.mult, ALU.mult).then_inc(ln_step[n], 1)
        dve.wait_ge(ln_step[n], 3 * t + 3)
        nc.vector.scalar_tensor_tensor(inv_sd[:, n, :], square[:, n, :], 3.0, guess[:, n, :],
                                       ALU.subtract, ALU.mult).then_inc(inv_sd_ready[n], 1)
        dve.wait_ge(inv_sd_ready[n], t + 1)

    def normalise(dve, to, n):
        return nc.vector.tensor_scalar(to, row_ps[n], mv[:, n, 0:1], inv_sd[:, n, :], ALU.subtract, ALU.mult)

    def guess_sd(act, t, n):
        act.wait_ge(var_ready[n], t + 1)
        nc.scalar.activation(ln_var[:, n, :], var[:, n, :], ACT.Ln).then_inc(log_ready[n], 1)
        act.wait_ge(log_ready[n], t + 1)
        nc.scalar.activation(guess[:, n, :], ln_var[:, n, :], ACT.Exp, scale=-0.5).then_inc(guess_ready[n], 1)

    def min_query(dve, t):
        dve.wait_ge(query_projected, t + 1)
        nc.vector.tensor_scalar(q_min[:, :, :], query_ps[:, :, :], 0.0, None, ALU.min).then_inc(q_min_ready, 1)

    def output_variance(dve, t):
        dve.wait_ge(mlp_done, t + 1)
        variance(dve, t, 1)

    def output(dve, t, u):
        inverse_sd(dve, t, 1)
        normalise(dve, scaled[:, :], 1).then_inc(scaled_ready, 1)
        dve.wait_ge(scaled_ready, 2 * t + 1)
        nc.vector.tensor_tensor(scaled[:, :], scaled[:, :], m.ln2_gh[:, :], ALU.mult).then_inc(scaled_ready, 1)
        dve.wait_ge(scaled_ready, 2 * t + 2)
        nc.vector.tensor_tensor(result[:, u, :], result[:, u, :], scaled[:, :], ALU.add).then_inc(mixed, 1)

    def dve_begin(dve):
        min_query(dve, 0)

    def dve(dve, i, u, place):
        t = 2 * i + u
        if place == 0:
            dve.wait_ge(q_exp_ready, t + 1)
            nc.vector.scalar_tensor_tensor(queries[:, :, :], query_ps[:, :, :], 0.0, q_min[:, :, :],
                                           ALU.max, ALU.add).then_inc(queries_ready, 1)
        if place == 1:
            dve.wait_ge(num_ready, t + 1)
            nc.vector.tensor_scalar(den[:, :, :], num_ps[:, :, P:KVW], ATT_EPS, 1.0 / N,
                                    ALU.add, ALU.mult).then_inc(den_ready, 1)
            dve.wait_ge(den_ready, t + 1)
            nc.vector.reciprocal(inv[:, :, :], den[:, :, :]).then_inc(inv_ready, 1)
            dve.wait_ge(inv_ready, t + 1)
            nc.vector.tensor_tensor(msg[:, :].rearrange("p (k h d) -> p k h d", k=KD, h=HC),
                                    num_ps[:, :, 0:P].rearrange("p k (h d) -> p k h d", h=HC),
                                    inv[:, :, :].rearrange("p k (h o) -> p k h o", o=1)
                                    .to_broadcast([P, KD, HC, HD]), ALU.mult).then_inc(msg_ready, 1)
            if not is_first(i, u):
                output_variance(dve, t - 1)
        if place == 2:
            if not is_first(i, u):
                output(dve, t - 1, 1 - u)
            dve.wait_ge(msg_projected, t + 1)
            variance(dve, t, 0)
            dve.wait_ge(result_free[u], i + 1)
            dve.sem_inc(m.passed, 1)
            nc.vector.tensor_tensor(result[:, u, :], tile[:, u, :], m.ln2_b[:, :], ALU.add).then_inc(base_ready, 1)
            inverse_sd(dve, t, 0)
            normalise(dve, msg[:, :], 0).then_inc(normed_ready, 1)
        if place == 3:
            min_query(dve, t + 1)

    def dve_end(dve):
        output_variance(dve, TURNS - 1)
        output(dve, TURNS - 1, 1)

    def copy_tile(act, t, u):
        act.wait_ge(tile_turned, t + 1)
        nc.scalar.copy(xt[:, u, :, :], tile_ps[:, :, :]).then_inc(xt_ready, 1)

    def exp_query(act, t):
        act.wait_ge(q_min_ready, t + 1)
        nc.scalar.activation(q_min[:, :, :], q_min[:, :, :], ACT.Exp).then_inc(q_exp_ready, 1)

    def act_begin(act):
        act.preload_act_table_set(TABLES)
        for u in range(2):
            act.sem_inc(result_free[u], 1)
        copy_tile(act, 0, 0)
        exp_query(act, 0)

    def act(act, i, u):
        t = 2 * i + u
        if not is_first(i, u):
            guess_sd(act, t - 1, 1)
        act.wait_ge(msg_turned, t + 1)
        nc.scalar.copy(msg_t[:, :, :], turn_ps[:, :, :]).then_inc(msg_t_ready, 1)
        copy_tile(act, t + 1, 1 - u)
        guess_sd(act, t, 0)
        act.wait_ge(norm_turned, t + 1)
        for h in range(KD):
            nc.scalar.activation(norm_t[:, h, :], turn_ps[:, h, :], ACT.Identity, scale=m.ln1_gh[:, h:h + 1],
                                 bias=m.ln1_b[:, h:h + 1]).then_inc(norm_t_ready, 1)
        exp_query(act, t + 1)
        act.wait_ge(hidden_done, t + 1)
        nc.scalar.activation(hidden[:, :, :], hidden_ps[:, :, :], ACT.Relu).then_inc(hidden_ready, 1)

    def act_end(act):
        guess_sd(act, TURNS - 1, 1)

    mix.load, mix.free, mix.store, mix.stored = load, free, store, all_stored
    mix.pe_begin, mix.pe, mix.pe_end = pe_begin, pe, pe_end
    mix.dve_begin, mix.dve, mix.dve_end = dve_begin, dve, dve_end
    mix.act_begin, mix.act, mix.act_end, mix.load_past = act_begin, act, act_end, load_past
    mix.load_weights = lambda sp: None
    mix.after = lambda: None
    return mix


def dense_first(nc, m):
    with ExitStack() as ctx:
        def sb(name, shape, dt=F32):
            return ctx.enter_context(nc.sbuf_tensor(name, shape, dt))

        sem = semaphores(nc, ctx)

        w_g1 = sb("w_g1", [P, KD, D])
        agg_now = sb("agg_now", [P, DT, KD, P])
        z_min = sb("z_min", [P, DT, D])
        z_exp = sb("z_exp", [P, DT, D])
        h_one = sb("h_one", [P, DT, D])
        h = sb("h", [P, 2, DT, D])
        z = [ctx.enter_context(nc.psum_tensor(f"z{j}", [P, BANK], F32))[:, 0:D] for j in range(DT)]

        weights_loaded = sem("g1_weights_loaded")
        agg_ready = sem("agg_ready")
        z_ready = sem("z_ready")
        z_min_ready = sem("z_min_ready")
        z_exp_ready = sem("z_exp_ready")
        h_one_ready = sem("h_one_ready")
        h_ready = sem("h_ready")
        h_stored = [sem(f"h_stored{u}") for u in range(2)]
        h_free = [sem(f"h_free{u}") for u in range(2)]
        loops = NT // (2 * DT)
        h1_blocks = m.h1.rearrange("(b j p) f -> b p j f", p=P, j=DT)

        def each(engine, body):
            with engine.Fori(0, loops) as i:
                for u in range(2):
                    for j in range(DT):
                        body(i, u, j, i * (2 * DT) + (u * DT + j))

        with nc.Block("dense1") as block:
            @block.gpsimd
            def _(pool):
                def copy(i, u, j, n):
                    pool.wait_ge(z_ready, n + 1)
                    pool.sem_inc(m.pool_passed, 1)
                    nc.gpsimd.tensor_copy(agg_now[:, j, :, :], m.agg[:, :, bass.ds(n * P, P)]).then_inc(agg_ready, 1)
                each(pool, copy)

            @block.tensor
            def _(pe):
                pe.sem_inc(z_ready, DT)
                pe.wait_ge(weights_loaded, 16)
                pe.sem_inc(m.pe_passed, 1)

                def product(i, u, j, n):
                    pe.wait_ge(agg_ready, n + 1)
                    pe.wait_ge(h_one_ready, n + 1)
                    nc.tensor.matmul(z[j], m.ones[0:1, :], m.b_g1[:, :], start=True, stop=False)
                    for k in range(KD):
                        last = nc.tensor.matmul(z[j], agg_now[:, j, k, :], w_g1[:, k, :],
                                                start=False, stop=(k == KD - 1))
                    last.then_inc(z_ready, 1)
                each(pe, product)

            @block.vector
            def _(dve):
                dve.sem_inc(h_one_ready, DT)

                def min_part(n, j):
                    dve.wait_ge(z_ready, n + (1 + DT))
                    nc.vector.tensor_scalar(z_min[:, j, :], z[j], 0.0, None, ALU.min).then_inc(z_min_ready, 1)

                def sum_part(n, j):
                    dve.wait_ge(z_exp_ready, n + 1)
                    nc.vector.scalar_tensor_tensor(h_one[:, j, :], z[j], 0.0, z_exp[:, j, :],
                                                   ALU.max, ALU.add).then_inc(h_one_ready, 1)

                with dve.Fori(0, loops) as i:
                    for u in range(2):
                        n = i * (2 * DT) + u * DT
                        min_part(n, 0)
                        for j in range(1, DT):
                            min_part(n + j, j)
                            sum_part(n + (j - 1), j - 1)
                        sum_part(n + (DT - 1), DT - 1)

            @block.scalar
            def _(act):
                def exp_part(n, j):
                    act.wait_ge(z_min_ready, n + 1)
                    nc.scalar.activation(z_exp[:, j, :], z_min[:, j, :], ACT.Exp).then_inc(z_exp_ready, 1)

                def less_one(i, u, n, j):
                    act.wait_ge(h_one_ready, n + (1 + DT))
                    nc.scalar.activation(h[:, u, j, :], h_one[:, j, :], ACT.Copy, bias=-1.0).then_inc(h_ready, 1)

                with act.Fori(0, loops) as i:
                    for u in range(2):
                        n = i * (2 * DT) + u * DT
                        act.wait_ge(h_free[u], i + 1)
                        act.sem_inc(m.act_passed, 1)
                        exp_part(n, 0)
                        for j in range(1, DT):
                            exp_part(n + j, j)
                            less_one(i, u, n + (j - 1), j - 1)
                        less_one(i, u, n + (DT - 1), DT - 1)

            @block.sync
            def _(sp):
                sp.dma_start(w_g1[:, :, :], m.in_w_g1.rearrange("(k p) n -> p k n", p=P)).then_inc(weights_loaded, 16)
                for u in range(2):
                    sp.sem_inc(h_free[u], 1)
                with sp.Fori(0, loops) as i:
                    for u in range(2):
                        sp.wait_ge(h_ready, i * (2 * DT) + (u + 1) * DT)
                        sp.dma_start(h1_blocks[bass.ds(2 * i + u, 1)].rearrange("b p j f -> (b p) j f"),
                                     h[:, u, :, :]).then_inc(h_stored[u], 16)
                        sp.wait_ge(h_stored[u], 16 * i + 16)
                        sp.sem_inc(h_free[u], 1)


def dense_second(nc, m):
    with ExitStack() as ctx:
        def sb(name, shape, dt=F32):
            return ctx.enter_context(nc.sbuf_tensor(name, shape, dt))

        sem = semaphores(nc, ctx)

        x_in = sb("x_in", [P, 2, DT, D])
        mix_in = sb("mix_in", [P, DT, D])
        agg_now = sb("agg_now2", [P, KD, P])
        z_min = sb("z2_min", [P, D])
        h_one = sb("h2_one", [P, D])
        xf = sb("xf", [P, DT, D])
        xf_t = sb("xf_t", [P, KD, P])
        stats = sb("x2_stats", [P, DT, 6])
        mv = sb("x2_mv", [P, DT, 2])
        var = sb("x2_var", [P, DT])
        guess = sb("x2_guess", [P, DT])
        square = sb("x2_square", [P, DT])
        inv_sd = sb("x2_inv_sd", [P, DT])
        logits = sb("logits", [P, DT, NE])
        most = sb("most", [P, DT])
        total = sb("total", [P, DT])
        top = sb("top", [P, DT, NE])
        top_at = sb("top_at", [P, DT, NE], U32)
        expert = sb("expert", [P, DT])
        chosen = sb("chosen", [P, DT, NE])
        counted = sb("counted", [P, DT, NE])
        seen = sb("seen", [P, NE])
        seen_now = sb("seen_now", [P, NE])
        nth = sb("nth", [P, DT])
        kept = sb("kept", [P, DT])
        row = sb("row", [P, DT])
        row_i = sb("row_i", [P, DT], I32)
        at = sb("at", [P, DT])
        experts_i = sb("experts_i", [P, NE], I32)
        experts_f = sb("experts_f", [P, NE])
        trash_i = sb("trash_i", [P, DT], I32)
        trash_f = sb("trash_f", [P, DT])
        blocks_i = sb("blocks_i", [1, NE], I32)
        blocks_f = sb("blocks_f", [1, NE])
        blocks_end = sb("blocks_end", [1, NE])
        blocks_one = sb("blocks_one", [1, NE])

        def ps(name, n):
            return ctx.enter_context(nc.psum_tensor(name, [P, BANK], F32))[:, 0:n]

        z = ps("z_second", D)
        xf_ps = ps("xf_ps", KD * P).rearrange("p (k n) -> p k n", k=KD)
        logit_ps = ps("logit_ps", DT * NE).rearrange("p (j e) -> p j e", j=DT)
        nth_ps = ps("nth_ps", DT * NE).rearrange("p (j e) -> p j e", j=DT)
        count_ps = ps("count_ps", NE)

        x_loaded = [sem(f"x2_x_loaded{u}") for u in range(2)]
        mix_loaded = sem("mix_loaded")
        base_ready = sem("base_ready")
        agg_ready = sem("agg2_ready")
        z_ready = sem("z2_ready")
        z_min_ready = sem("z2_min_ready")
        z_exp_ready = sem("z2_exp_ready")
        h_one_ready = sem("h2_one_ready")
        x2_ready = sem("x2_ready")
        xf_ready = sem("xf_ready")
        xf_turned = sem("xf_turned")
        xf_t_ready = sem("xf_t_ready")
        logits_done = sem("logits_done")
        x2_stored = [sem(f"x2_stored{u}") for u in range(2)]
        x_free = [sem(f"x2_free{u}") for u in range(2)]
        scattered = sem("scattered")
        xf_free = sem("xf_free")
        var_ready = sem("x2_var_ready")
        log_ready = sem("x2_log_ready")
        guess_ready = sem("x2_guess_ready")
        shifted_ready = sem("shifted_ready")
        exps_ready = sem("exps_ready")
        chosen_ready = sem("chosen_ready")
        nth_done = sem("nth_done")
        rows_ready = sem("rows_ready")
        step = sem("dense2_step")
        iotas = sem("dense2_iotas")
        consts = sem("dense2_consts")
        counts_done = sem("counts_done")
        tail = sem("dense2_tail")
        loops = NT // (2 * DT)
        STEPS = 21

        def blocks(of):
            return of.rearrange("(b j p) f -> b p j f", p=P, j=DT)

        with nc.Block("dense2") as block:
            @block.sync
            def _(sp):
                sp.wait_ge(m.buffers_zeroed, 32)
                for u in range(2):
                    sp.sem_inc(x_free[u], 1)
                with sp.Fori(0, loops) as i:
                    for u in range(2):
                        b = 2 * i + u
                        sp.wait_ge(x_free[u], i + 1)
                        sp.dma_start(x_in[:, u, :, :],
                                     blocks(m.x)[bass.ds(b, 1)].rearrange("b p j f -> (b p) j f")
                                     ).then_inc(x_loaded[u], 16)
                        sp.wait_ge(base_ready, b + 1)
                        sp.dma_start(mix_in[:, :, :],
                                     blocks(m.mix)[bass.ds(b, 1)].rearrange("b p j f -> (b p) j f")
                                     ).then_inc(mix_loaded, 16)
                        sp.wait_ge(x2_ready, (b + 1) * DT)
                        sp.dma_start(blocks(m.x2)[bass.ds(b, 1)].rearrange("b p j f -> (b p) j f"),
                                     x_in[:, u, :, :]).then_inc(x2_stored[u], 16)
                        sp.wait_ge(x2_stored[u], 16 * i + 16)
                        sp.sem_inc(x_free[u], 1)

            @block.gpsimd
            def _(pool):
                pool.sem_inc(base_ready, 1)
                pool.sem_inc(xf_free, 1)
                nc.gpsimd.iota(experts_i[:, :], [[1, NE]], base=0, channel_multiplier=0).then_inc(iotas, 1)
                nc.gpsimd.iota(trash_i[:, :], [[P, DT]], base=TRASH, channel_multiplier=1).then_inc(iotas, 1)
                with pool.Fori(0, loops) as i:
                    for u in range(2):
                        b = 2 * i + u
                        pool.wait_ge(x_loaded[u], 16 * i + 16)
                        pool.wait_ge(mix_loaded, 16 * b + 16)
                        pool.sem_inc(m.pool_passed, 1)
                        nc.gpsimd.tensor_tensor(x_in[:, u, :, :], x_in[:, u, :, :], mix_in[:, :, :],
                                                ALU.add).then_inc(base_ready, 1)
                        wait_apart(pool, rows_ready, b + 1, m.pool_passed)
                        for j in range(DT):
                            nc.gpsimd.indirect_dma_start(
                                out=m.xe, out_offset=bass.IndirectOffsetOnAxis(ap=row_i[:, j:j + 1], axis=0),
                                in_=xf[:, j, :], in_offset=None).then_inc(scattered, 16)
                        pool.wait_ge(scattered, 16 * DT * (b + 1))
                        pool.sem_inc(xf_free, 1)

            @block.scalar
            def _(act):
                act.preload_act_table_set(TABLES)
                with act.Fori(0, loops) as i:
                    for u in range(2):
                        b = 2 * i + u
                        for j in range(DT):
                            n = b * DT + j
                            act.wait_ge(z_ready, n + 1)
                            nc.scalar.copy(agg_now[:, :, :], m.agg[:, :, bass.ds(n * P, P)]).then_inc(agg_ready, 1)
                            act.wait_ge(z_min_ready, n + 1)
                            nc.scalar.activation(z_min[:, :], z_min[:, :], ACT.Exp).then_inc(z_exp_ready, 1)
                        act.wait_ge(var_ready, b + 1)
                        nc.scalar.activation(guess[:, :], var[:, :], ACT.Ln).then_inc(log_ready, 1)
                        act.wait_ge(log_ready, b + 1)
                        nc.scalar.activation(guess[:, :], guess[:, :], ACT.Exp, scale=-0.5).then_inc(guess_ready, 1)
                        for j in range(DT):
                            act.wait_ge(xf_turned, b * DT + j + 1)
                            nc.scalar.copy(xf_t[:, :, :], xf_ps[:, :, :]).then_inc(xf_t_ready, 1)
                        act.wait_ge(shifted_ready, b + 1)
                        nc.scalar.activation(logits[:, :, :], logits[:, :, :], ACT.Exp).then_inc(exps_ready, 1)

            @block.tensor
            def _(pe):
                pe.sem_inc(z_ready, 1)
                with pe.Fori(0, loops) as i:
                    for u in range(2):
                        b = 2 * i + u
                        for j in range(DT):
                            n = b * DT + j
                            pe.wait_ge(agg_ready, n + 1)
                            pe.wait_ge(h_one_ready, n + 1)
                            nc.tensor.matmul(z, m.ones[0:1, :], m.b_g2[:, :], start=True, stop=False)
                            for k in range(KD):
                                last = nc.tensor.matmul(z, agg_now[:, k, :], m.w_g2[:, k, :], start=False,
                                                        stop=(k == KD - 1))
                            last.then_inc(z_ready, 1)
                        pe.wait_ge(xf_ready, b + 1)
                        for j in range(DT):
                            for h in range(KD):
                                last = nc.tensor.transpose(xf_ps[:, h, :], xf[:, j, h * P:(h + 1) * P], m.ident[:, :])
                            last.then_inc(xf_turned, 1)
                            pe.wait_ge(xf_t_ready, b * DT + j + 1)
                            for k in range(KD):
                                last = nc.tensor.matmul(logit_ps[:, j, :], xf_t[:, k, :], m.gate_w[:, k, :],
                                                        start=(k == 0), stop=(k == KD - 1))
                        last.then_inc(logits_done, 1)
                        pe.wait_ge(chosen_ready, b + 1)
                        nc.tensor.matmul(nth_ps[:, :, :], m.upto[:, :], chosen[:, :, :], start=True, stop=False)
                        for j in range(1, DT):
                            nc.tensor.matmul(nth_ps[:, j:DT, :], m.ones[:, :], chosen[:, 0:DT - j, :],
                                             start=False, stop=False)
                        nc.tensor.matmul(nth_ps[:, :, :], m.ones[:, :],
                                         seen[:, :].rearrange("p (o e) -> p o e", o=1).to_broadcast([P, DT, NE]),
                                         start=False, stop=True).then_inc(nth_done, 1)
                pe.wait_ge(counts_done, 1)
                nc.tensor.matmul(count_ps, m.ones[:, :], seen[:, :], start=True, stop=True).then_inc(tail, 1)

            @block.vector
            def _(dve):
                dve.sem_inc(h_one_ready, 1)
                dve.wait_ge(iotas, 2)
                nc.vector.tensor_copy(experts_f[:, :], experts_i[:, :]).then_inc(consts, 1)
                nc.vector.tensor_copy(trash_f[:, :], trash_i[:, :]).then_inc(consts, 1)
                nc.vector.memset(seen[:, :], 0.0).then_inc(consts, 1)
                dve.wait_ge(consts, 3)

                def wide(of, n=NE):
                    return of.rearrange("p (j o) -> p j o", o=1).to_broadcast([P, DT, n])

                with dve.Fori(0, loops) as i:
                    for u in range(2):
                        b = 2 * i + u
                        count = [0]

                        def link(instruction):
                            count[0] += 1
                            instruction.then_inc(step, 1)
                            wait_apart(dve, step, b * STEPS + count[0], m.passed)

                        dve.wait_ge(base_ready, b + 2)
                        dve.sem_inc(m.passed, 1)
                        for j in range(DT):
                            n = b * DT + j
                            dve.wait_ge(z_ready, n + 2)
                            nc.vector.tensor_scalar(z_min[:, :], z, 0.0, None, ALU.min).then_inc(z_min_ready, 1)
                            dve.wait_ge(z_exp_ready, n + 1)
                            nc.vector.scalar_tensor_tensor(h_one[:, :], z, 0.0, z_min[:, :],
                                                           ALU.max, ALU.add).then_inc(h_one_ready, 1)
                            dve.wait_ge(h_one_ready, n + 2)
                            nc.vector.scalar_tensor_tensor(x_in[:, u, j, :], h_one[:, :], -1.0, x_in[:, u, j, :],
                                                           ALU.add, ALU.add).then_inc(x2_ready, 1)
                            wait_apart(dve, x2_ready, n + 1, m.passed)
                            last = nc.vector.bn_stats(stats[:, j, :], x_in[:, u, j, :])
                        link(last)
                        for j in range(DT):
                            last = nc.vector.bn_aggr(mv[:, j, :], stats[:, j, :])
                        link(last)
                        nc.vector.tensor_scalar(var[:, :], mv[:, :, 1], LN_EPS, None, ALU.add).then_inc(var_ready, 1)
                        dve.wait_ge(guess_ready, b + 1)
                        link(nc.vector.tensor_tensor(square[:, :], guess[:, :], guess[:, :], ALU.mult))
                        link(nc.vector.tensor_tensor(square[:, :], square[:, :], var[:, :], ALU.mult))
                        link(nc.vector.tensor_scalar(square[:, :], square[:, :], -0.5, 1.5, ALU.mult, ALU.add))
                        link(nc.vector.tensor_tensor(inv_sd[:, :], guess[:, :], square[:, :], ALU.mult))
                        wait_apart(dve, xf_free, b + 1, m.passed)
                        for j in range(DT):
                            last = nc.vector.tensor_scalar(xf[:, j, :], x_in[:, u, j, :], mv[:, j, 0:1],
                                                           inv_sd[:, j:j + 1], ALU.subtract, ALU.mult)
                        last.then_inc(xf_ready, 1)
                        dve.wait_ge(logits_done, b + 1)
                        link(nc.vector.tensor_tensor(logits[:, :, :], logit_ps[:, :, :],
                                                     m.gate_b[:, :].rearrange("p (o e) -> p o e", o=1)
                                                     .to_broadcast([P, DT, NE]), ALU.add))
                        link(nc.vector.tensor_reduce(most[:, :], logits[:, :, :], AX.X, ALU.max))
                        nc.vector.tensor_tensor(logits[:, :, :], logits[:, :, :], wide(most[:, :]),
                                                ALU.subtract).then_inc(shifted_ready, 1)
                        dve.wait_ge(exps_ready, b + 1)
                        link(nc.vector.tensor_reduce(total[:, :], logits[:, :, :], AX.X, ALU.add))
                        link(nc.vector.reciprocal(total[:, :], total[:, :]))
                        link(nc.vector.tensor_tensor(logits[:, :, :], logits[:, :, :], wide(total[:, :]), ALU.mult))
                        for j in range(DT):
                            last = nc.vector.max(top[:, j, :], logits[:, j, :])
                        link(last)
                        for j in range(DT):
                            last = nc.vector.max_index(top_at[:, j, :], top[:, j, :], logits[:, j, :])
                        link(last)
                        link(nc.vector.tensor_copy(expert[:, :], top_at[:, :, 0]))
                        link(nc.vector.tensor_tensor(chosen[:, :, :],
                                                     experts_f[:, :].rearrange("p (o e) -> p o e", o=1)
                                                     .to_broadcast([P, DT, NE]), wide(expert[:, :]), ALU.is_equal))
                        valid = m.valid[:, bass.ds(b * DT, DT)]
                        nc.vector.tensor_tensor(chosen[:, :, :], chosen[:, :, :], wide(valid),
                                                ALU.mult).then_inc(chosen_ready, 1)
                        dve.wait_ge(nth_done, b + 1)
                        nc.vector.tensor_reduce(seen_now[:, :], chosen[:, :, :].rearrange("p j e -> p e j"),
                                                AX.X, ALU.add)
                        link(nc.vector.tensor_tensor(counted[:, :, :], nth_ps[:, :, :], chosen[:, :, :], ALU.mult))
                        nc.vector.tensor_tensor(seen[:, :], seen[:, :], seen_now[:, :], ALU.add)
                        link(nc.vector.tensor_reduce(nth[:, :], counted[:, :, :], AX.X, ALU.add))
                        nc.vector.tensor_scalar(kept[:, :], nth[:, :], float(CAP), None, ALU.is_le)
                        link(nc.vector.scalar_tensor_tensor(row[:, :], expert[:, :], float(ROWS), nth[:, :],
                                                            ALU.mult, ALU.add))
                        nc.vector.tensor_scalar(at[:, :], nth[:, :], float(CAP), 1.0, ALU.min, ALU.subtract)
                        link(nc.vector.tensor_tensor(kept[:, :], kept[:, :], valid, ALU.mult))
                        nc.vector.scalar_tensor_tensor(row[:, :], row[:, :], -1.0, trash_f[:, :], ALU.add, ALU.subtract)
                        link(nc.vector.scalar_tensor_tensor(at[:, :], expert[:, :], float(ROWS), at[:, :],
                                                            ALU.mult, ALU.add))
                        nc.vector.tensor_tensor(m.place[:, bass.ds(b * DT, DT)], at[:, :], valid, ALU.mult)
                        nc.vector.tensor_tensor(m.prob[:, bass.ds(b * DT, DT)], top[:, :, 0], kept[:, :], ALU.mult)
                        link(nc.vector.tensor_tensor(row[:, :], row[:, :], kept[:, :], ALU.mult))
                        nc.vector.tensor_tensor(row_i[:, :], row[:, :], trash_f[:, :], ALU.add).then_inc(rows_ready, 1)
                        assert count[0] == STEPS, count[0]
                nc.vector.memset(blocks_one[:, :], 1.0).then_inc(counts_done, 1)
                dve.wait_ge(tail, 1)
                nc.vector.tensor_scalar(blocks_i[:, :], count_ps[0:1, :], float(CAP), float(TB - 1),
                                        ALU.min, ALU.add).then_inc(tail, 1)
                dve.wait_ge(tail, 2)
                nc.vector.tensor_scalar(blocks_i[:, :], blocks_i[:, :], LOG_TB, None,
                                        ALU.arith_shift_right).then_inc(tail, 1)
                dve.wait_ge(tail, 3)
                nc.vector.tensor_scalar(blocks_f[:, :], blocks_i[:, :], 1.0, None, ALU.max).then_inc(tail, 1)
                dve.wait_ge(tail, 4)
                nc.vector.tensor_tensor_scan(blocks_end[:, :], blocks_one[:, :], blocks_f[:, :], 0.0,
                                             ALU.mult, ALU.add).then_inc(tail, 1)
                dve.wait_ge(tail, 5)
                nc.vector.tensor_copy(m.blocks[0:1, :, 1], blocks_end[:, :]).then_inc(tail, 1)
                nc.vector.tensor_tensor(m.blocks[0:1, :, 0], blocks_end[:, :], blocks_f[:, :],
                                        ALU.subtract).then_inc(tail, 1)
                dve.wait_ge(tail, 7)


def experts(nc, m):
    with ExitStack() as ctx:
        def sb(name, shape, dt=F32):
            return ctx.enter_context(nc.sbuf_tensor(name, shape, dt))

        sem = semaphores(nc, ctx)

        def ps(name, n):
            return ctx.enter_context(nc.psum_tensor(name, [P, BANK], F32))[:, 0:n]

        TT = TB // P
        w1 = [sb(f"w1_{u}", [P, KD, F]) for u in range(2)]
        w2 = [sb(f"w2_{u}", [P, FC, D]) for u in range(2)]
        b1 = [sb(f"b1_{u}", [P, FC]) for u in range(2)]
        b2 = [sb(f"b2_{u}", [P, D]) for u in range(2)]
        tokens = sb("tokens", [P, TT, D])
        tokens_t = sb("tokens_t", [P, KD, TB])
        hidden = sb("e_hidden", [P, FC, TB])
        y = sb("y", [P, TT, D])
        turn_ps = ps("e_turn_ps", KD * TB).rearrange("p (k n) -> p k n", k=KD)
        HB = 4
        hidden_ps = [ps(f"e_hidden_ps{f}", TB) for f in range(HB)]
        y_ps = [ps(f"y_ps{tt}", D) for tt in range(TT)]

        weights_loaded = [sem(f"weights_loaded{u}") for u in range(2)]
        tokens_loaded = sem("tokens_loaded")
        turned = sem("e_turned")
        tokens_t_ready = sem("tokens_t_ready")
        hidden_done = sem("e_hidden_done")
        by_act = sem("hidden_by_act")
        by_dve = sem("hidden_by_dve")
        y_done = sem("y_done")
        y_ready = sem("y_ready")
        y_stored = sem("y_stored")

        def bounds(engine, e):
            return [engine.value_load(m.blocks[0:1, bass.ds(e, 1), k], min_val=0, max_val=NE * ROWS // TB)
                    for k in range(2)]

        def rows_of(of, e, n, first):
            at = (e * ROWS + (n - first) * TB).with_bounds(min_val=0, max_val=(NE * ROWS - TB))
            return of[bass.ds(at, TB), :].rearrange("(j p) f -> p j f", p=P)

        def each(engine, body):
            with engine.Fori(0, NE // 2) as ii:
                for u in range(2):
                    e = 2 * ii + u
                    first, end = bounds(engine, e)
                    with engine.Fori(first, end) as n:
                        body(e, u, ii, n, first)

        with nc.Block("experts") as block:
            @block.gpsimd
            def _(pool):
                def load(e, u):
                    one = bass.ds(e, 1)
                    pool.dma_start(w1[u][:, :, :], m.w_e1[one].rearrange("o (k p) f -> p (o k) f", p=P)
                                   ).then_inc(weights_loaded[u], 16)
                    pool.dma_start(w2[u][:, :, :], m.w_e2[one].rearrange("o (k p) f -> p (o k) f", p=P)
                                   ).then_inc(weights_loaded[u], 16)
                    pool.dma_start(b1[u][:, :], m.in_b_e1[:, one, :].rearrange("p o f -> p (o f)")
                                   ).then_inc(weights_loaded[u], 16)
                    pool.dma_start(b2[u][:, :], m.in_b_e2[one, :].to_broadcast([P, D])
                                   ).then_inc(weights_loaded[u], 16)

                for u in range(2):
                    load(u, u)
                with pool.Fori(0, NE // 2 - 1) as ii:
                    for u in range(2):
                        first, end = bounds(pool, 2 * ii + u)
                        wait_apart(pool, y_ready, (end + 1) * TT, m.pool_passed)
                        load(2 * ii + (2 + u), u)

            @block.sync
            def _(sp):
                def load(e, u, ii, n, first):
                    sp.wait_ge(turned, n + 1)
                    sp.dma_start(tokens[:, :, :], rows_of(m.xe, e, n, first)).then_inc(tokens_loaded, 16)

                each(sp, load)
                first, end = bounds(sp, NE - 1)
                sp.wait_ge(turned, end + 1)
                sp.dma_start(tokens[:, :, :], m.xe[0:TB, :].rearrange("(j p) f -> p j f", p=P)
                             ).then_inc(tokens_loaded, 16)
                wait_apart(sp, y_stored, (end + 1) * 16, m.sp_passed)

            @block.tensor
            def _(pe):
                def turn(n):
                    pe.wait_ge(tokens_loaded, 16 * n + 16)
                    for j in range(TT):
                        for h in range(KD):
                            last = nc.tensor.transpose(turn_ps[:, h, j * P:(j + 1) * P],
                                                       tokens[:, j, h * P:(h + 1) * P], m.ident[:, :])
                    last.then_inc(turned, 1)

                def block_of(e, u, ii, n, first):
                    pe.wait_ge(weights_loaded[u], 64 * ii + 64)
                    pe.wait_ge(tokens_t_ready, n + 1)
                    for f in range(FC):
                        if f >= HB:
                            pe.wait_ge(by_dve if f % 2 else by_act, n * (FC // 2) + ((f - HB) // 2 + 1))
                        for k in range(KD):
                            last = nc.tensor.matmul(hidden_ps[f % HB], w1[u][:, k, f * P:(f + 1) * P],
                                                    tokens_t[:, k, :], start=(k == 0), stop=(k == KD - 1))
                        last.then_inc(hidden_done, 1)
                    turn(n + 1)
                    pe.wait_ge(y_ready, n * TT + TT)
                    for tt in range(TT):
                        for f in range(FC):
                            if tt == 0 and f in (0, FC - 2):
                                have = (n * (FC // 2)) + (FC // 2 - 1 if f == 0 else FC // 2)
                                pe.wait_ge(by_act, have)
                                pe.wait_ge(by_dve, have)
                            last = nc.tensor.matmul(y_ps[tt], hidden[:, f, tt * P:(tt + 1) * P], w2[u][:, f, :],
                                                    start=(f == 0), stop=(f == FC - 1))
                        last.then_inc(y_done, 1)

                pe.sem_inc(turned, 1)
                turn(0)
                each(pe, block_of)

            @block.scalar
            def _(act):
                def copy(n):
                    act.wait_ge(turned, n + 2)
                    nc.scalar.copy(tokens_t[:, :, :], turn_ps[:, :, :]).then_inc(tokens_t_ready, 1)

                def block_of(e, u, ii, n, first):
                    for f in range(0, FC, 2):
                        act.wait_ge(hidden_done, n * FC + (f + 1))
                        nc.scalar.activation(hidden[:, f, :], hidden_ps[f % HB], ACT.Relu, bias=b1[u][:, f:f + 1]
                                             ).then_inc(by_act, 1)
                    copy(n + 1)
                    act.wait_ge(y_ready, n * TT + 2 * TT)
                    act.dma_start(rows_of(m.ye, e, n, first), y[:, :, :]).then_inc(y_stored, 16)

                act.dma_start(m.ye[TRASH:TRASH + P, :], m.zeros[:, 0:D]).then_inc(y_stored, 16)
                copy(0)
                each(act, block_of)

            @block.vector
            def _(dve):
                def block_of(e, u, ii, n, first):
                    for f in range(1, FC, 2):
                        dve.wait_ge(hidden_done, n * FC + (f + 1))
                        nc.vector.tensor_scalar(hidden[:, f, :], hidden_ps[f % HB], b1[u][:, f:f + 1], 0.0,
                                                ALU.add, ALU.max).then_inc(by_dve, 1)
                    wait_apart(dve, y_stored, 16 * n + 16, m.passed)
                    for tt in range(TT):
                        dve.wait_ge(y_done, n * TT + (tt + 1))
                        nc.vector.tensor_tensor(y[:, tt, :], y_ps[tt], b2[u][:, :], ALU.add).then_inc(y_ready, 1)

                dve.sem_inc(y_ready, TT)
                each(dve, block_of)


def combine(nc, m):
    with ExitStack() as ctx:
        def sb(name, shape, dt=F32):
            return ctx.enter_context(nc.sbuf_tensor(name, shape, dt))

        sem = semaphores(nc, ctx)

        x2 = sb("x2_in", [P, 2, DT, D])
        ye = sb("ye_in", [P, 2, DT, D])
        scaled = sb("y_scaled", [P, DT, D])
        result = sb("y_result", [P, 2, DT, D])
        place_now = sb("place_now", [P, 2, DT], I32)
        prob_now = sb("prob_now", [P, 2, DT])
        finite = sb("finite", [P, DT, D], U8)
        nan = sb("nan", [P, DT, D], U8)
        zeros = sb("y_zeros", [P, DT, D])

        x2_loaded = [sem(f"c_x2_loaded{u}") for u in range(2)]
        gathered = [sem(f"gathered{u}") for u in range(2)]
        place_ready = sem("place_ready")
        prob_ready = sem("prob_ready")
        scaled_ready = sem("c_scaled_ready")
        masks = sem("c_masks")
        out_ready = sem("out_ready")
        out_stored = [sem(f"out_stored{u}") for u in range(2)]
        out_free = [sem(f"out_free{u}") for u in range(2)]
        zeroed = sem("c_zeroed")
        loops = NT // (2 * DT)

        def blocks(of):
            return of.rearrange("(b j p) f -> b p j f", p=P, j=DT)

        with nc.Block("combine") as block:
            @block.sync
            def _(sp):
                for u in range(2):
                    sp.sem_inc(out_free[u], 1)
                    sp.dma_start(x2[:, u, :, :], blocks(m.x2)[u]).then_inc(x2_loaded[u], 16)

                def store(b, i, u):
                    sp.wait_ge(out_ready, b + 3)
                    sp.dma_start(blocks(m.out)[bass.ds(b, 1)].rearrange("b p j f -> (b p) j f"),
                                 result[:, u, :, :]).then_inc(out_stored[u], 16)

                with sp.Fori(1, loops) as i:
                    for u in range(2):
                        b = 2 * i + u
                        store(b - 2, i - 1, u)
                        sp.dma_start(x2[:, u, :, :], blocks(m.x2)[bass.ds(b, 1)].rearrange("b p j f -> (b p) j f")
                                     ).then_inc(x2_loaded[u], 16)
                        sp.wait_ge(out_stored[u], 16 * i)
                        sp.sem_inc(out_free[u], 1)
                for u in range(2):
                    store(2 * (loops - 1) + u, loops - 1, u)
                for u in range(2):
                    sp.wait_ge(out_stored[u], 16 * loops)

            @block.gpsimd
            def _(pool):
                nc.gpsimd.memset(zeros[:, :, :], 0.0).then_inc(zeroed, 1)
                with pool.Fori(0, loops) as i:
                    for u in range(2):
                        b = 2 * i + u
                        wait_apart(pool, out_ready, b + 1, m.pool_passed)
                        nc.gpsimd.tensor_copy(place_now[:, u, :], m.place[:, bass.ds(b * DT, DT)]).then_inc(place_ready, 1)
                        nc.gpsimd.tensor_copy(prob_now[:, u, :], m.prob[:, bass.ds(b * DT, DT)]).then_inc(prob_ready, 1)
                        wait_apart(pool, place_ready, b + 1, m.pool_passed)
                        for j in range(DT):
                            nc.gpsimd.indirect_dma_start(
                                out=ye[:, u, j, :], out_offset=None, in_=m.ye[0:TRASH, :],
                                in_offset=bass.IndirectOffsetOnAxis(ap=place_now[:, u, j:j + 1], axis=0)
                            ).then_inc(gathered[u], 16)

            @block.scalar
            def _(act):
                with act.Fori(0, loops) as i:
                    for u in range(2):
                        b = 2 * i + u
                        act.wait_ge(prob_ready, b + 1)
                        act.wait_ge(gathered[u], 16 * DT * (i + 1))
                        act.wait_ge(out_ready, b + 2)
                        for j in range(DT):
                            last = nc.scalar.activation(scaled[:, j, :], ye[:, u, j, :], ACT.Copy,
                                                        scale=prob_now[:, u, j:j + 1])
                        last.then_inc(scaled_ready, 1)

            @block.vector
            def _(dve):
                dve.sem_inc(out_ready, 2)
                dve.wait_ge(zeroed, 1)
                with dve.Fori(0, loops) as i:
                    for u in range(2):
                        b = 2 * i + u
                        now = result[:, u, :, :]
                        dve.wait_ge(scaled_ready, b + 1)
                        dve.wait_ge(out_free[u], i + 1)
                        nc.vector.tensor_scalar(now, scaled[:, :, :], -1e4, 1e4, ALU.max, ALU.min)
                        nc.vector.tensor_scalar(finite[:, :, :], scaled[:, :, :], 0.0, 0.0,
                                                ALU.mult, ALU.is_equal)
                        nc.vector.tensor_tensor(nan[:, :, :], scaled[:, :, :], scaled[:, :, :],
                                                ALU.not_equal).then_inc(masks, 1)
                        wait_apart(dve, masks, 3 * b + 1, m.passed)
                        nc.vector.copy_predicated(now, finite[:, :, :], scaled[:, :, :]).then_inc(masks, 1)
                        wait_apart(dve, masks, 3 * b + 2, m.passed)
                        nc.vector.copy_predicated(now, nan[:, :, :], zeros[:, :, :]).then_inc(masks, 1)
                        dve.wait_ge(masks, 3 * b + 3)
                        dve.wait_ge(x2_loaded[u], 16 * i + 16)
                        nc.vector.tensor_tensor(now, now, x2[:, u, :, :], ALU.add).then_inc(out_ready, 1)


def program(nc, ins, out, scratch):
    m = Memory()
    (m.x, m.in_src, m.in_dst, m.in_dst_rows, m.in_wgt, m.in_w_g1, m.in_b_g1, m.in_w_g2, m.in_b_g2,
     m.in_w_q, m.in_w_k, m.in_w_v, m.in_w_m, m.in_w_1, m.in_w_2, m.in_ln1_g, m.in_ln1_b, m.in_ln2_g, m.in_ln2_b,
     m.in_gate_w, m.in_gate_b, m.w_e1, m.in_b_e1, m.w_e2, m.in_b_e2) = ins
    m.out = out
    m.xn = scratch("xn", [NP + P, D], F32)
    m.h1 = scratch("h1", [NP, D], F32)
    m.mix = scratch("mix", [NP, D], F32)
    m.x2 = scratch("x2", [NP, D], F32)
    m.xe = scratch("xe", [TRASH + DT * P, D], F32)
    m.ye = scratch("ye", [TRASH + P, D], F32)
    m.low_dram = scratch("low_dram", [TURNS, TURN], I32)
    m.more_dram = scratch("more_dram", [TURNS, 1], I32)

    with ExitStack() as ctx:
        def sb(name, shape, dt=F32):
            return ctx.enter_context(nc.sbuf_tensor(name, shape, dt))

        m.passed = ctx.enter_context(nc.semaphore("passed"))
        m.pool_passed = ctx.enter_context(nc.semaphore("pool_passed"))
        m.pe_passed = ctx.enter_context(nc.semaphore("pe_passed"))
        m.sp_passed = ctx.enter_context(nc.semaphore("sp_passed"))
        m.act_passed = ctx.enter_context(nc.semaphore("act_passed"))
        m.buffers_zeroed = ctx.enter_context(nc.semaphore("buffers_zeroed"))
        m.wgt = sb("wgt", [P, NCH + SLOTS])
        m.dst_rel = sb("dst_rel", [P, NCH + SLOTS])
        m.table = sb("table", [1, TURNS, TURN + 2], I32)
        m.cols = sb("cols", [P, WIN])
        m.eps = sb("eps", [P, 1])
        m.ident = sb("ident", [P, P])
        m.upto = sb("upto", [P, P])
        m.ones = sb("ones", [P, P])
        m.zeros = sb("zeros", [P, KD * KVS])
        m.valid = sb("valid", [P, NT])
        m.w_q = sb("w_q", [P, KD, D])
        m.w_m = sb("w_m", [P, KD, D])
        m.w_g2 = sb("w_g2", [P, KD, D])
        m.w_1 = sb("w_1", [P, 2 * KD, F1])
        m.w_2 = sb("w_2", [P, F1 // P, D])
        m.b_g1 = sb("b_g1", [1, D])
        m.b_g2 = sb("b_g2", [1, D])
        m.ln1_gh = sb("ln1_gh", [P, KD])
        m.ln2_gh = sb("ln2_gh", [P, D])
        m.ln1_b = sb("ln1_b", [P, KD])
        m.ln2_b = sb("ln2_b", [P, D])
        m.gate_w = sb("gate_w", [P, KD, NE])
        m.gate_b = sb("gate_b", [P, NE])
        m.blocks = sb("blocks", [1, NE, 2], I32)
        m.kv = sb("kv", [P, KD, KVW])
        m.place = sb("place", [P, NT], I32)
        m.prob = sb("prob", [P, NT])
        prepare(nc, m)
        with ExitStack() as agg_ctx:
            m.agg = agg_ctx.enter_context(nc.sbuf_tensor("agg", [P, KD, AGG], F32))
            gather(nc, m, 1, m.xn, keys_values)
            dense_first(nc, m)
            gather(nc, m, 2, m.h1, attend)
            dense_second(nc, m)
        experts(nc, m)
        combine(nc, m)


def kernel(x, src, dst, edge_weight, L0_gnn_W1, L0_gnn_b1, L0_gnn_W2, L0_gnn_b2, L0_mix_Wq, L0_mix_Wk, L0_mix_Wv,
           L0_mix_Wm, L0_mix_W1, L0_mix_W2, L0_mix_g1, L0_mix_b1, L0_mix_g2, L0_mix_b2, L0_ffn_gate_w, L0_ffn_gate_b,
           L0_ffn_w1, L0_ffn_b1, L0_ffn_w2, L0_ffn_b2):
    import concourse.bacc as bacc
    from concourse.bass_utils import run_bass_kernel_spmd as run

    nc = bacc.Bacc("TRN2", target_bir_lowering=False, num_devices=1)

    def padded(a, n, value=0):
        a = np.asarray(a)
        return np.concatenate([a, np.full((n - a.shape[0],) + a.shape[1:], value, a.dtype)])

    def columns(a):
        return np.ascontiguousarray(a.reshape(NCH, P).T)

    dst_padded = padded(dst, NCH * P, N - 1)
    arrays = {
        "x": padded(x, NP),
        "src": padded(src, NCH * P).reshape(TURNS, SLOTS, P).transpose(0, 2, 1),
        "dst": columns(dst_padded),
        "dst_rows": dst_padded.reshape(TURNS, SLOTS * P),
        "edge_weight": columns(padded(edge_weight, NCH * P)),
        "gnn_W1": L0_gnn_W1, "gnn_b1": L0_gnn_b1, "gnn_W2": L0_gnn_W2, "gnn_b2": L0_gnn_b2,
        "mix_Wq": L0_mix_Wq, "mix_Wk": L0_mix_Wk, "mix_Wv": L0_mix_Wv, "mix_Wm": L0_mix_Wm,
        "mix_W1": L0_mix_W1, "mix_W2": L0_mix_W2,
        "mix_g1": np.asarray(L0_mix_g1).reshape(KD, P).T, "mix_b1": np.asarray(L0_mix_b1).reshape(KD, P).T,
        "mix_g2": L0_mix_g2, "mix_b2": L0_mix_b2,
        "gate_w": L0_ffn_gate_w, "gate_b": L0_ffn_gate_b,
        "ffn_w1": L0_ffn_w1, "ffn_b1": np.asarray(L0_ffn_b1).reshape(NE, FC, P).transpose(2, 0, 1),
        "ffn_w2": L0_ffn_w2, "ffn_b2": L0_ffn_b2,
    }
    arrays = {f"in_{k}": np.ascontiguousarray(v) for k, v in arrays.items()}
    ins = [nc.dram_tensor(k, v.shape, mybir.dt.from_np(v.dtype), kind="ExternalInput").ap() for k, v in arrays.items()]
    out = nc.dram_tensor("out", (NP, D), F32, kind="ExternalOutput").ap()

    def scratch(name, shape, dt):
        return nc.dram_tensor(name, shape, dt, kind=SCRATCH_KIND).ap()

    program(nc, ins, out, scratch)
    return run(nc, [arrays], core_ids=[0]).results[0]["out"][:N]


SCRATCH_KIND = "Internal"
```

```python
import concourse.bass as bass
from concourse import mybir
from contextlib import ExitStack
import numpy as np

F32 = mybir.dt.float32
I32 = mybir.dt.int32
U32 = mybir.dt.uint32
U8 = mybir.dt.uint8
ALU = mybir.AluOpType
ACT = mybir.ActivationFunctionType
AX = mybir.AxisListType

P = 128
N = 12500
D = 256
KD = D // P
E = 212500
GROUP = 8
TURN = 2
SLOTS = GROUP * TURN
TURNS = -(-E // (P * SLOTS))
NCH = TURNS * SLOTS
NT = TURNS
NP = NT * P
WIN = 128
AGG = NP + WIN
LN_EPS = 1e-5
ATT_EPS = 1e-6
H = 8
HC = P // (D // H)
HD = D // H
KVW = P + HC
BANK = 512
KVS = P + 1
F1 = 512
NE = 8
F = 1024
FC = F // P
CAP = -(-5 * N // (4 * NE))
ROWS = -(-CAP // P) * P
TB = 256
TRASH = NE * ROWS
PB = 4
PSLOTS = 2
DT = 4
PAIR = 2
TABLES = "natural_log_exp_and_others"
LOG_WIN = 7
LOG_TB = 8
assert 1 << LOG_WIN == WIN and 1 << LOG_TB == TB and NP >= N and TURNS % 2 == 0 and NT % (PB * PSLOTS) == 0 and NT % (2 * DT) == 0


def wait_apart(engine, semaphore, value, passed):
    engine.wait_ge(semaphore, value)
    engine.sem_inc(passed, 1)


def semaphores(nc, ctx, suffix=""):
    taken = []

    def sem(name):
        taken.append(nc.alloc_semaphore(name=f"{name}{suffix}"))
        return taken[-1]

    def clear():
        nc.clear_and_free_semaphores(taken)
        nc.all_engine_barrier()

    ctx.callback(clear)
    return sem


class Memory:
    pass


def prepare(nc, m):
    with ExitStack() as ctx:
        def sb(name, shape, dt):
            return ctx.enter_context(nc.sbuf_tensor(name, shape, dt))

        sem = semaphores(nc, ctx)

        rows = sb("ln_rows", [P, PSLOTS, PB, D], F32)
        normed = sb("ln_normed", [P, PSLOTS, PB, D], F32)
        stats = sb("ln_stats", [P, PSLOTS, PB, 6], F32)
        mv = sb("ln_mean_var", [P, PSLOTS, PB, 2], F32)
        sd = sb("ln_sd", [P, PSLOTS, PB], F32)
        rstd = sb("ln_rstd", [P, PSLOTS, PB], F32)
        dst_rows = sb("dst_rows", [TURNS, TURN, GROUP * P], I32)
        low = sb("low", [TURNS, TURN], I32)
        high = sb("high", [TURNS, TURN], I32)
        span = sb("span", [TURNS, TURN], I32)
        more = sb("more", [TURNS, 1], I32)
        dst_i = sb("dst_i", [P, NCH], I32)
        dst_f = sb("dst_f", [P, NCH], F32)
        low_all = sb("low_all", [P, TURNS * TURN], I32)
        low_f = sb("low_f", [P, TURNS * TURN], F32)
        more_row = sb("more_row", [1, TURNS], I32)
        more_f = sb("more_f", [1, TURNS], F32)
        more_sum = sb("more_sum", [1, TURNS], F32)
        more_one = sb("more_one", [1, TURNS], F32)
        iota_i = sb("iota_i", [P, WIN], I32)
        node_i = sb("node_i", [P, NT], I32)

        consts_loaded = sem("consts_loaded")
        edges_loaded = sem("edges_loaded")
        x_loaded = [sem(f"x_loaded{s}") for s in range(PSLOTS)]
        mv_done = sem("mean_var_done")
        sd_done = sem("sd_done")
        eps_set = sem("eps_set")
        rstd_done = sem("rstd_done")
        xn_done = sem("xn_done")
        xn_stored = [sem(f"xn_stored{s}") for s in range(PSLOTS)]
        step = sem("prepare_step")
        spans_done = sem("spans_done")
        spans_stored = sem("spans_stored")
        spans_back = sem("spans_back")
        iotas_done = sem("iotas_done")
        tables_done = sem("tables_done")
        zero_set = sem("zero_set")
        pad_stored = sem("pad_stored")

        x_blocks = m.x.rearrange("(b p j) f -> b p j f", p=P, j=PB)
        xn_blocks = m.xn[0:NP, :].rearrange("(b p j) f -> b p j f", p=P, j=PB)
        n_blocks = NT // PB
        loops = n_blocks // PSLOTS
        consts = [
            (m.w_q[:, :, :], m.in_w_q.rearrange("(k p) n -> p k n", p=P)),
            (m.w_m[:, :, :], m.in_w_m.rearrange("(k p) n -> p k n", p=P)),
            (m.w_g2[:, :, :], m.in_w_g2.rearrange("(k p) n -> p k n", p=P)),
            (m.w_1[:, :, :], m.in_w_1.rearrange("(k p) n -> p k n", p=P)),
            (m.w_2[:, :, :], m.in_w_2.rearrange("(k p) n -> p k n", p=P)),
            (m.b_g1[:, :], m.in_b_g1.rearrange("(o n) -> o n", o=1)),
            (m.b_g2[:, :], m.in_b_g2.rearrange("(o n) -> o n", o=1)),
            (m.ln1_gh[:, :], m.in_ln1_g),
            (m.ln1_b[:, :], m.in_ln1_b),
            (m.ln2_gh[:, :], m.in_ln2_g.rearrange("(o n) -> o n", o=1).to_broadcast([P, D])),
            (m.ln2_b[:, :], m.in_ln2_b.rearrange("(o n) -> o n", o=1).to_broadcast([P, D])),
            (m.gate_w[:, :, :], m.in_gate_w.rearrange("(k p) n -> p k n", p=P)),
            (m.gate_b[:, :], m.in_gate_b.rearrange("(o n) -> o n", o=1).to_broadcast([P, NE])),
            (m.wgt[:, 0:NCH], m.in_wgt),
        ]

        with nc.Block("prepare") as block:
            @block.sync
            def _(sp):
                sp.dma_start(dst_rows[:, :, :],
                             m.in_dst_rows.rearrange("t (g e) -> t g e", g=TURN)).then_inc(edges_loaded, 16)
                sp.dma_start(dst_i[:, :], m.in_dst).then_inc(edges_loaded, 16)
                for s in range(PSLOTS):
                    sp.dma_start(rows[:, s, :, :], x_blocks[s]).then_inc(x_loaded[s], 16)
                with sp.Fori(1, loops) as i:
                    for s in range(PSLOTS):
                        sp.wait_ge(xn_done, i * PSLOTS + (s + 1 - PSLOTS))
                        sp.dma_start(rows[:, s, :, :],
                                     x_blocks[bass.ds(i * PSLOTS + s, 1)].rearrange("b p j f -> (b p) j f")
                                     ).then_inc(x_loaded[s], 16)
                for to, of in consts:
                    sp.dma_start(to, of).then_inc(consts_loaded, 16)
                sp.wait_ge(spans_done, 2)
                sp.dma_start(m.low_dram[:, :], low[:, :]).then_inc(spans_stored, 16)
                sp.dma_start(m.more_dram[:, :], more[:, :]).then_inc(spans_stored, 16)
                sp.wait_ge(spans_stored, 32)
                sp.dma_start(low_all[:, :],
                             m.low_dram.rearrange("(o t) g -> o (t g)", o=1).to_broadcast([P, TURNS * TURN])
                             ).then_inc(spans_back, 16)
                sp.dma_start(m.table[0:1, :, 0:TURN],
                             m.low_dram.rearrange("(o t) g -> o t g", o=1)).then_inc(spans_back, 16)
                sp.dma_start(more_row[:, :],
                             m.more_dram.rearrange("(o t) g -> o (t g)", o=1)).then_inc(spans_back, 16)
                sp.wait_ge(consts_loaded, 16 * len(consts))

            @block.scalar
            def _(act):
                def store(i, s):
                    act.wait_ge(xn_done, i * PSLOTS + s + 1)
                    act.dma_start(xn_blocks[bass.ds(i * PSLOTS + s, 1)].rearrange("b p j f -> (b p) j f"),
                                  normed[:, s, :, :]).then_inc(xn_stored[s], 16)

                act.wait_ge(eps_set, 1)
                with act.Fori(0, loops) as i:
                    for s in range(PSLOTS):
                        act.wait_ge(mv_done, i * PSLOTS + s + 1)
                        nc.scalar.activation(sd[:, s, :], mv[:, s, :, 1], ACT.Sqrt,
                                             bias=m.eps[:, 0:1]).then_inc(sd_done, 1)
                        if s:
                            store(i, s - 1)
                    store(i, PSLOTS - 1)
                act.wait_ge(zero_set, 1)
                act.dma_start(m.xn[NP:NP + P, :], m.zeros[:, 0:D]).then_inc(pad_stored, 16)
                for buffer in (m.xe[0:TRASH, :], m.ye):
                    act.dma_start(buffer.rearrange("(p n) f -> p n f", p=P),
                                  m.zeros[:, 0:D].rearrange("p (o f) -> p o f", o=1)
                                  .to_broadcast([P, buffer.shape[0] // P, D])).then_inc(m.buffers_zeroed, 16)
                act.wait_ge(pad_stored, 16)
                for s in range(PSLOTS):
                    act.wait_ge(xn_stored[s], 16 * loops)

            @block.gpsimd
            def _(pool):
                nc.gpsimd.memset(m.zeros[:, :], 0.0).then_inc(zero_set, 1)
                nc.gpsimd.memset(m.ones[:, :], 1.0).then_inc(zero_set, 1)
                nc.gpsimd.iota(iota_i[:, :], [[1, WIN]], base=0, channel_multiplier=0).then_inc(iotas_done, 1)
                nc.gpsimd.iota(node_i[:, :], [[P, NT]], base=0, channel_multiplier=1).then_inc(iotas_done, 1)
                pool.wait_ge(zero_set, 2)
                nc.gpsimd.affine_select(out=m.ident[:, :], in_=m.zeros[:, 0:P], compare_op=ALU.not_equal, fill=1.0,
                                        base=0, pattern=[[-1, P]], channel_multiplier=1).then_inc(iotas_done, 1)
                nc.gpsimd.affine_select(out=m.upto[:, :], in_=m.ones[:, :], compare_op=ALU.is_ge, fill=0.0,
                                        base=0, pattern=[[1, P]], channel_multiplier=-1).then_inc(iotas_done, 1)

            @block.vector
            def _(dve):
                nc.vector.memset(m.eps[:, :], LN_EPS).then_inc(eps_set, 1)
                dve.wait_ge(edges_loaded, 32)
                nc.vector.tensor_reduce(low[:, :], dst_rows[:, :, :], AX.X, ALU.min).then_inc(spans_done, 1)
                nc.vector.tensor_reduce(high[:, :], dst_rows[:, :, :], AX.X, ALU.max).then_inc(step, 1)
                nc.vector.tensor_copy(dst_f[:, :], dst_i[:, :]).then_inc(step, 1)
                dve.wait_ge(step, 2)
                nc.vector.tensor_tensor(span[:, :], high[:, :], low[:, :], ALU.subtract).then_inc(step, 1)
                dve.wait_ge(step, 3)
                nc.vector.tensor_scalar(high[:, :], span[:, :], LOG_WIN, None,
                                        ALU.arith_shift_right).then_inc(step, 1)
                dve.wait_ge(step, 4)
                nc.vector.tensor_reduce(more[:, :], high[:, :], AX.X, ALU.max).then_inc(spans_done, 1)
                stat_steps = 5

                def turn(i, s, first):
                    dve.wait_ge(x_loaded[s], 16 * i + 16)
                    for j in range(PB):
                        last = nc.vector.bn_stats(stats[:, s, j, :], rows[:, s, j, :])
                    last.then_inc(step, 1)
                    wait_apart(dve, step, i * PSLOTS + (s + stat_steps), m.passed)
                    for j in range(PB):
                        last = nc.vector.bn_aggr(mv[:, s, j, :], stats[:, s, j, :])
                    last.then_inc(mv_done, 1)
                    dve.wait_ge(sd_done, i * PSLOTS + s + 1)
                    nc.vector.reciprocal(rstd[:, s, :], sd[:, s, :]).then_inc(rstd_done, 1)
                    dve.wait_ge(rstd_done, i * PSLOTS + s + 1)
                    if not first:
                        dve.wait_ge(xn_stored[s], 16 * i)
                    for j in range(PB):
                        last = nc.vector.tensor_scalar(normed[:, s, j, :], rows[:, s, j, :], mv[:, s, j, 0:1],
                                                       rstd[:, s, j:j + 1], ALU.subtract, ALU.mult)
                    last.then_inc(xn_done, 1)

                for s in range(PSLOTS):
                    turn(0, s, True)
                with dve.Fori(1, loops) as i:
                    for s in range(PSLOTS):
                        turn(i, s, False)
                dve.wait_ge(iotas_done, 4)
                nc.vector.tensor_copy(m.cols[:, :], iota_i[:, :]).then_inc(tables_done, 1)
                nc.vector.tensor_scalar(m.valid[:, :], node_i[:, :], float(N), None, ALU.is_lt).then_inc(tables_done, 1)
                dve.wait_ge(spans_back, 48)
                nc.vector.tensor_copy(low_f[:, :], low_all[:, :]).then_inc(tables_done, 1)
                nc.vector.tensor_copy(more_f[:, :], more_row[:, :]).then_inc(tables_done, 1)
                nc.vector.memset(more_one[:, :], 1.0).then_inc(tables_done, 1)
                dve.wait_ge(tables_done, 5)
                nc.vector.tensor_tensor(m.dst_rel[:, 0:NCH].rearrange("p (g c) -> p g c", c=GROUP),
                                        dst_f[:, :].rearrange("p (g c) -> p g c", c=GROUP),
                                        low_f[:, :].rearrange("p (g o) -> p g o", o=1)
                                        .to_broadcast([P, TURNS * TURN, GROUP]), ALU.subtract).then_inc(tables_done, 1)
                nc.vector.tensor_tensor_scan(more_sum[:, :], more_one[:, :], more_f[:, :], 0.0,
                                             ALU.mult, ALU.add).then_inc(tables_done, 1)
                dve.wait_ge(tables_done, 7)
                nc.vector.tensor_copy(m.table[0:1, :, TURN + 1], more_sum[:, :]).then_inc(tables_done, 1)
                nc.vector.tensor_tensor(m.table[0:1, :, TURN], more_sum[:, :], more_f[:, :],
                                        ALU.subtract).then_inc(tables_done, 1)
                nc.vector.memset(m.dst_rel[:, NCH:NCH + SLOTS], 0.0).then_inc(tables_done, 1)
                nc.vector.memset(m.wgt[:, NCH:NCH + SLOTS], 0.0).then_inc(tables_done, 1)
                dve.wait_ge(consts_loaded, 16 * len(consts))
                nc.vector.tensor_scalar(m.ln1_gh[:, :], m.ln1_gh[:, :], -0.5, None, ALU.mult).then_inc(tables_done, 1)
                nc.vector.tensor_scalar(m.ln2_gh[:, :], m.ln2_gh[:, :], -0.5, None, ALU.mult).then_inc(tables_done, 1)
                dve.wait_ge(tables_done, 13)


def gather(nc, m, layer, source, mixer):
    with ExitStack() as ctx:
        def sb(name, shape, dt=F32):
            return ctx.enter_context(nc.sbuf_tensor(f"{name}{layer}", shape, dt))

        sem = semaphores(nc, ctx, layer)

        def ps(name, a, b):
            bank = ctx.enter_context(nc.psum_tensor(f"{name}{layer}", [P, BANK], F32))
            return bank[:, 0:a * b].rearrange("p (a b) -> p a b", a=a)

        rows = sb("rows", [P, 2, SLOTS, D])
        sel = sb("sel", [P, SLOTS, WIN])
        idx = sb("idx", [P, 2, SLOTS], I32)
        rel_now = sb("rel_now", [P, SLOTS])
        wgt_now = sb("wgt_now", [P, SLOTS])
        sums = [ps(f"sums{g}_", KD, WIN) for g in range(TURN)]

        idx_loaded = [sem(f"idx_loaded{u}_") for u in range(2)]
        rows_loaded = [[sem(f"rows_loaded{u}{g}_") for g in range(TURN)] for u in range(2)]
        rows_used = [sem(f"rows_used{u}_") for u in range(2)]
        sel_ready = [sem(f"sel_ready{g}_") for g in range(TURN)]
        summed = [sem(f"summed{g}_") for g in range(TURN)]
        now_ready = sem("now_ready")
        added = sem("added")
        agg_zeroed = sem("agg_zeroed")
        further_sel = sem("further_sel")
        further_sum = sem("further_sum")
        further_step = sem("further_step")

        mix = mixer(nc, m, sb, sem, ps)
        loops = TURNS // 2

        def window_products(g, h, u, before):
            for c in range(GROUP):
                k = g * GROUP + c
                last = nc.tensor.matmul(sums[g][:, h, :], rows[:, u, k, h * P:(h + 1) * P], sel[:, k, :],
                                        start=(c == 0), stop=(c == GROUP - 1))
                if c == 0 and before is not None:
                    last.then_inc(before, 1)
            return last

        def selection(g):
            for c in range(GROUP):
                k = g * GROUP + c
                last = nc.vector.tensor_scalar(sel[:, k, :], m.cols[:, :], rel_now[:, k:k + 1], wgt_now[:, k:k + 1],
                                               ALU.is_equal, ALU.mult)
            return last

        def add_window(g, at):
            window = m.agg[:, :, bass.ds(at, WIN)]
            return nc.vector.tensor_tensor(window, window, sums[g][:, :, :], ALU.add)

        def turns(engine, body):
            for u in range(2):
                body(0, u)
            with engine.Fori(1, loops) as i:
                for u in range(2):
                    body(i, u)

        with nc.Block(f"gather{layer}") as block:
            @block.sync
            def _(sp):
                for u in range(2):
                    sp.dma_start(idx[:, u, :], m.in_src[u]).then_inc(idx_loaded[u], 16)
                    mix.load(sp, u, u)
                mix.load_weights(sp)
                with sp.Fori(1, loops) as i:
                    for u in range(2):
                        sp.wait_ge(rows_loaded[u][TURN - 1], 16 * GROUP * i)
                        sp.dma_start(idx[:, u, :], m.in_src[bass.ds(2 * i + u, 1)].rearrange("o p c -> (o p) c")
                                     ).then_inc(idx_loaded[u], 16)
                        mix.free(sp, i - 1, u)
                        mix.load(sp, 2 * i + u, u)
                        mix.store(sp, i - 1, u)
                mix.load_past(sp)
                mix.stored(sp)
                sp.wait_ge(m.buffers_zeroed, 32)

            @block.gpsimd
            def _(pool):
                with pool.Fori(0, loops) as i:
                    for u in range(2):
                        pool.wait_ge(idx_loaded[u], 16 * i + 16)
                        wait_apart(pool, rows_used[u], i + 1, m.pool_passed)
                        for k in range(SLOTS):
                            nc.gpsimd.indirect_dma_start(
                                out=rows[:, u, k, :], out_offset=None, in_=source,
                                in_offset=bass.IndirectOffsetOnAxis(ap=idx[:, u, k:k + 1], axis=0)
                            ).then_inc(rows_loaded[u][k // GROUP], 16)

            @block.vector
            def _(dve):
                def take(t):
                    nc.vector.tensor_copy(rel_now[:, :], m.dst_rel[:, bass.ds(t * SLOTS, SLOTS)]).then_inc(now_ready, 1)
                    nc.vector.tensor_copy(wgt_now[:, :], m.wgt[:, bass.ds(t * SLOTS, SLOTS)]).then_inc(now_ready, 1)
                    dve.wait_ge(now_ready, 2 * t + 2)
                    selection(0).then_inc(sel_ready[0], 1)

                nc.vector.memset(m.agg[:, :, :], 0.0).then_inc(agg_zeroed, 1)
                mix.dve_begin(dve)
                dve.wait_ge(agg_zeroed, 1)
                take(0)
                def turn(i, u):
                    t = 2 * i + u
                    mix.dve(dve, i, u, 0)
                    selection(1).then_inc(sel_ready[1], 1)
                    mix.dve(dve, i, u, 1)
                    low = [dve.value_load(m.table[0:1, bass.ds(t, 1), g], min_val=0, max_val=N - 1)
                           for g in range(TURN)]
                    dve.wait_ge(summed[0], t + 1)
                    add_window(0, low[0]).then_inc(added, 1)
                    mix.dve(dve, i, u, 2)
                    first = dve.value_load(m.table[0:1, bass.ds(t, 1), TURN], min_val=0, max_val=NP)
                    end = dve.value_load(m.table[0:1, bass.ds(t, 1), TURN + 1], min_val=0, max_val=NP)
                    dve.wait_ge(summed[1], t + 1)
                    wait_apart(dve, added, 2 * t + 1, m.passed)
                    add_window(1, low[1]).then_inc(added, 1)
                    wait_apart(dve, added, 2 * t + 2, m.passed)
                    with dve.If(first < end):
                        with dve.Fori(first, end) as w:
                            nc.vector.tensor_scalar(rel_now[:, :], rel_now[:, :], float(-WIN), None,
                                                    ALU.add).then_inc(further_step, 1)
                            dve.wait_ge(further_step, 3 * w + 1)
                            for g in range(TURN):
                                last = selection(g)
                            last.then_inc(further_sel, 1)
                            dve.wait_ge(further_sum, w + 1)
                            for g in range(TURN):
                                at = low[g] + (w - first + 1) * WIN
                                inside = at <= NP
                                at = dve.snap(inside * at + (1 - inside) * NP).with_bounds(min_val=0, max_val=NP)
                                add_window(g, at).then_inc(further_step, 1)
                                wait_apart(dve, further_step, 3 * w + g + 2, m.passed)
                    take(t + 1)
                    mix.dve(dve, i, u, 3)

                turns(dve, turn)
                mix.dve_end(dve)

            @block.scalar
            def _(act):
                mix.act_begin(act)
                turns(act, lambda i, u: mix.act(act, i, u))
                mix.act_end(act)

            @block.tensor
            def _(pe):
                pe.sem_inc(rows_used[0], 1)
                mix.pe_begin(pe)

                def turn(i, u):
                    t = 2 * i + u
                    first = pe.value_load(m.table[0:1, bass.ds(t, 1), TURN], min_val=0, max_val=NP)
                    end = pe.value_load(m.table[0:1, bass.ds(t, 1), TURN + 1], min_val=0, max_val=NP)
                    mix.pe(pe, i, u, 0)
                    for g in range(TURN):
                        for h in range(KD):
                            if h == 0:
                                pe.wait_ge(sel_ready[g], t + 1)
                                pe.wait_ge(rows_loaded[u][g], 16 * GROUP * (i + 1))
                            last = window_products(g, h, u, rows_used[1 - u] if g == 0 and h == 0 else None)
                            if h == KD - 1:
                                last.then_inc(summed[g], 1)
                            if g * KD + h < TURN * KD - 1:
                                mix.pe(pe, i, u, 1 + g * KD + h)
                    with pe.If(first < end):
                        with pe.Fori(first, end) as w:
                            pe.wait_ge(further_sel, w + 1)
                            for g in range(TURN):
                                for h in range(KD):
                                    last = window_products(g, h, u, None)
                            last.then_inc(further_sum, 1)
                    mix.pe(pe, i, u, TURN * KD)

                turns(pe, turn)
                mix.pe_end(pe)
        mix.after()


def keys_values(nc, m, sb, sem, ps):
    mix = Memory()
    w_k = sb("w_k", [P, KD, D])
    w_v = sb("w_v", [P, KD, D])
    tile = sb("kv_tile", [P, 2, D])
    xt = sb("kv_xt", [P, KD, P])
    k_min = sb("k_min", [P, D])
    k_exp = sb("k_exp", [P, D])
    keys = sb("keys", [P, D])
    values = sb("values", [P, KD, KVS])
    turned = ps("kv_turned", KD, P)
    proj = [ps(f"kv_proj{n}_", 1, D) for n in range(2)]
    total = ps("kv_total", KD, KVS)

    weights_loaded = sem("kv_weights_loaded")
    tile_loaded = [sem(f"kv_tile_loaded{u}_") for u in range(2)]
    tile_turned = sem("kv_tile_turned")
    xt_ready = sem("kv_xt_ready")
    projected = sem("kv_projected")
    k_min_ready = sem("k_min_ready")
    k_exp_ready = sem("k_exp_ready")
    keys_ready = sem("keys_ready")
    values_ready = sem("values_ready")
    total_opened = sem("kv_total_opened")
    total_done = sem("kv_total_done")
    kv_zeroed = sem("kv_zeroed")
    kv_done = sem("kv_done")

    def load(sp, t, u):
        sp.dma_start(tile[:, u, :], m.xn[bass.ds(t * P, P), :]).then_inc(tile_loaded[u], 16)

    def load_weights(sp):
        for to, of in ((w_k, m.in_w_k), (w_v, m.in_w_v)):
            sp.dma_start(to[:, :, :], of.rearrange("(k p) n -> p k n", p=P)).then_inc(weights_loaded, 16)

    def free(sp, i, u):
        sp.wait_ge(tile_turned, 2 * i + (u + 1))

    def pe_begin(pe):
        pe.wait_ge(weights_loaded, 32)
        nc.tensor.matmul(total[:, :, :], m.ident[:, :], m.zeros[:, :].rearrange("p (k n) -> p k n", k=KD),
                         start=True, stop=False)

    def pe(pe, i, u, place):
        t = 2 * i + u
        if place == 0:
            pe.wait_ge(tile_loaded[u], 16 * i + 16)
            for h in range(KD):
                last = nc.tensor.transpose(turned[:, h, :], tile[:, u, h * P:(h + 1) * P], m.ident[:, :])
            last.then_inc(tile_turned, 1)
        if place == 1:
            pe.wait_ge(xt_ready, t + 1)
            for n, w in enumerate((w_k, w_v)):
                for k in range(KD):
                    last = nc.tensor.matmul(proj[n][:, 0, :], xt[:, k, :], w[:, k, :], start=(k == 0), stop=(k == KD - 1))
            last.then_inc(projected, 1)
        if place == 3:
            pe.wait_ge(keys_ready, t + 1)
            pe.wait_ge(values_ready, 2 * t + 2)
            for h in range(KD):
                nc.tensor.matmul(total[:, h, :], keys[:, h * P:(h + 1) * P], values[:, h, :], start=False, stop=False)

    def pe_end(pe):
        nc.tensor.matmul(total[:, :, :], m.ident[:, :], m.zeros[:, :].rearrange("p (k n) -> p k n", k=KD),
                         start=False, stop=True).then_inc(total_done, 1)

    def dve(dve, i, u, place):
        t = 2 * i + u
        if place == 1:
            dve.wait_ge(projected, t + 1)
            nc.vector.tensor_scalar(k_min[:, :], proj[0][:, 0, :], 0.0, None, ALU.min).then_inc(k_min_ready, 1)
        if place == 2:
            dve.wait_ge(k_exp_ready, t + 1)
            nc.vector.scalar_tensor_tensor(keys[:, :], proj[0][:, 0, :], 0.0, k_exp[:, :],
                                           ALU.max, ALU.add).then_inc(keys_ready, 1)

    def act(act, i, u):
        t = 2 * i + u
        act.wait_ge(tile_turned, t + 1)
        nc.scalar.copy(xt[:, :, :], turned[:, :, :]).then_inc(xt_ready, 1)
        act.wait_ge(projected, t + 1)
        nc.scalar.copy(values[:, :, 0:P], proj[1][:, 0, :].rearrange("p (k n) -> p k n", k=KD)).then_inc(values_ready, 1)
        nc.scalar.copy(values[:, :, P:KVS],
                       m.valid[:, bass.ds(t, 1)].rearrange("p (o n) -> p o n", o=1).to_broadcast([P, KD, 1])
                       ).then_inc(values_ready, 1)
        act.wait_ge(k_min_ready, t + 1)
        nc.scalar.activation(k_exp[:, :], k_min[:, :], ACT.Exp).then_inc(k_exp_ready, 1)

    def after():
        with nc.Block("kv") as block:
            @block.vector
            def _(dve):
                dve.wait_ge(total_done, 1)
                nc.vector.memset(m.kv[:, :, :], 0.0).then_inc(kv_zeroed, 1)
                dve.wait_ge(kv_zeroed, 1)
                for j in range(HC):
                    head = slice(j * HD, (j + 1) * HD)
                    nc.vector.tensor_scalar(m.kv[head, :, head], total[head, :, head], 1.0 / N, None, ALU.mult)
                    nc.vector.tensor_copy(m.kv[head, :, P + j:P + j + 1], total[head, :, P:KVS]).then_inc(kv_done, 1)
                dve.wait_ge(kv_done, HC)

    mix.load, mix.free, mix.pe_begin, mix.pe, mix.pe_end = load, free, pe_begin, pe, pe_end
    mix.dve, mix.act, mix.after = dve, act, after
    mix.store = lambda sp, i, u: None
    mix.load_weights = load_weights
    mix.load_past = mix.stored = mix.dve_begin = mix.act_begin = mix.dve_end = mix.act_end = lambda engine: None
    return mix


def attend(nc, m, sb, sem, ps):
    mix = Memory()
    tile = sb("tile", [P, 2, D])
    xt = sb("xt", [P, 2, KD, P])
    q_min = sb("q_min", [P, KD, P])
    queries = sb("queries", [P, KD, P])
    den = sb("den", [P, KD, HC])
    inv = sb("inv", [P, KD, HC])
    msg = sb("msg", [P, D])
    msg_t = sb("msg_t", [P, KD, P])
    norm_t = sb("norm_t", [P, KD, P])
    hidden = sb("hidden", [P, F1 // P, P])
    scaled = sb("scaled", [P, D])
    result = sb("result", [P, 2, D])
    stats = sb("stats", [P, 2, 6])
    mv = sb("mv", [P, 2, 2])
    var = sb("var", [P, 2, 1])
    ln_var = sb("ln_var", [P, 2, 1])
    guess = sb("guess", [P, 2, 1])
    square = sb("square", [P, 2, 1])
    inv_sd = sb("inv_sd", [P, 2, 1])

    tile_ps = ps("tile_ps", KD, P)
    query_ps = tile_ps
    num_ps = ps("num_ps", KD, KVW)
    turn_ps = ps("turn_ps", KD, P)
    row_ps = [ps(f"row_ps{n}_", 1, D)[:, 0, :] for n in range(2)]
    hidden_ps = ps("hidden_ps", F1 // P, P)

    tile_loaded = [sem(f"tile_loaded{u}_") for u in range(2)]
    tile_turned = sem("tile_turned")
    xt_ready = sem("xt_ready")
    query_projected = sem("query_projected")
    q_min_ready = sem("q_min_ready")
    q_exp_ready = sem("q_exp_ready")
    queries_ready = sem("queries_ready")
    num_ready = sem("num_ready")
    den_ready = sem("den_ready")
    inv_ready = sem("inv_ready")
    msg_ready = sem("msg_ready")
    msg_turned = sem("msg_turned")
    msg_t_ready = sem("msg_t_ready")
    msg_projected = sem("msg_projected")
    normed_ready = sem("normed_ready")
    norm_turned = sem("norm_turned")
    norm_t_ready = sem("norm_t_ready")
    hidden_done = sem("hidden_done")
    hidden_ready = sem("hidden_ready")
    mlp_done = sem("mlp_done")
    base_ready = sem("base_ready")
    scaled_ready = sem("scaled_ready")
    mixed = sem("mixed")
    stored = [sem(f"mix_stored{u}_") for u in range(2)]
    result_free = [sem(f"result_free{u}_") for u in range(2)]
    ln_step = [sem(f"ln_step{n}_") for n in range(2)]
    var_ready = [sem(f"var_ready{n}_") for n in range(2)]
    log_ready = [sem(f"log_ready{n}_") for n in range(2)]
    guess_ready = [sem(f"guess_ready{n}_") for n in range(2)]
    inv_sd_ready = [sem(f"inv_sd_ready{n}_") for n in range(2)]

    def is_first(i, u):
        return isinstance(i, int) and i == 0 and u == 0

    def load(sp, t, u):
        sp.dma_start(tile[:, u, :], m.xn[bass.ds(t * P, P), :]).then_inc(tile_loaded[u], 16)

    def free(sp, i, u):
        sp.wait_ge(base_ready, 2 * i + (u + 1))

    def store(sp, i, u):
        t = 2 * i + u
        sp.wait_ge(mixed, t + 1)
        sp.dma_start(m.mix[bass.ds(t * P, P), :], result[:, u, :]).then_inc(stored[u], 16)
        sp.wait_ge(stored[u], 16 * i + 16)
        sp.sem_inc(result_free[u], 1)

    def load_past(sp):
        free(sp, TURNS // 2 - 1, 0)
        load(sp, TURNS, 0)

    def all_stored(sp):
        for u in range(2):
            store(sp, TURNS // 2 - 1, u)

    def turn_tile(pe, t, u, i):
        pe.wait_ge(tile_loaded[u], 16 * i + 16)
        for h in range(KD):
            last = nc.tensor.transpose(tile_ps[:, h, :], tile[:, u, h * P:(h + 1) * P], m.ident[:, :])
        last.then_inc(tile_turned, 1)

    def project_queries(pe, t, u):
        pe.wait_ge(xt_ready, t + 1)
        for h in range(KD):
            for k in range(KD):
                last = nc.tensor.matmul(query_ps[:, h, :], m.w_q[:, k, h * P:(h + 1) * P], xt[:, u, k, :],
                                        start=(k == 0), stop=(k == KD - 1))
        last.then_inc(query_projected, 1)

    def mlp_output(pe, t):
        pe.wait_ge(hidden_ready, t + 1)
        for o in range(F1 // P):
            last = nc.tensor.matmul(row_ps[1], hidden[:, o, :], m.w_2[:, o, :], start=(o == 0),
                                    stop=(o == F1 // P - 1))
        last.then_inc(mlp_done, 1)

    def pe_begin(pe):
        turn_tile(pe, 0, 0, 0)
        project_queries(pe, 0, 0)

    def pe(pe, i, u, place):
        t = 2 * i + u
        if place == 1:
            pe.wait_ge(queries_ready, t + 1)
            for h in range(KD):
                last = nc.tensor.matmul(num_ps[:, h, :], queries[:, h, :], m.kv[:, h, :], start=True, stop=True)
            last.then_inc(num_ready, 1)
            if not is_first(i, u):
                mlp_output(pe, t - 1)
        if place == 2:
            pe.wait_ge(msg_ready, t + 1)
            for h in range(KD):
                last = nc.tensor.transpose(turn_ps[:, h, :], msg[:, h * P:(h + 1) * P], m.ident[:, :])
            last.then_inc(msg_turned, 1)
            turn_tile(pe, t + 1, 1 - u, i + u)
            pe.wait_ge(msg_t_ready, t + 1)
            for k in range(KD):
                last = nc.tensor.matmul(row_ps[0], msg_t[:, k, :], m.w_m[:, k, :], start=(k == 0), stop=(k == KD - 1))
            last.then_inc(msg_projected, 1)
        if place == 4:
            pe.wait_ge(normed_ready, t + 1)
            for h in range(KD):
                last = nc.tensor.transpose(turn_ps[:, h, :], msg[:, h * P:(h + 1) * P], m.ident[:, :])
            last.then_inc(norm_turned, 1)
            project_queries(pe, t + 1, 1 - u)
            pe.wait_ge(norm_t_ready, 2 * t + 2)
            for o in range(F1 // P):
                for k in range(2 * KD):
                    of = xt[:, u, k, :] if k < KD else norm_t[:, k - KD, :]
                    last = nc.tensor.matmul(hidden_ps[:, o, :], m.w_1[:, k, o * P:(o + 1) * P], of,
                                            start=(k == 0), stop=(k == 2 * KD - 1))
            last.then_inc(hidden_done, 1)

    def pe_end(pe):
        mlp_output(pe, TURNS - 1)

    def variance(dve, t, n):
        nc.vector.bn_stats(stats[:, n, :], row_ps[n]).then_inc(ln_step[n], 1)
        wait_apart(dve, ln_step[n], 3 * t + 1, m.passed)
        nc.vector.bn_aggr(mv[:, n, :], stats[:, n, :]).then_inc(ln_step[n], 1)
        dve.wait_ge(ln_step[n], 3 * t + 2)
        nc.vector.tensor_scalar(var[:, n, :], mv[:, n, 1:2], LN_EPS, None, ALU.add).then_inc(var_ready[n], 1)

    def inverse_sd(dve, t, n):
        dve.wait_ge(guess_ready[n], t + 1)
        nc.vector.scalar_tensor_tensor(square[:, n, :], guess[:, n, :], var[:, n, :], guess[:, n, :],
                                       ALU.mult, ALU.mult).then_inc(ln_step[n], 1)
        dve.wait_ge(ln_step[n], 3 * t + 3)
        nc.vector.scalar_tensor_tensor(inv_sd[:, n, :], square[:, n, :], 3.0, guess[:, n, :],
                                       ALU.subtract, ALU.mult).then_inc(inv_sd_ready[n], 1)
        dve.wait_ge(inv_sd_ready[n], t + 1)

    def normalise(dve, to, n):
        return nc.vector.tensor_scalar(to, row_ps[n], mv[:, n, 0:1], inv_sd[:, n, :], ALU.subtract, ALU.mult)

    def guess_sd(act, t, n):
        act.wait_ge(var_ready[n], t + 1)
        nc.scalar.activation(ln_var[:, n, :], var[:, n, :], ACT.Ln).then_inc(log_ready[n], 1)
        act.wait_ge(log_ready[n], t + 1)
        nc.scalar.activation(guess[:, n, :], ln_var[:, n, :], ACT.Exp, scale=-0.5).then_inc(guess_ready[n], 1)

    def min_query(dve, t):
        dve.wait_ge(query_projected, t + 1)
        nc.vector.tensor_scalar(q_min[:, :, :], query_ps[:, :, :], 0.0, None, ALU.min).then_inc(q_min_ready, 1)

    def output_variance(dve, t):
        dve.wait_ge(mlp_done, t + 1)
        variance(dve, t, 1)

    def output(dve, t, u):
        inverse_sd(dve, t, 1)
        normalise(dve, scaled[:, :], 1).then_inc(scaled_ready, 1)
        dve.wait_ge(scaled_ready, 2 * t + 1)
        nc.vector.tensor_tensor(scaled[:, :], scaled[:, :], m.ln2_gh[:, :], ALU.mult).then_inc(scaled_ready, 1)
        dve.wait_ge(scaled_ready, 2 * t + 2)
        nc.vector.tensor_tensor(result[:, u, :], result[:, u, :], scaled[:, :], ALU.add).then_inc(mixed, 1)

    def dve_begin(dve):
        min_query(dve, 0)

    def dve(dve, i, u, place):
        t = 2 * i + u
        if place == 0:
            dve.wait_ge(q_exp_ready, t + 1)
            nc.vector.scalar_tensor_tensor(queries[:, :, :], query_ps[:, :, :], 0.0, q_min[:, :, :],
                                           ALU.max, ALU.add).then_inc(queries_ready, 1)
        if place == 1:
            dve.wait_ge(num_ready, t + 1)
            nc.vector.tensor_scalar(den[:, :, :], num_ps[:, :, P:KVW], ATT_EPS, 1.0 / N,
                                    ALU.add, ALU.mult).then_inc(den_ready, 1)
            dve.wait_ge(den_ready, t + 1)
            nc.vector.reciprocal(inv[:, :, :], den[:, :, :]).then_inc(inv_ready, 1)
            dve.wait_ge(inv_ready, t + 1)
            nc.vector.tensor_tensor(msg[:, :].rearrange("p (k h d) -> p k h d", k=KD, h=HC),
                                    num_ps[:, :, 0:P].rearrange("p k (h d) -> p k h d", h=HC),
                                    inv[:, :, :].rearrange("p k (h o) -> p k h o", o=1)
                                    .to_broadcast([P, KD, HC, HD]), ALU.mult).then_inc(msg_ready, 1)
            if not is_first(i, u):
                output_variance(dve, t - 1)
        if place == 2:
            if not is_first(i, u):
                output(dve, t - 1, 1 - u)
            dve.wait_ge(msg_projected, t + 1)
            variance(dve, t, 0)
            dve.wait_ge(result_free[u], i + 1)
            dve.sem_inc(m.passed, 1)
            nc.vector.tensor_tensor(result[:, u, :], tile[:, u, :], m.ln2_b[:, :], ALU.add).then_inc(base_ready, 1)
            inverse_sd(dve, t, 0)
            normalise(dve, msg[:, :], 0).then_inc(normed_ready, 1)
        if place == 3:
            min_query(dve, t + 1)

    def dve_end(dve):
        output_variance(dve, TURNS - 1)
        output(dve, TURNS - 1, 1)

    def copy_tile(act, t, u):
        act.wait_ge(tile_turned, t + 1)
        nc.scalar.copy(xt[:, u, :, :], tile_ps[:, :, :]).then_inc(xt_ready, 1)

    def exp_query(act, t):
        act.wait_ge(q_min_ready, t + 1)
        nc.scalar.activation(q_min[:, :, :], q_min[:, :, :], ACT.Exp).then_inc(q_exp_ready, 1)

    def act_begin(act):
        act.preload_act_table_set(TABLES)
        for u in range(2):
            act.sem_inc(result_free[u], 1)
        copy_tile(act, 0, 0)
        exp_query(act, 0)

    def act(act, i, u):
        t = 2 * i + u
        if not is_first(i, u):
            guess_sd(act, t - 1, 1)
        act.wait_ge(msg_turned, t + 1)
        nc.scalar.copy(msg_t[:, :, :], turn_ps[:, :, :]).then_inc(msg_t_ready, 1)
        copy_tile(act, t + 1, 1 - u)
        guess_sd(act, t, 0)
        act.wait_ge(norm_turned, t + 1)
        for h in range(KD):
            nc.scalar.activation(norm_t[:, h, :], turn_ps[:, h, :], ACT.Identity, scale=m.ln1_gh[:, h:h + 1],
                                 bias=m.ln1_b[:, h:h + 1]).then_inc(norm_t_ready, 1)
        exp_query(act, t + 1)
        act.wait_ge(hidden_done, t + 1)
        nc.scalar.activation(hidden[:, :, :], hidden_ps[:, :, :], ACT.Relu).then_inc(hidden_ready, 1)

    def act_end(act):
        guess_sd(act, TURNS - 1, 1)

    mix.load, mix.free, mix.store, mix.stored = load, free, store, all_stored
    mix.pe_begin, mix.pe, mix.pe_end = pe_begin, pe, pe_end
    mix.dve_begin, mix.dve, mix.dve_end = dve_begin, dve, dve_end
    mix.act_begin, mix.act, mix.act_end, mix.load_past = act_begin, act, act_end, load_past
    mix.load_weights = lambda sp: None
    mix.after = lambda: None
    return mix


def dense_first(nc, m):
    with ExitStack() as ctx:
        def sb(name, shape, dt=F32):
            return ctx.enter_context(nc.sbuf_tensor(name, shape, dt))

        sem = semaphores(nc, ctx)

        w_g1 = sb("w_g1", [P, KD, D])
        agg_now = sb("agg_now", [P, DT, KD, P])
        z_min = sb("z_min", [P, DT, D])
        z_exp = sb("z_exp", [P, DT, D])
        h_one = sb("h_one", [P, DT, D])
        h = sb("h", [P, 2, DT, D])
        z = [ctx.enter_context(nc.psum_tensor(f"z{j}", [P, BANK], F32))[:, 0:D] for j in range(DT)]

        weights_loaded = sem("g1_weights_loaded")
        agg_ready = sem("agg_ready")
        z_ready = sem("z_ready")
        z_min_ready = sem("z_min_ready")
        z_exp_ready = sem("z_exp_ready")
        h_one_ready = sem("h_one_ready")
        h_ready = sem("h_ready")
        h_stored = [sem(f"h_stored{u}") for u in range(2)]
        h_free = [sem(f"h_free{u}") for u in range(2)]
        loops = NT // (2 * DT)
        h1_blocks = m.h1.rearrange("(b j p) f -> b p j f", p=P, j=DT)

        def each(engine, body):
            with engine.Fori(0, loops) as i:
                for u in range(2):
                    for j in range(DT):
                        body(i, u, j, i * (2 * DT) + (u * DT + j))

        with nc.Block("dense1") as block:
            @block.gpsimd
            def _(pool):
                def copy(i, u, j, n):
                    pool.wait_ge(z_ready, n + 1)
                    pool.sem_inc(m.pool_passed, 1)
                    nc.gpsimd.tensor_copy(agg_now[:, j, :, :], m.agg[:, :, bass.ds(n * P, P)]).then_inc(agg_ready, 1)
                each(pool, copy)

            @block.tensor
            def _(pe):
                pe.sem_inc(z_ready, DT)
                pe.wait_ge(weights_loaded, 16)
                pe.sem_inc(m.pe_passed, 1)

                def product(i, u, j, n):
                    pe.wait_ge(agg_ready, n + 1)
                    pe.wait_ge(h_one_ready, n + 1)
                    nc.tensor.matmul(z[j], m.ones[0:1, :], m.b_g1[:, :], start=True, stop=False)
                    for k in range(KD):
                        last = nc.tensor.matmul(z[j], agg_now[:, j, k, :], w_g1[:, k, :],
                                                start=False, stop=(k == KD - 1))
                    last.then_inc(z_ready, 1)
                each(pe, product)

            @block.vector
            def _(dve):
                dve.sem_inc(h_one_ready, DT)

                def min_part(n, j):
                    dve.wait_ge(z_ready, n + (1 + DT))
                    nc.vector.tensor_scalar(z_min[:, j, :], z[j], 0.0, None, ALU.min).then_inc(z_min_ready, 1)

                def sum_part(n, j):
                    dve.wait_ge(z_exp_ready, n + 1)
                    nc.vector.scalar_tensor_tensor(h_one[:, j, :], z[j], 0.0, z_exp[:, j, :],
                                                   ALU.max, ALU.add).then_inc(h_one_ready, 1)

                with dve.Fori(0, loops) as i:
                    for u in range(2):
                        n = i * (2 * DT) + u * DT
                        min_part(n, 0)
                        for j in range(1, DT):
                            min_part(n + j, j)
                            sum_part(n + (j - 1), j - 1)
                        sum_part(n + (DT - 1), DT - 1)

            @block.scalar
            def _(act):
                def exp_part(n, j):
                    act.wait_ge(z_min_ready, n + 1)
                    nc.scalar.activation(z_exp[:, j, :], z_min[:, j, :], ACT.Exp).then_inc(z_exp_ready, 1)

                def less_one(i, u, n, j):
                    act.wait_ge(h_one_ready, n + (1 + DT))
                    nc.scalar.activation(h[:, u, j, :], h_one[:, j, :], ACT.Copy, bias=-1.0).then_inc(h_ready, 1)

                with act.Fori(0, loops) as i:
                    for u in range(2):
                        n = i * (2 * DT) + u * DT
                        act.wait_ge(h_free[u], i + 1)
                        act.sem_inc(m.act_passed, 1)
                        exp_part(n, 0)
                        for j in range(1, DT):
                            exp_part(n + j, j)
                            less_one(i, u, n + (j - 1), j - 1)
                        less_one(i, u, n + (DT - 1), DT - 1)

            @block.sync
            def _(sp):
                sp.dma_start(w_g1[:, :, :], m.in_w_g1.rearrange("(k p) n -> p k n", p=P)).then_inc(weights_loaded, 16)
                for u in range(2):
                    sp.sem_inc(h_free[u], 1)
                with sp.Fori(0, loops) as i:
                    for u in range(2):
                        sp.wait_ge(h_ready, i * (2 * DT) + (u + 1) * DT)
                        sp.dma_start(h1_blocks[bass.ds(2 * i + u, 1)].rearrange("b p j f -> (b p) j f"),
                                     h[:, u, :, :]).then_inc(h_stored[u], 16)
                        sp.wait_ge(h_stored[u], 16 * i + 16)
                        sp.sem_inc(h_free[u], 1)


def dense_second(nc, m):
    with ExitStack() as ctx:
        def sb(name, shape, dt=F32):
            return ctx.enter_context(nc.sbuf_tensor(name, shape, dt))

        sem = semaphores(nc, ctx)

        x_in = sb("x_in", [P, 2, PAIR, D])
        mix_in = sb("mix_in", [P, 2, PAIR, D])
        agg_now = sb("agg_now2", [P, 2, KD, PAIR * P])
        z_min = sb("z2_min", [P, PAIR, D])
        h_one = sb("h2_one", [P, PAIR, D])
        xf = sb("xf_rows", [P, 2, PAIR, D])
        xf_t = sb("xf_t", [P, PAIR * KD, P])
        stats = sb("x2_stats", [P, PAIR, 6])
        mv = sb("x2_mv", [P, 2, PAIR, 2])
        var = sb("x2_var", [P, PAIR])
        guess = sb("x2_guess", [P, PAIR])
        square = sb("x2_square", [P, PAIR])
        inv_sd = sb("x2_inv_sd", [P, PAIR])

        def ps(name, a, b):
            bank = ctx.enter_context(nc.psum_tensor(name, [P, BANK], F32))
            return bank[:, 0:a * b].rearrange("p (a b) -> p a b", a=a)

        z = [ps(f"z_second{u}", PAIR, D) for u in range(2)]
        xf_ps = ps("xf_ps", PAIR * KD, P)
        logit_ps = [ps(f"logit_ps{u}", PAIR, NE) for u in range(2)]

        x_loaded = [sem(f"x2_x_loaded{u}") for u in range(2)]
        mix_loaded = [sem(f"mix_loaded{u}") for u in range(2)]
        base_ready = sem("x2_base_ready")
        agg_ready = sem("agg2_ready")
        z_ready = sem("z2_ready")
        z_min_ready = sem("z2_min_ready")
        z_exp_ready = sem("z2_exp_ready")
        h_one_ready = sem("h2_one_ready")
        x2_ready = sem("x2_ready")
        x2_stored = [sem(f"x2_stored{u}") for u in range(2)]
        xf_stored = [sem(f"xf_stored{u}") for u in range(2)]
        stored = sem("x2_and_xf_stored")
        var_ready = sem("x2_var_ready")
        log_ready = sem("x2_log_ready")
        guess_ready = sem("x2_guess_ready")
        xf_ready = sem("xf_ready")
        xf_turned = sem("xf_turned")
        xf_t_ready = sem("xf_t_ready")
        logits_done = sem("logits_done")
        logits_ready = sem("logits_ready")
        step = sem("dense2_step")
        loops = NT // PAIR // 2
        UNITS = 2 * loops
        STEPS = 6

        def blocks(of):
            return of.rearrange("(b j p) f -> b p j f", p=P, j=PAIR)

        def units(engine, body):
            for u in range(2):
                body(0, u)
            with engine.Fori(1, loops) as i:
                for u in range(2):
                    body(i, u)

        def past(i, u, n):
            return isinstance(i, int) and 2 * i + u < n

        with nc.Block("dense2") as block:
            @block.sync
            def _(sp):
                def load(q, u):
                    sp.dma_start(x_in[:, u, :, :], blocks(m.x)[bass.ds(q, 1)].rearrange("b p j f -> (b p) j f")
                                 ).then_inc(x_loaded[u], 16)
                    sp.dma_start(mix_in[:, u, :, :], blocks(m.mix)[bass.ds(q, 1)].rearrange("b p j f -> (b p) j f")
                                 ).then_inc(mix_loaded[u], 16)

                def store(q, i, u):
                    sp.wait_ge(x2_ready, q + 1)
                    sp.dma_start(blocks(m.x2)[bass.ds(q, 1)].rearrange("b p j f -> (b p) j f"),
                                 x_in[:, u, :, :]).then_inc(x2_stored[u], 16)
                    sp.wait_ge(xf_ready, q + 1)
                    sp.dma_start(blocks(m.xf)[bass.ds(q, 1)].rearrange("b p j f -> (b p) j f"),
                                 xf[:, u, :, :]).then_inc(xf_stored[u], 16)
                    sp.wait_ge(x2_stored[u], 16 * i + 16)
                    sp.wait_ge(xf_stored[u], 16 * i + 16)
                    sp.sem_inc(stored, 1)

                for u in range(2):
                    load(u, u)
                with sp.Fori(1, loops) as i:
                    for u in range(2):
                        q = 2 * i + u
                        store(q - 2, i - 1, u)
                        load(q, u)
                for u in range(2):
                    store(UNITS - 2 + u, loops - 1, u)

            @block.gpsimd
            def _(pool):
                def add(i, u):
                    pool.wait_ge(x_loaded[u], 16 * i + 16)
                    pool.wait_ge(mix_loaded[u], 16 * i + 16)
                    pool.sem_inc(m.pool_passed, 1)
                    nc.gpsimd.tensor_tensor(x_in[:, u, :, :], x_in[:, u, :, :], mix_in[:, u, :, :],
                                            ALU.add).then_inc(base_ready, 1)
                units(pool, add)

            @block.scalar
            def _(act):
                def copy_agg(q, u):
                    nc.scalar.copy(agg_now[:, u, :, :], m.agg[:, :, bass.ds(q * (PAIR * P), PAIR * P)]
                                   ).then_inc(agg_ready, 1)

                def copy_xf(q):
                    act.wait_ge(xf_turned, q + 1)
                    nc.scalar.copy(xf_t[:, :, :], xf_ps[:, :, :]).then_inc(xf_t_ready, 1)

                def unit(i, u, more=True):
                    q = 2 * i + u
                    act.wait_ge(z_min_ready, q + 1)
                    nc.scalar.activation(z_min[:, :, :], z_min[:, :, :], ACT.Exp).then_inc(z_exp_ready, 1)
                    if not past(i, u, 2):
                        copy_xf(q - 2)
                    if more:
                        copy_agg(q + 2, u)
                    act.wait_ge(var_ready, q + 1)
                    nc.scalar.activation(guess[:, :], var[:, :], ACT.Ln).then_inc(log_ready, 1)
                    act.wait_ge(log_ready, q + 1)
                    nc.scalar.activation(guess[:, :], guess[:, :], ACT.Exp, scale=-0.5).then_inc(guess_ready, 1)

                act.preload_act_table_set(TABLES)
                for u in range(2):
                    copy_agg(u, u)
                for u in range(2):
                    unit(0, u)
                with act.Fori(1, loops - 1) as i:
                    for u in range(2):
                        unit(i, u)
                for u in range(2):
                    unit(loops - 1, u, more=False)
                for q in (UNITS - 2, UNITS - 1):
                    copy_xf(q)

            @block.tensor
            def _(pe):
                def turn_rows(q, u):
                    pe.wait_ge(xf_ready, q + 1)
                    for j in range(PAIR):
                        for h in range(KD):
                            last = nc.tensor.transpose(xf_ps[:, j * KD + h, :], xf[:, u, j, h * P:(h + 1) * P],
                                                       m.ident[:, :])
                    last.then_inc(xf_turned, 1)

                def gate_products(q, u):
                    pe.wait_ge(xf_t_ready, q + 1)
                    pe.wait_ge(logits_ready, q + 1)
                    for j in range(PAIR):
                        for k in range(KD):
                            last = nc.tensor.matmul(logit_ps[u][:, j, :], xf_t[:, j * KD + k, :], m.gate_w[:, k, :],
                                                    start=(k == 0), stop=(k == KD - 1))
                    last.then_inc(logits_done, 1)

                def unit(i, u):
                    q = 2 * i + u
                    if not past(i, u, 2):
                        turn_rows(q - 2, u)
                    pe.wait_ge(agg_ready, q + 1)
                    if not past(i, u, 2):
                        pe.wait_ge(h_one_ready, q - 1)
                    for j in range(PAIR):
                        nc.tensor.matmul(z[u][:, j, :], m.ones[0:1, :], m.b_g2[:, :], start=True, stop=False)
                        for k in range(KD):
                            last = nc.tensor.matmul(z[u][:, j, :], agg_now[:, u, k, j * P:(j + 1) * P],
                                                    m.w_g2[:, k, :], start=False, stop=(k == KD - 1))
                    last.then_inc(z_ready, 1)
                    if not past(i, u, 2):
                        gate_products(q - 2, u)

                units(pe, unit)
                for u in range(2):
                    turn_rows(UNITS - 2 + u, u)
                    gate_products(UNITS - 2 + u, u)

            @block.vector
            def _(dve):
                def normalise(q, u, i):
                    dve.wait_ge(guess_ready, q + 1)
                    nc.vector.tensor_tensor(square[:, :], guess[:, :], guess[:, :], ALU.mult).then_inc(step, 1)
                    wait_apart(dve, step, q * STEPS + 3, m.passed)
                    nc.vector.tensor_tensor(square[:, :], square[:, :], var[:, :], ALU.mult).then_inc(step, 1)
                    wait_apart(dve, step, q * STEPS + 4, m.passed)
                    nc.vector.tensor_scalar(square[:, :], square[:, :], -0.5, 1.5, ALU.mult, ALU.add).then_inc(step, 1)
                    wait_apart(dve, step, q * STEPS + 5, m.passed)
                    nc.vector.tensor_tensor(inv_sd[:, :], guess[:, :], square[:, :], ALU.mult).then_inc(step, 1)
                    dve.wait_ge(stored, q + 1)
                    dve.sem_inc(m.passed, 1)
                    wait_apart(dve, step, q * STEPS + 6, m.passed)
                    for j in range(PAIR):
                        last = nc.vector.tensor_scalar(xf[:, u, j, :], x_in[:, u, j, :], mv[:, u, j, 0:1],
                                                       inv_sd[:, j:j + 1], ALU.subtract, ALU.mult)
                    last.then_inc(xf_ready, 1)

                def take_logits(q, u):
                    dve.wait_ge(logits_done, q + 1)
                    nc.vector.tensor_tensor(m.logits[:, bass.ds(q * PAIR, PAIR), :], logit_ps[u][:, :, :],
                                            m.gate_b[:, :].rearrange("p (o e) -> p o e", o=1)
                                            .to_broadcast([P, PAIR, NE]), ALU.add).then_inc(logits_ready, 1)

                def unit(i, u):
                    q = 2 * i + u
                    dve.wait_ge(z_ready, q + 1)
                    nc.vector.tensor_scalar(z_min[:, :, :], z[u][:, :, :], 0.0, None, ALU.min).then_inc(z_min_ready, 1)
                    if not past(i, u, 1):
                        normalise(q - 1, 1 - u, i)
                    dve.wait_ge(z_exp_ready, q + 1)
                    nc.vector.scalar_tensor_tensor(h_one[:, :, :], z[u][:, :, :], 0.0, z_min[:, :, :],
                                                   ALU.max, ALU.add).then_inc(h_one_ready, 1)
                    dve.wait_ge(base_ready, q + 1)
                    dve.sem_inc(m.passed, 1)
                    dve.wait_ge(h_one_ready, q + 1)
                    nc.vector.scalar_tensor_tensor(x_in[:, u, :, :], h_one[:, :, :], -1.0, x_in[:, u, :, :],
                                                   ALU.add, ALU.add).then_inc(x2_ready, 1)
                    wait_apart(dve, x2_ready, q + 1, m.passed)
                    for j in range(PAIR):
                        last = nc.vector.bn_stats(stats[:, j, :], x_in[:, u, j, :])
                    last.then_inc(step, 1)
                    wait_apart(dve, step, q * STEPS + 1, m.passed)
                    for j in range(PAIR):
                        last = nc.vector.bn_aggr(mv[:, u, j, :], stats[:, j, :])
                    last.then_inc(step, 1)
                    dve.wait_ge(step, q * STEPS + 2)
                    nc.vector.tensor_scalar(var[:, :], mv[:, u, :, 1], LN_EPS, None, ALU.add).then_inc(var_ready, 1)
                    if not past(i, u, 2):
                        take_logits(q - 2, u)

                dve.sem_inc(stored, 2)
                dve.sem_inc(logits_ready, 2)
                units(dve, unit)
                normalise(UNITS - 1, 1, loops - 1)
                for u in range(2):
                    take_logits(UNITS - 2 + u, u)


def route(nc, m):
    with ExitStack() as ctx:
        def sb(name, shape, dt=F32):
            return ctx.enter_context(nc.sbuf_tensor(name, shape, dt))

        sem = semaphores(nc, ctx)

        def ps(name):
            bank = ctx.enter_context(nc.psum_tensor(name, [P, BANK], F32))
            return bank[:, 0:HALF * NE].rearrange("p (j e) -> p j e", e=NE)

        HALF = NT // 2
        probs = sb("probs", [P, NT, NE])
        most = sb("most", [P, NT])
        total = sb("total", [P, NT])
        top = sb("top", [P, NT])
        marked = sb("marked", [P, NT, NE])
        first = sb("first", [P, NT])
        chosen = sb("chosen", [P, NT, NE])
        counts = sb("counts", [P, NT, NE])
        ends = sb("ends", [P, NT, NE])
        nth = sb("nth", [P, NT])
        expert_row = sb("expert_row", [P, NT])
        kept = sb("kept", [P, NT])
        row = sb("row", [P, NT])
        at = sb("at", [P, NT])
        one = sb("route_one", [P, NT])
        left_i = sb("left_i", [P, NE], I32)
        left_f = sb("left_f", [P, NE])
        spare_i = sb("spare_i", [P, NT], I32)
        spare_f = sb("spare_f", [P, NT])
        blocks_i = sb("blocks_i", [1, NE], I32)
        blocks_f = sb("blocks_f", [1, NE])
        blocks_end = sb("blocks_end", [1, NE])
        nth_ps = [ps(f"nth_ps{k}") for k in range(2)]
        count_ps = [ps(f"count_ps{k}") for k in range(2)]

        iotas = sem("route_iotas")
        shifted = sem("route_shifted")
        exps_ready = sem("route_exps")
        chosen_ready = sem("chosen_ready")
        counted = sem("counted")
        step = sem("route_step")

        def by_tile(of):
            return of.rearrange("p (j o) -> p j o", o=1).to_broadcast([P, NT, NE])

        def by_expert(of):
            return of.rearrange("p (o e) -> p o e", o=1).to_broadcast([P, NT, NE])

        with nc.Block("route") as block:
            @block.gpsimd
            def _(pool):
                nc.gpsimd.iota(left_i[:, :], [[-1, NE]], base=NE, channel_multiplier=0).then_inc(iotas, 1)
                nc.gpsimd.iota(spare_i[:, :], [[P, NT]], base=TRASH, channel_multiplier=1).then_inc(iotas, 1)

            @block.scalar
            def _(act):
                act.wait_ge(shifted, 1)
                nc.scalar.activation(probs[:, :, :], m.logits[:, :, :], ACT.Exp).then_inc(exps_ready, 1)

            @block.tensor
            def _(pe):
                pe.wait_ge(chosen_ready, 1)
                for k in range(2):
                    half = chosen[:, k * HALF:(k + 1) * HALF, :]
                    nc.tensor.matmul(nth_ps[k], m.upto[:, :], half, start=True, stop=True)
                    nc.tensor.matmul(count_ps[k], m.ones[:, :], half, start=True, stop=True).then_inc(counted, 1)

            @block.vector
            def _(dve):
                count = [0]

                def link(instruction):
                    count[0] += 1
                    instruction.then_inc(step, 1)
                    dve.wait_ge(step, count[0])

                link(nc.vector.tensor_reduce(most[:, :], m.logits[:, :, :], AX.X, ALU.max))
                nc.vector.tensor_tensor(m.logits[:, :, :], m.logits[:, :, :], by_tile(most[:, :]),
                                        ALU.subtract).then_inc(shifted, 1)
                dve.wait_ge(iotas, 2)
                nc.vector.tensor_copy(left_f[:, :], left_i[:, :])
                nc.vector.tensor_copy(spare_f[:, :], spare_i[:, :])
                link(nc.vector.memset(one[:, :], 1.0))
                dve.wait_ge(exps_ready, 1)
                link(nc.vector.tensor_reduce(total[:, :], probs[:, :, :], AX.X, ALU.add))
                link(nc.vector.reciprocal(total[:, :], total[:, :]))
                link(nc.vector.tensor_tensor(probs[:, :, :], probs[:, :, :], by_tile(total[:, :]), ALU.mult))
                link(nc.vector.tensor_reduce(top[:, :], probs[:, :, :], AX.X, ALU.max))
                link(nc.vector.tensor_tensor(marked[:, :, :], probs[:, :, :], by_tile(top[:, :]), ALU.is_equal))
                link(nc.vector.tensor_tensor(marked[:, :, :], marked[:, :, :], by_expert(left_f[:, :]), ALU.mult))
                link(nc.vector.tensor_reduce(first[:, :], marked[:, :, :], AX.X, ALU.max))
                link(nc.vector.tensor_tensor(chosen[:, :, :], by_tile(first[:, :]), by_expert(left_f[:, :]),
                                             ALU.is_equal))
                nc.vector.tensor_tensor(chosen[:, :, :], chosen[:, :, :], by_tile(m.valid[:, :]),
                                        ALU.mult).then_inc(chosen_ready, 1)
                nc.vector.tensor_scalar(expert_row[:, :], first[:, :], float(-ROWS), float(NE * ROWS),
                                        ALU.mult, ALU.add)
                dve.wait_ge(counted, 2)
                for k in range(2):
                    last = nc.vector.tensor_copy(counts[:, k * HALF:(k + 1) * HALF, :], count_ps[k])
                link(last)
                for e in range(NE):
                    last = nc.vector.tensor_tensor_scan(ends[:, :, e], one[:, :], counts[:, :, e], 0.0,
                                                        ALU.mult, ALU.add)
                link(last)
                link(nc.vector.tensor_tensor(counts[:, :, :], ends[:, :, :], counts[:, :, :], ALU.subtract))
                for k in range(2):
                    half = counts[:, k * HALF:(k + 1) * HALF, :]
                    last = nc.vector.tensor_tensor(half, half, nth_ps[k], ALU.add)
                link(last)
                link(nc.vector.tensor_tensor(counts[:, :, :], counts[:, :, :], chosen[:, :, :], ALU.mult))
                link(nc.vector.tensor_reduce(nth[:, :], counts[:, :, :], AX.X, ALU.add))
                nc.vector.tensor_scalar(kept[:, :], nth[:, :], float(CAP), None, ALU.is_le)
                nc.vector.tensor_scalar(at[:, :], nth[:, :], float(CAP), 1.0, ALU.min, ALU.subtract)
                link(nc.vector.tensor_tensor(row[:, :], expert_row[:, :], nth[:, :], ALU.add))
                link(nc.vector.tensor_tensor(kept[:, :], kept[:, :], m.valid[:, :], ALU.mult))
                link(nc.vector.scalar_tensor_tensor(row[:, :], row[:, :], -1.0, spare_f[:, :],
                                                    ALU.add, ALU.subtract))
                link(nc.vector.tensor_tensor(row[:, :], row[:, :], kept[:, :], ALU.mult))
                nc.vector.tensor_tensor(m.row[:, :], row[:, :], spare_f[:, :], ALU.add)
                link(nc.vector.tensor_tensor(at[:, :], expert_row[:, :], at[:, :], ALU.add))
                nc.vector.tensor_tensor(m.place[:, :], at[:, :], m.valid[:, :], ALU.mult)
                nc.vector.tensor_tensor(m.prob[:, :], top[:, :], kept[:, :], ALU.mult)
                link(nc.vector.tensor_scalar(blocks_i[:, :], ends[0:1, NT - 1, :], float(CAP), float(TB - 1),
                                             ALU.min, ALU.add))
                link(nc.vector.tensor_scalar(blocks_i[:, :], blocks_i[:, :], LOG_TB, None, ALU.arith_shift_right))
                link(nc.vector.tensor_scalar(blocks_f[:, :], blocks_i[:, :], 1.0, None, ALU.max))
                link(nc.vector.tensor_tensor_scan(blocks_end[:, :], one[0:1, 0:NE], blocks_f[:, :], 0.0,
                                                  ALU.mult, ALU.add))
                nc.vector.tensor_copy(m.blocks[0:1, :, 1], blocks_end[:, :])
                link(nc.vector.tensor_tensor(m.blocks[0:1, :, 0], blocks_end[:, :], blocks_f[:, :], ALU.subtract))


def scatter(nc, m):
    with ExitStack() as ctx:
        def sb(name, shape, dt=F32):
            return ctx.enter_context(nc.sbuf_tensor(name, shape, dt))

        sem = semaphores(nc, ctx)
        rows = sb("s_rows", [P, 2, DT, D])
        row_now = sb("row_now", [P, 2, DT], I32)
        rows_loaded = [sem(f"s_rows_loaded{u}") for u in range(2)]
        row_ready = [sem(f"s_row_ready{u}") for u in range(2)]
        scattered = [sem(f"scattered{u}") for u in range(2)]
        loops = NT // (2 * DT)
        xf_blocks = m.xf.rearrange("(b j p) f -> b p j f", p=P, j=DT)

        with nc.Block("scatter") as block:
            @block.sync
            def _(sp):
                for u in range(2):
                    sp.dma_start(rows[:, u, :, :], xf_blocks[u]).then_inc(rows_loaded[u], 16)
                with sp.Fori(1, loops) as i:
                    for u in range(2):
                        sp.wait_ge(scattered[u], 16 * DT * i)
                        sp.dma_start(rows[:, u, :, :],
                                     xf_blocks[bass.ds(2 * i + u, 1)].rearrange("b p j f -> (b p) j f")
                                     ).then_inc(rows_loaded[u], 16)

            @block.vector
            def _(dve):
                def take(b, u):
                    nc.vector.tensor_copy(row_now[:, u, :], m.row[:, bass.ds(b * DT, DT)]).then_inc(row_ready[u], 1)

                for u in range(2):
                    take(u, u)
                with dve.Fori(1, loops) as i:
                    for u in range(2):
                        wait_apart(dve, scattered[u], 16 * DT * i, m.passed)
                        take(2 * i + u, u)

            @block.gpsimd
            def _(pool):
                with pool.Fori(0, loops) as i:
                    for u in range(2):
                        pool.wait_ge(row_ready[u], i + 1)
                        pool.sem_inc(m.pool_passed, 1)
                        wait_apart(pool, rows_loaded[u], 16 * i + 16, m.pool_passed)
                        for j in range(DT):
                            nc.gpsimd.indirect_dma_start(
                                out=m.xe, out_offset=bass.IndirectOffsetOnAxis(ap=row_now[:, u, j:j + 1], axis=0),
                                in_=rows[:, u, j, :], in_offset=None).then_inc(scattered[u], 16)
                for u in range(2):
                    pool.wait_ge(scattered[u], 16 * DT * loops)
                    pool.sem_inc(m.pool_passed, 1)


def experts(nc, m):
    with ExitStack() as ctx:
        def sb(name, shape, dt=F32):
            return ctx.enter_context(nc.sbuf_tensor(name, shape, dt))

        sem = semaphores(nc, ctx)

        def ps(name, n):
            return ctx.enter_context(nc.psum_tensor(name, [P, BANK], F32))[:, 0:n]

        TT = TB // P
        w1 = [sb(f"w1_{u}", [P, KD, F]) for u in range(2)]
        w2 = [sb(f"w2_{u}", [P, FC, D]) for u in range(2)]
        b1 = [sb(f"b1_{u}", [P, FC]) for u in range(2)]
        b2 = [sb(f"b2_{u}", [P, D]) for u in range(2)]
        tokens = sb("tokens", [P, TT, D])
        tokens_t = sb("tokens_t", [P, KD, TB])
        hidden = sb("e_hidden", [P, FC, TB])
        y = sb("y", [P, TT, D])
        turn_ps = ps("e_turn_ps", KD * TB).rearrange("p (k n) -> p k n", k=KD)
        HB = 4
        hidden_ps = [ps(f"e_hidden_ps{f}", TB) for f in range(HB)]
        y_ps = [ps(f"y_ps{tt}", D) for tt in range(TT)]

        weights_loaded = [sem(f"weights_loaded{u}") for u in range(2)]
        tokens_loaded = sem("tokens_loaded")
        turned = sem("e_turned")
        tokens_t_ready = sem("tokens_t_ready")
        hidden_done = sem("e_hidden_done")
        by_act = sem("hidden_by_act")
        by_dve = sem("hidden_by_dve")
        y_done = sem("y_done")
        y_ready = sem("y_ready")
        y_stored = sem("y_stored")

        def bounds(engine, e):
            return [engine.value_load(m.blocks[0:1, bass.ds(e, 1), k], min_val=0, max_val=NE * ROWS // TB)
                    for k in range(2)]

        def rows_of(of, e, n, first):
            at = (e * ROWS + (n - first) * TB).with_bounds(min_val=0, max_val=(NE * ROWS - TB))
            return of[bass.ds(at, TB), :].rearrange("(j p) f -> p j f", p=P)

        def each(engine, body):
            with engine.Fori(0, NE // 2) as ii:
                for u in range(2):
                    e = 2 * ii + u
                    first, end = bounds(engine, e)
                    with engine.Fori(first, end) as n:
                        body(e, u, ii, n, first)

        with nc.Block("experts") as block:
            @block.gpsimd
            def _(pool):
                def load(e, u):
                    one = bass.ds(e, 1)
                    pool.dma_start(w1[u][:, :, :], m.w_e1[one].rearrange("o (k p) f -> p (o k) f", p=P)
                                   ).then_inc(weights_loaded[u], 16)
                    pool.dma_start(w2[u][:, :, :], m.w_e2[one].rearrange("o (k p) f -> p (o k) f", p=P)
                                   ).then_inc(weights_loaded[u], 16)
                    pool.dma_start(b1[u][:, :], m.in_b_e1[:, one, :].rearrange("p o f -> p (o f)")
                                   ).then_inc(weights_loaded[u], 16)
                    pool.dma_start(b2[u][:, :], m.in_b_e2[one, :].to_broadcast([P, D])
                                   ).then_inc(weights_loaded[u], 16)

                for u in range(2):
                    load(u, u)
                with pool.Fori(0, NE // 2 - 1) as ii:
                    for u in range(2):
                        first, end = bounds(pool, 2 * ii + u)
                        wait_apart(pool, y_ready, (end + 1) * TT, m.pool_passed)
                        load(2 * ii + (2 + u), u)

            @block.sync
            def _(sp):
                def load(e, u, ii, n, first):
                    sp.wait_ge(turned, n + 1)
                    sp.dma_start(tokens[:, :, :], rows_of(m.xe, e, n, first)).then_inc(tokens_loaded, 16)

                each(sp, load)
                first, end = bounds(sp, NE - 1)
                sp.wait_ge(turned, end + 1)
                sp.dma_start(tokens[:, :, :], m.xe[0:TB, :].rearrange("(j p) f -> p j f", p=P)
                             ).then_inc(tokens_loaded, 16)
                wait_apart(sp, y_stored, (end + 1) * 16, m.sp_passed)

            @block.tensor
            def _(pe):
                def turn(n):
                    pe.wait_ge(tokens_loaded, 16 * n + 16)
                    for j in range(TT):
                        for h in range(KD):
                            last = nc.tensor.transpose(turn_ps[:, h, j * P:(j + 1) * P],
                                                       tokens[:, j, h * P:(h + 1) * P], m.ident[:, :])
                    last.then_inc(turned, 1)

                def block_of(e, u, ii, n, first):
                    pe.wait_ge(weights_loaded[u], 64 * ii + 64)
                    pe.wait_ge(tokens_t_ready, n + 1)
                    for f in range(FC):
                        if f >= HB:
                            pe.wait_ge(by_dve if f % 2 else by_act, n * (FC // 2) + ((f - HB) // 2 + 1))
                        for k in range(KD):
                            last = nc.tensor.matmul(hidden_ps[f % HB], w1[u][:, k, f * P:(f + 1) * P],
                                                    tokens_t[:, k, :], start=(k == 0), stop=(k == KD - 1))
                        last.then_inc(hidden_done, 1)
                    turn(n + 1)
                    pe.wait_ge(y_ready, n * TT + TT)
                    for tt in range(TT):
                        for f in range(FC):
                            if tt == 0 and f in (0, FC - 2):
                                have = (n * (FC // 2)) + (FC // 2 - 1 if f == 0 else FC // 2)
                                pe.wait_ge(by_act, have)
                                pe.wait_ge(by_dve, have)
                            last = nc.tensor.matmul(y_ps[tt], hidden[:, f, tt * P:(tt + 1) * P], w2[u][:, f, :],
                                                    start=(f == 0), stop=(f == FC - 1))
                        last.then_inc(y_done, 1)

                pe.sem_inc(turned, 1)
                turn(0)
                each(pe, block_of)

            @block.scalar
            def _(act):
                def copy(n):
                    act.wait_ge(turned, n + 2)
                    nc.scalar.copy(tokens_t[:, :, :], turn_ps[:, :, :]).then_inc(tokens_t_ready, 1)

                def block_of(e, u, ii, n, first):
                    for f in range(0, FC, 2):
                        act.wait_ge(hidden_done, n * FC + (f + 1))
                        nc.scalar.activation(hidden[:, f, :], hidden_ps[f % HB], ACT.Relu, bias=b1[u][:, f:f + 1]
                                             ).then_inc(by_act, 1)
                    copy(n + 1)
                    act.wait_ge(y_ready, n * TT + 2 * TT)
                    act.dma_start(rows_of(m.ye, e, n, first), y[:, :, :]).then_inc(y_stored, 16)

                act.dma_start(m.ye[TRASH:TRASH + P, :], m.zeros[:, 0:D]).then_inc(y_stored, 16)
                copy(0)
                each(act, block_of)

            @block.vector
            def _(dve):
                def block_of(e, u, ii, n, first):
                    for f in range(1, FC, 2):
                        dve.wait_ge(hidden_done, n * FC + (f + 1))
                        nc.vector.tensor_scalar(hidden[:, f, :], hidden_ps[f % HB], b1[u][:, f:f + 1], 0.0,
                                                ALU.add, ALU.max).then_inc(by_dve, 1)
                    wait_apart(dve, y_stored, 16 * n + 16, m.passed)
                    for tt in range(TT):
                        dve.wait_ge(y_done, n * TT + (tt + 1))
                        nc.vector.tensor_tensor(y[:, tt, :], y_ps[tt], b2[u][:, :], ALU.add).then_inc(y_ready, 1)

                dve.sem_inc(y_ready, TT)
                each(dve, block_of)


def combine(nc, m):
    with ExitStack() as ctx:
        def sb(name, shape, dt=F32):
            return ctx.enter_context(nc.sbuf_tensor(name, shape, dt))

        sem = semaphores(nc, ctx)

        x2 = sb("x2_in", [P, 2, DT, D])
        ye = sb("ye_in", [P, 2, DT, D])
        scaled = sb("y_scaled", [P, DT, D])
        result = sb("y_result", [P, 2, DT, D])
        place_now = sb("place_now", [P, 2, DT], I32)
        prob_now = sb("prob_now", [P, 2, DT])
        finite = sb("finite", [P, DT, D], U8)
        nan = sb("nan", [P, DT, D], U8)
        zeros = sb("y_zeros", [P, DT, D])

        x2_loaded = [sem(f"c_x2_loaded{u}") for u in range(2)]
        gathered = [sem(f"gathered{u}") for u in range(2)]
        place_ready = sem("place_ready")
        prob_ready = sem("prob_ready")
        scaled_ready = sem("c_scaled_ready")
        masks = sem("c_masks")
        out_ready = sem("out_ready")
        out_stored = [sem(f"out_stored{u}") for u in range(2)]
        out_free = [sem(f"out_free{u}") for u in range(2)]
        zeroed = sem("c_zeroed")
        loops = NT // (2 * DT)

        def blocks(of):
            return of.rearrange("(b j p) f -> b p j f", p=P, j=DT)

        with nc.Block("combine") as block:
            @block.sync
            def _(sp):
                for u in range(2):
                    sp.sem_inc(out_free[u], 1)
                    sp.dma_start(x2[:, u, :, :], blocks(m.x2)[u]).then_inc(x2_loaded[u], 16)

                def store(b, i, u):
                    sp.wait_ge(out_ready, b + 3)
                    sp.dma_start(blocks(m.out)[bass.ds(b, 1)].rearrange("b p j f -> (b p) j f"),
                                 result[:, u, :, :]).then_inc(out_stored[u], 16)

                with sp.Fori(1, loops) as i:
                    for u in range(2):
                        b = 2 * i + u
                        store(b - 2, i - 1, u)
                        sp.dma_start(x2[:, u, :, :], blocks(m.x2)[bass.ds(b, 1)].rearrange("b p j f -> (b p) j f")
                                     ).then_inc(x2_loaded[u], 16)
                        sp.wait_ge(out_stored[u], 16 * i)
                        sp.sem_inc(out_free[u], 1)
                for u in range(2):
                    store(2 * (loops - 1) + u, loops - 1, u)
                for u in range(2):
                    sp.wait_ge(out_stored[u], 16 * loops)

            @block.gpsimd
            def _(pool):
                nc.gpsimd.memset(zeros[:, :, :], 0.0).then_inc(zeroed, 1)
                with pool.Fori(0, loops) as i:
                    for u in range(2):
                        b = 2 * i + u
                        wait_apart(pool, out_ready, b + 1, m.pool_passed)
                        nc.gpsimd.tensor_copy(place_now[:, u, :], m.place[:, bass.ds(b * DT, DT)]).then_inc(place_ready, 1)
                        nc.gpsimd.tensor_copy(prob_now[:, u, :], m.prob[:, bass.ds(b * DT, DT)]).then_inc(prob_ready, 1)
                        wait_apart(pool, place_ready, b + 1, m.pool_passed)
                        for j in range(DT):
                            nc.gpsimd.indirect_dma_start(
                                out=ye[:, u, j, :], out_offset=None, in_=m.ye[0:TRASH, :],
                                in_offset=bass.IndirectOffsetOnAxis(ap=place_now[:, u, j:j + 1], axis=0)
                            ).then_inc(gathered[u], 16)

            @block.scalar
            def _(act):
                with act.Fori(0, loops) as i:
                    for u in range(2):
                        b = 2 * i + u
                        act.wait_ge(prob_ready, b + 1)
                        act.wait_ge(gathered[u], 16 * DT * (i + 1))
                        act.wait_ge(out_ready, b + 2)
                        for j in range(DT):
                            last = nc.scalar.activation(scaled[:, j, :], ye[:, u, j, :], ACT.Copy,
                                                        scale=prob_now[:, u, j:j + 1])
                        last.then_inc(scaled_ready, 1)

            @block.vector
            def _(dve):
                dve.sem_inc(out_ready, 2)
                dve.wait_ge(zeroed, 1)
                with dve.Fori(0, loops) as i:
                    for u in range(2):
                        b = 2 * i + u
                        now = result[:, u, :, :]
                        dve.wait_ge(scaled_ready, b + 1)
                        dve.wait_ge(out_free[u], i + 1)
                        nc.vector.tensor_scalar(now, scaled[:, :, :], -1e4, 1e4, ALU.max, ALU.min)
                        nc.vector.tensor_scalar(finite[:, :, :], scaled[:, :, :], 0.0, 0.0,
                                                ALU.mult, ALU.is_equal)
                        nc.vector.tensor_tensor(nan[:, :, :], scaled[:, :, :], scaled[:, :, :],
                                                ALU.not_equal).then_inc(masks, 1)
                        wait_apart(dve, masks, 3 * b + 1, m.passed)
                        nc.vector.copy_predicated(now, finite[:, :, :], scaled[:, :, :]).then_inc(masks, 1)
                        wait_apart(dve, masks, 3 * b + 2, m.passed)
                        nc.vector.copy_predicated(now, nan[:, :, :], zeros[:, :, :]).then_inc(masks, 1)
                        dve.wait_ge(masks, 3 * b + 3)
                        dve.wait_ge(x2_loaded[u], 16 * i + 16)
                        nc.vector.tensor_tensor(now, now, x2[:, u, :, :], ALU.add).then_inc(out_ready, 1)


def program(nc, ins, out, scratch):
    m = Memory()
    (m.x, m.in_src, m.in_dst, m.in_dst_rows, m.in_wgt, m.in_w_g1, m.in_b_g1, m.in_w_g2, m.in_b_g2,
     m.in_w_q, m.in_w_k, m.in_w_v, m.in_w_m, m.in_w_1, m.in_w_2, m.in_ln1_g, m.in_ln1_b, m.in_ln2_g, m.in_ln2_b,
     m.in_gate_w, m.in_gate_b, m.w_e1, m.in_b_e1, m.w_e2, m.in_b_e2) = ins
    m.out = out
    m.xn = scratch("xn", [NP + P, D], F32)
    m.h1 = scratch("h1", [NP, D], F32)
    m.mix = scratch("mix", [NP, D], F32)
    m.x2 = scratch("x2", [NP, D], F32)
    m.xe = scratch("xe", [TRASH + NP, D], F32)
    m.xf = scratch("xf", [NP, D], F32)
    m.ye = scratch("ye", [TRASH + P, D], F32)
    m.low_dram = scratch("low_dram", [TURNS, TURN], I32)
    m.more_dram = scratch("more_dram", [TURNS, 1], I32)

    with ExitStack() as ctx:
        def sb(name, shape, dt=F32):
            return ctx.enter_context(nc.sbuf_tensor(name, shape, dt))

        m.passed = ctx.enter_context(nc.semaphore("passed"))
        m.pool_passed = ctx.enter_context(nc.semaphore("pool_passed"))
        m.pe_passed = ctx.enter_context(nc.semaphore("pe_passed"))
        m.sp_passed = ctx.enter_context(nc.semaphore("sp_passed"))
        m.act_passed = ctx.enter_context(nc.semaphore("act_passed"))
        m.buffers_zeroed = ctx.enter_context(nc.semaphore("buffers_zeroed"))
        m.wgt = sb("wgt", [P, NCH + SLOTS])
        m.dst_rel = sb("dst_rel", [P, NCH + SLOTS])
        m.table = sb("table", [1, TURNS, TURN + 2], I32)
        m.cols = sb("cols", [P, WIN])
        m.eps = sb("eps", [P, 1])
        m.ident = sb("ident", [P, P])
        m.upto = sb("upto", [P, P])
        m.ones = sb("ones", [P, P])
        m.zeros = sb("zeros", [P, KD * KVS])
        m.valid = sb("valid", [P, NT])
        m.w_q = sb("w_q", [P, KD, D])
        m.w_m = sb("w_m", [P, KD, D])
        m.w_g2 = sb("w_g2", [P, KD, D])
        m.w_1 = sb("w_1", [P, 2 * KD, F1])
        m.w_2 = sb("w_2", [P, F1 // P, D])
        m.b_g1 = sb("b_g1", [1, D])
        m.b_g2 = sb("b_g2", [1, D])
        m.ln1_gh = sb("ln1_gh", [P, KD])
        m.ln2_gh = sb("ln2_gh", [P, D])
        m.ln1_b = sb("ln1_b", [P, KD])
        m.ln2_b = sb("ln2_b", [P, D])
        m.gate_w = sb("gate_w", [P, KD, NE])
        m.gate_b = sb("gate_b", [P, NE])
        m.blocks = sb("blocks", [1, NE, 2], I32)
        m.kv = sb("kv", [P, KD, KVW])
        m.logits = sb("logits", [P, NT, NE])
        m.row = sb("row_of", [P, NT], I32)
        m.place = sb("place", [P, NT], I32)
        m.prob = sb("prob", [P, NT])
        prepare(nc, m)
        with ExitStack() as agg_ctx:
            m.agg = agg_ctx.enter_context(nc.sbuf_tensor("agg", [P, KD, AGG], F32))
            gather(nc, m, 1, m.xn, keys_values)
            dense_first(nc, m)
            gather(nc, m, 2, m.h1, attend)
            dense_second(nc, m)
        route(nc, m)
        scatter(nc, m)
        experts(nc, m)
        combine(nc, m)


def kernel(x, src, dst, edge_weight, L0_gnn_W1, L0_gnn_b1, L0_gnn_W2, L0_gnn_b2, L0_mix_Wq, L0_mix_Wk, L0_mix_Wv,
           L0_mix_Wm, L0_mix_W1, L0_mix_W2, L0_mix_g1, L0_mix_b1, L0_mix_g2, L0_mix_b2, L0_ffn_gate_w, L0_ffn_gate_b,
           L0_ffn_w1, L0_ffn_b1, L0_ffn_w2, L0_ffn_b2):
    import concourse.bacc as bacc
    from concourse.bass_utils import run_bass_kernel_spmd as run

    nc = bacc.Bacc("TRN2", target_bir_lowering=False, num_devices=1)

    def padded(a, n, value=0):
        a = np.asarray(a)
        return np.concatenate([a, np.full((n - a.shape[0],) + a.shape[1:], value, a.dtype)])

    def columns(a):
        return np.ascontiguousarray(a.reshape(NCH, P).T)

    dst_padded = padded(dst, NCH * P, N - 1)
    arrays = {
        "x": padded(x, NP),
        "src": padded(src, NCH * P).reshape(TURNS, SLOTS, P).transpose(0, 2, 1),
        "dst": columns(dst_padded),
        "dst_rows": dst_padded.reshape(TURNS, SLOTS * P),
        "edge_weight": columns(padded(edge_weight, NCH * P)),
        "gnn_W1": L0_gnn_W1, "gnn_b1": L0_gnn_b1, "gnn_W2": L0_gnn_W2, "gnn_b2": L0_gnn_b2,
        "mix_Wq": L0_mix_Wq, "mix_Wk": L0_mix_Wk, "mix_Wv": L0_mix_Wv, "mix_Wm": L0_mix_Wm,
        "mix_W1": L0_mix_W1, "mix_W2": L0_mix_W2,
        "mix_g1": np.asarray(L0_mix_g1).reshape(KD, P).T, "mix_b1": np.asarray(L0_mix_b1).reshape(KD, P).T,
        "mix_g2": L0_mix_g2, "mix_b2": L0_mix_b2,
        "gate_w": L0_ffn_gate_w, "gate_b": L0_ffn_gate_b,
        "ffn_w1": L0_ffn_w1, "ffn_b1": np.asarray(L0_ffn_b1).reshape(NE, FC, P).transpose(2, 0, 1),
        "ffn_w2": L0_ffn_w2, "ffn_b2": L0_ffn_b2,
    }
    arrays = {f"in_{k}": np.ascontiguousarray(v) for k, v in arrays.items()}
    ins = [nc.dram_tensor(k, v.shape, mybir.dt.from_np(v.dtype), kind="ExternalInput").ap() for k, v in arrays.items()]
    out = nc.dram_tensor("out", (NP, D), F32, kind="ExternalOutput").ap()

    def scratch(name, shape, dt):
        return nc.dram_tensor(name, shape, dt, kind=SCRATCH_KIND).ap()

    program(nc, ins, out, scratch)
    return run(nc, [arrays], core_ids=[0]).results[0]["out"][:N]


SCRATCH_KIND = "Internal"
```

```python
import concourse.bass as bass
from concourse import mybir
from contextlib import ExitStack
import numpy as np

F32 = mybir.dt.float32
I32 = mybir.dt.int32
U8 = mybir.dt.uint8
ALU = mybir.AluOpType
ACT = mybir.ActivationFunctionType
AX = mybir.AxisListType

P = 128
N = 12500
D = 256
KD = D // P
E = 212500
GROUP = 8
TURN = 2
SLOTS = GROUP * TURN
TURNS = -(-E // (P * SLOTS))
NCH = TURNS * SLOTS
NT = TURNS
NP = NT * P
WIN = 128
AGG = NP + WIN
LN_EPS = 1e-5
ATT_EPS = 1e-6
H = 8
HC = P // (D // H)
HD = D // H
KVW = P + HC
BANK = 512
KVS = P + 1
F1 = 512
NE = 8
F = 1024
FC = F // P
CAP = -(-5 * N // (4 * NE))
ROWS = -(-CAP // P) * P
TB = 256
TRASH = NE * ROWS
XW = D + 2
ZERO = -(-(TRASH // P) // TURNS)
PB = 2
PSLOTS = 4
ST = 2
SETS = 4
PAIR = 2
TABLES = "natural_log_exp_and_others"
LOG_WIN = 7
LOG_TB = 8
assert 1 << LOG_WIN == WIN and 1 << LOG_TB == TB and NP >= N and TURNS % 2 == 0 and NT % (PB * PSLOTS) == 0 and NT % (SETS * ST) == 0


def wait_apart(engine, semaphore, value, passed):
    engine.wait_ge(semaphore, value)
    engine.sem_inc(passed, 1)


def semaphores(nc, ctx, suffix=""):
    taken = []

    def sem(name):
        taken.append(nc.alloc_semaphore(name=f"{name}{suffix}"))
        return taken[-1]

    def clear():
        nc.clear_and_free_semaphores(taken)
        nc.all_engine_barrier()

    ctx.callback(clear)
    return sem


class Memory:
    pass


def two_by_two(engine, loops, body, peeled=1):
    for i in range(peeled):
        for u in range(2):
            body(i, u)
    with engine.Fori(peeled, loops) as i:
        for u in range(2):
            body(i, u)


def before_first(i, u, n):
    return isinstance(i, int) and 2 * i + u < n


def prepare(nc, m):
    with ExitStack() as ctx:
        def sb(name, shape, dt):
            return ctx.enter_context(nc.sbuf_tensor(name, shape, dt))

        sem = semaphores(nc, ctx)

        rows = sb("ln_rows", [P, PSLOTS, PB, D], F32)
        normed = sb("ln_normed", [P, PSLOTS, PB, D], F32)
        stats = sb("ln_stats", [P, PSLOTS, PB, 6], F32)
        mv = sb("ln_mean_var", [P, PSLOTS, PB, 2], F32)
        sd = sb("ln_sd", [P, PSLOTS, PB], F32)
        rstd = sb("ln_rstd", [P, PSLOTS, PB], F32)
        dst_rows = sb("dst_rows", [TURNS, TURN, GROUP * P], I32)
        low = sb("low", [TURNS, TURN], I32)
        high = sb("high", [TURNS, TURN], I32)
        span = sb("span", [TURNS, TURN], I32)
        more = sb("more", [TURNS, 1], I32)
        dst_i = sb("dst_i", [P, NCH], I32)
        dst_f = sb("dst_f", [P, NCH], F32)
        low_all = sb("low_all", [P, TURNS * TURN], I32)
        low_f = sb("low_f", [P, TURNS * TURN], F32)
        more_row = sb("more_row", [1, TURNS], I32)
        more_f = sb("more_f", [1, TURNS], F32)
        more_sum = sb("more_sum", [1, TURNS], F32)
        more_one = sb("more_one", [1, TURNS], F32)
        iota_i = sb("iota_i", [P, WIN], I32)
        node_i = sb("node_i", [P, NT], I32)

        consts_loaded = sem("consts_loaded")
        edges_loaded = sem("edges_loaded")
        x_loaded = [sem(f"x_loaded{s}") for s in range(PSLOTS)]
        mv_done = sem("mean_var_done")
        sd_done = sem("sd_done")
        eps_set = sem("eps_set")
        rstd_done = sem("rstd_done")
        xn_done = sem("xn_done")
        xn_stored = [sem(f"xn_stored{s}") for s in range(PSLOTS)]
        step = sem("prepare_step")
        spans_done = sem("spans_done")
        spans_stored = sem("spans_stored")
        spans_back = sem("spans_back")
        iotas_done = sem("iotas_done")
        tables_done = sem("tables_done")
        zero_set = sem("zero_set")
        pad_stored = sem("pad_stored")

        x_blocks = m.x.rearrange("(b p j) f -> b p j f", p=P, j=PB)
        xn_blocks = m.xn[0:NP, :].rearrange("(b p j) f -> b p j f", p=P, j=PB)
        n_blocks = NT // PB
        loops = n_blocks // PSLOTS
        consts = [
            (m.w_q[:, :, :], m.in_w_q.rearrange("(k p) n -> p k n", p=P)),
            (m.w_m[:, :, :], m.in_w_m.rearrange("(k p) n -> p k n", p=P)),
            (m.w_1[:, :, :], m.in_w_1.rearrange("(k p) n -> p k n", p=P)),
            (m.w_2[:, :, :], m.in_w_2.rearrange("(k p) n -> p k n", p=P)),
            (m.ln1_gh[:, :], m.in_ln1_g),
            (m.ln1_b[:, :], m.in_ln1_b),
            (m.ln2_gh[:, :], m.in_ln2_g.rearrange("(o n) -> o n", o=1).to_broadcast([P, D])),
            (m.ln2_b[:, :], m.in_ln2_b.rearrange("(o n) -> o n", o=1).to_broadcast([P, D])),
            (m.gate_w[:, :, :], m.in_gate_w.rearrange("(k p) n -> p k n", p=P)),
            (m.gate_b[:, :], m.in_gate_b.rearrange("(o n) -> o n", o=1).to_broadcast([P, NE])),
            (m.wgt[:, 0:NCH], m.in_wgt),
        ]

        with nc.Block("prepare") as block:
            @block.sync
            def _(sp):
                sp.dma_start(dst_rows[:, :, :],
                             m.in_dst_rows.rearrange("t (g e) -> t g e", g=TURN)).then_inc(edges_loaded, 16)
                sp.dma_start(dst_i[:, :], m.in_dst).then_inc(edges_loaded, 16)
                for s in range(PSLOTS):
                    sp.dma_start(rows[:, s, :, :], x_blocks[s]).then_inc(x_loaded[s], 16)
                with sp.Fori(1, loops) as i:
                    for s in range(PSLOTS):
                        sp.wait_ge(xn_done, i * PSLOTS + (s + 1 - PSLOTS))
                        sp.dma_start(rows[:, s, :, :],
                                     x_blocks[bass.ds(i * PSLOTS + s, 1)].rearrange("b p j f -> (b p) j f")
                                     ).then_inc(x_loaded[s], 16)
                for to, of in consts:
                    sp.dma_start(to, of).then_inc(consts_loaded, 16)
                sp.wait_ge(consts_loaded, 16 * len(consts))

            @block.scalar
            def _(act):
                def store(i, s):
                    act.wait_ge(xn_done, i * PSLOTS + s + 1)
                    act.dma_start(xn_blocks[bass.ds(i * PSLOTS + s, 1)].rearrange("b p j f -> (b p) j f"),
                                  normed[:, s, :, :]).then_inc(xn_stored[s], 16)

                act.wait_ge(eps_set, 1)
                with act.Fori(0, loops) as i:
                    for s in range(PSLOTS):
                        act.wait_ge(mv_done, i * PSLOTS + s + 1)
                        nc.scalar.activation(sd[:, s, :], mv[:, s, :, 1], ACT.Sqrt,
                                             bias=m.eps[:, 0:1]).then_inc(sd_done, 1)
                        if s:
                            store(i, s - 1)
                    store(i, PSLOTS - 1)
                act.wait_ge(zero_set, 1)
                act.dma_start(m.xn[NP:NP + P, :], m.zeros[:, 0:D]).then_inc(pad_stored, 16)
                act.wait_ge(pad_stored, 16)
                for s in range(PSLOTS):
                    act.wait_ge(xn_stored[s], 16 * loops)

            @block.gpsimd
            def _(pool):
                nc.gpsimd.memset(m.zeros[:, :], 0.0).then_inc(zero_set, 1)
                nc.gpsimd.memset(m.ones[:, :], 1.0).then_inc(zero_set, 1)
                nc.gpsimd.iota(iota_i[:, :], [[1, WIN]], base=0, channel_multiplier=0).then_inc(iotas_done, 1)
                nc.gpsimd.iota(node_i[:, :], [[P, NT]], base=0, channel_multiplier=1).then_inc(iotas_done, 1)
                pool.wait_ge(zero_set, 2)
                nc.gpsimd.affine_select(out=m.ident[:, :], in_=m.zeros[:, 0:P], compare_op=ALU.not_equal, fill=1.0,
                                        base=0, pattern=[[-1, P]], channel_multiplier=1).then_inc(iotas_done, 1)
                nc.gpsimd.affine_select(out=m.upto[:, :], in_=m.ones[:, :], compare_op=ALU.is_ge, fill=0.0,
                                        base=0, pattern=[[1, P]], channel_multiplier=-1).then_inc(iotas_done, 1)
                pool.wait_ge(spans_done, 2)
                pool.dma_start(m.low_dram[:, :], low[:, :]).then_inc(spans_stored, 16)
                pool.dma_start(m.more_dram[:, :], more[:, :]).then_inc(spans_stored, 16)
                pool.wait_ge(spans_stored, 32)
                pool.dma_start(low_all[:, :],
                             m.low_dram.rearrange("(o t) g -> o (t g)", o=1).to_broadcast([P, TURNS * TURN])
                             ).then_inc(spans_back, 16)
                pool.dma_start(m.table[0:1, :, 0:TURN],
                             m.low_dram.rearrange("(o t) g -> o t g", o=1)).then_inc(spans_back, 16)
                pool.dma_start(more_row[:, :],
                             m.more_dram.rearrange("(o t) g -> o (t g)", o=1)).then_inc(spans_back, 16)

            @block.vector
            def _(dve):
                nc.vector.memset(m.eps[:, :], LN_EPS).then_inc(eps_set, 1)
                dve.wait_ge(edges_loaded, 32)
                nc.vector.tensor_reduce(low[:, :], dst_rows[:, :, :], AX.X, ALU.min).then_inc(spans_done, 1)
                nc.vector.tensor_reduce(high[:, :], dst_rows[:, :, :], AX.X, ALU.max).then_inc(step, 1)
                nc.vector.tensor_copy(dst_f[:, :], dst_i[:, :]).then_inc(step, 1)
                dve.wait_ge(step, 2)
                nc.vector.tensor_tensor(span[:, :], high[:, :], low[:, :], ALU.subtract).then_inc(step, 1)
                dve.wait_ge(step, 3)
                nc.vector.tensor_scalar(high[:, :], span[:, :], LOG_WIN, None,
                                        ALU.arith_shift_right).then_inc(step, 1)
                dve.wait_ge(step, 4)
                nc.vector.tensor_reduce(more[:, :], high[:, :], AX.X, ALU.max).then_inc(spans_done, 1)
                stat_steps = 5

                def statistics(i, s):
                    dve.wait_ge(x_loaded[s], 16 * i + 16)
                    for j in range(PB):
                        last = nc.vector.bn_stats(stats[:, s, j, :], rows[:, s, j, :])
                    last.then_inc(step, 1)
                    wait_apart(dve, step, i * PSLOTS + (s + stat_steps), m.passed)
                    for j in range(PB):
                        last = nc.vector.bn_aggr(mv[:, s, j, :], stats[:, s, j, :])
                    last.then_inc(mv_done, 1)

                def normalise(i, s, first):
                    dve.wait_ge(sd_done, i * PSLOTS + (s + 1))
                    nc.vector.reciprocal(rstd[:, s, :], sd[:, s, :]).then_inc(rstd_done, 1)
                    dve.wait_ge(rstd_done, i * PSLOTS + (s + 1))
                    if not first:
                        dve.wait_ge(xn_stored[s], 16 * i)
                    for j in range(PB):
                        last = nc.vector.tensor_scalar(normed[:, s, j, :], rows[:, s, j, :], mv[:, s, j, 0:1],
                                                       rstd[:, s, j:j + 1], ALU.subtract, ALU.mult)
                    last.then_inc(xn_done, 1)

                def turn(i, first):
                    for s in range(PSLOTS):
                        statistics(i, s)
                        if s:
                            normalise(i, s - 1, first)
                        elif not first:
                            normalise(i - 1, PSLOTS - 1, isinstance(i, int) and i == 1)

                turn(0, True)
                turn(1, False)
                with dve.Fori(2, loops) as i:
                    turn(i, False)
                normalise(loops - 1, PSLOTS - 1, False)
                dve.wait_ge(iotas_done, 4)
                nc.vector.tensor_copy(m.cols[:, :], iota_i[:, :]).then_inc(tables_done, 1)
                nc.vector.tensor_scalar(m.valid[:, :], node_i[:, :], float(N), None, ALU.is_lt).then_inc(tables_done, 1)
                dve.wait_ge(spans_back, 48)
                nc.vector.tensor_copy(low_f[:, :], low_all[:, :]).then_inc(tables_done, 1)
                nc.vector.tensor_copy(more_f[:, :], more_row[:, :]).then_inc(tables_done, 1)
                nc.vector.memset(more_one[:, :], 1.0).then_inc(tables_done, 1)
                dve.wait_ge(tables_done, 5)
                nc.vector.tensor_tensor(m.dst_rel[:, 0:NCH].rearrange("p (g c) -> p g c", c=GROUP),
                                        dst_f[:, :].rearrange("p (g c) -> p g c", c=GROUP),
                                        low_f[:, :].rearrange("p (g o) -> p g o", o=1)
                                        .to_broadcast([P, TURNS * TURN, GROUP]), ALU.subtract).then_inc(tables_done, 1)
                nc.vector.tensor_tensor_scan(more_sum[:, :], more_one[:, :], more_f[:, :], 0.0,
                                             ALU.mult, ALU.add).then_inc(tables_done, 1)
                dve.wait_ge(tables_done, 7)
                nc.vector.tensor_copy(m.table[0:1, :, TURN + 1], more_sum[:, :]).then_inc(tables_done, 1)
                nc.vector.tensor_tensor(m.table[0:1, :, TURN], more_sum[:, :], more_f[:, :],
                                        ALU.subtract).then_inc(tables_done, 1)
                nc.vector.memset(m.dst_rel[:, NCH:NCH + SLOTS], 0.0).then_inc(tables_done, 1)
                nc.vector.memset(m.wgt[:, NCH:NCH + SLOTS], 0.0).then_inc(tables_done, 1)
                dve.wait_ge(consts_loaded, 16 * len(consts))
                nc.vector.tensor_scalar(m.ln1_gh[:, :], m.ln1_gh[:, :], -0.5, None, ALU.mult).then_inc(tables_done, 1)
                nc.vector.tensor_scalar(m.ln2_gh[:, :], m.ln2_gh[:, :], -0.5, None, ALU.mult).then_inc(tables_done, 1)
                dve.wait_ge(tables_done, 13)


def gather(nc, m, layer, source, mixer):
    with ExitStack() as ctx:
        def sb(name, shape, dt=F32):
            return ctx.enter_context(nc.sbuf_tensor(f"{name}{layer}", shape, dt))

        sem = semaphores(nc, ctx, layer)

        def ps(name, a, b):
            bank = ctx.enter_context(nc.psum_tensor(f"{name}{layer}", [P, BANK], F32))
            return bank[:, 0:a * b].rearrange("p (a b) -> p a b", a=a)

        rows = sb("rows", [P, 2, SLOTS, D])
        sel = sb("sel", [P, SLOTS, WIN])
        idx = sb("idx", [P, 2, SLOTS], I32)
        rel_now = sb("rel_now", [P, SLOTS])
        wgt_now = sb("wgt_now", [P, SLOTS])
        sums = [ps(f"sums{g}_", KD, WIN) for g in range(TURN)]

        idx_loaded = [sem(f"idx_loaded{u}_") for u in range(2)]
        rows_loaded = [[sem(f"rows_loaded{u}{g}_") for g in range(TURN)] for u in range(2)]
        rows_used = [sem(f"rows_used{u}_") for u in range(2)]
        sel_ready = [sem(f"sel_ready{g}_") for g in range(TURN)]
        summed = [sem(f"summed{g}_") for g in range(TURN)]
        now_ready = sem("now_ready")
        added = sem("added")
        agg_zeroed = sem("agg_zeroed")
        further_sel = sem("further_sel")
        further_sum = sem("further_sum")
        further_step = sem("further_step")

        mix = mixer(nc, m, sb, sem, ps)
        loops = TURNS // 2

        def window_products(g, h, u, before):
            for c in range(GROUP):
                k = g * GROUP + c
                last = nc.tensor.matmul(sums[g][:, h, :], rows[:, u, k, h * P:(h + 1) * P], sel[:, k, :],
                                        start=(c == 0), stop=(c == GROUP - 1))
                if c == 0 and before is not None:
                    last.then_inc(before, 1)
            return last

        def selection(g):
            for c in range(GROUP):
                k = g * GROUP + c
                last = nc.vector.tensor_scalar(sel[:, k, :], m.cols[:, :], rel_now[:, k:k + 1], wgt_now[:, k:k + 1],
                                               ALU.is_equal, ALU.mult)
            return last

        def add_window(g, at):
            window = m.agg[:, :, bass.ds(at, WIN)]
            return nc.vector.tensor_tensor(window, window, sums[g][:, :, :], ALU.add)

        with nc.Block(f"gather{layer}") as block:
            @block.sync
            def _(sp):
                for u in range(2):
                    sp.dma_start(idx[:, u, :], m.in_src[u]).then_inc(idx_loaded[u], 16)
                    mix.load(sp, u, u)
                mix.load_weights(sp)
                with sp.Fori(1, loops) as i:
                    for u in range(2):
                        sp.wait_ge(rows_loaded[u][TURN - 1], 16 * GROUP * i)
                        sp.dma_start(idx[:, u, :], m.in_src[bass.ds(2 * i + u, 1)].rearrange("o p c -> (o p) c")
                                     ).then_inc(idx_loaded[u], 16)
                        mix.free(sp, i - 1, u)
                        mix.load(sp, 2 * i + u, u)
                        mix.store(sp, i - 1, u)
                mix.load_past(sp)
                mix.stored(sp)
                sp.wait_ge(m.xe_zeroed, 16 * TURNS)

            @block.gpsimd
            def _(pool):
                with pool.Fori(0, loops) as i:
                    for u in range(2):
                        pool.wait_ge(idx_loaded[u], 16 * i + 16)
                        wait_apart(pool, rows_used[u], i + 1, m.pool_passed)
                        for k in range(SLOTS):
                            nc.gpsimd.indirect_dma_start(
                                out=rows[:, u, k, :], out_offset=None, in_=source,
                                in_offset=bass.IndirectOffsetOnAxis(ap=idx[:, u, k:k + 1], axis=0)
                            ).then_inc(rows_loaded[u][k // GROUP], 16)

            @block.vector
            def _(dve):
                def take(t):
                    nc.vector.tensor_copy(rel_now[:, :], m.dst_rel[:, bass.ds(t * SLOTS, SLOTS)]).then_inc(now_ready, 1)
                    nc.vector.tensor_copy(wgt_now[:, :], m.wgt[:, bass.ds(t * SLOTS, SLOTS)]).then_inc(now_ready, 1)
                    dve.wait_ge(now_ready, 2 * t + 2)
                    selection(0).then_inc(sel_ready[0], 1)

                nc.vector.memset(m.agg[:, :, :], 0.0).then_inc(agg_zeroed, 1)
                mix.dve_begin(dve)
                dve.wait_ge(agg_zeroed, 1)
                take(0)
                def turn(i, u):
                    t = 2 * i + u
                    mix.dve(dve, i, u, 0)
                    selection(1).then_inc(sel_ready[1], 1)
                    mix.dve(dve, i, u, 1)
                    low = [dve.value_load(m.table[0:1, bass.ds(t, 1), g], min_val=0, max_val=N - 1)
                           for g in range(TURN)]
                    dve.wait_ge(summed[0], t + 1)
                    add_window(0, low[0]).then_inc(added, 1)
                    mix.dve(dve, i, u, 2)
                    first = dve.value_load(m.table[0:1, bass.ds(t, 1), TURN], min_val=0, max_val=NP)
                    end = dve.value_load(m.table[0:1, bass.ds(t, 1), TURN + 1], min_val=0, max_val=NP)
                    dve.wait_ge(summed[1], t + 1)
                    wait_apart(dve, added, 2 * t + 1, m.passed)
                    add_window(1, low[1]).then_inc(added, 1)
                    wait_apart(dve, added, 2 * t + 2, m.passed)
                    with dve.If(first < end):
                        with dve.Fori(first, end) as w:
                            nc.vector.tensor_scalar(rel_now[:, :], rel_now[:, :], float(-WIN), None,
                                                    ALU.add).then_inc(further_step, 1)
                            dve.wait_ge(further_step, 3 * w + 1)
                            for g in range(TURN):
                                last = selection(g)
                            last.then_inc(further_sel, 1)
                            dve.wait_ge(further_sum, w + 1)
                            for g in range(TURN):
                                at = low[g] + (w - first + 1) * WIN
                                inside = at <= NP
                                at = dve.snap(inside * at + (1 - inside) * NP).with_bounds(min_val=0, max_val=NP)
                                add_window(g, at).then_inc(further_step, 1)
                                wait_apart(dve, further_step, 3 * w + g + 2, m.passed)
                    take(t + 1)
                    mix.dve(dve, i, u, 3)

                two_by_two(dve, loops, turn)
                mix.dve_end(dve)

            @block.scalar
            def _(act):
                mix.act_begin(act)
                two_by_two(act, loops, lambda i, u: mix.act(act, i, u))
                mix.act_end(act)

            @block.tensor
            def _(pe):
                pe.sem_inc(rows_used[0], 1)
                mix.pe_begin(pe)

                def turn(i, u):
                    t = 2 * i + u
                    first = pe.value_load(m.table[0:1, bass.ds(t, 1), TURN], min_val=0, max_val=NP)
                    end = pe.value_load(m.table[0:1, bass.ds(t, 1), TURN + 1], min_val=0, max_val=NP)
                    mix.pe(pe, i, u, 0)
                    for g in range(TURN):
                        for h in range(KD):
                            if h == 0:
                                pe.wait_ge(sel_ready[g], t + 1)
                                pe.wait_ge(rows_loaded[u][g], 16 * GROUP * (i + 1))
                            last = window_products(g, h, u, rows_used[1 - u] if g == 0 and h == 0 else None)
                            if h == KD - 1:
                                last.then_inc(summed[g], 1)
                            if g * KD + h < TURN * KD - 1:
                                mix.pe(pe, i, u, 1 + g * KD + h)
                    with pe.If(first < end):
                        with pe.Fori(first, end) as w:
                            pe.wait_ge(further_sel, w + 1)
                            for g in range(TURN):
                                for h in range(KD):
                                    last = window_products(g, h, u, None)
                            last.then_inc(further_sum, 1)
                    mix.pe(pe, i, u, TURN * KD)

                two_by_two(pe, loops, turn)
                mix.pe_end(pe)
        mix.after()


def keys_values(nc, m, sb, sem, ps):
    mix = Memory()
    w_k = sb("w_k", [P, KD, D])
    w_v = sb("w_v", [P, KD, D])
    tile = sb("kv_tile", [P, 2, D])
    xt = sb("kv_xt", [P, KD, P])
    k_min = sb("k_min", [P, D])
    k_exp = sb("k_exp", [P, D])
    keys = sb("keys", [P, D])
    values = sb("values", [P, KD, KVS])
    turned = ps("kv_turned", KD, P)
    proj = [ps(f"kv_proj{n}_", 1, D) for n in range(2)]
    total = ps("kv_total", KD, KVS)

    weights_loaded = sem("kv_weights_loaded")
    tile_loaded = [sem(f"kv_tile_loaded{u}_") for u in range(2)]
    tile_turned = sem("kv_tile_turned")
    xt_ready = sem("kv_xt_ready")
    projected = sem("kv_projected")
    k_min_ready = sem("k_min_ready")
    k_exp_ready = sem("k_exp_ready")
    keys_ready = sem("keys_ready")
    values_ready = sem("values_ready")
    total_opened = sem("kv_total_opened")
    total_done = sem("kv_total_done")
    kv_zeroed = sem("kv_zeroed")
    kv_done = sem("kv_done")

    def load(sp, t, u):
        sp.dma_start(tile[:, u, :], m.xn[bass.ds(t * P, P), :]).then_inc(tile_loaded[u], 16)

    def load_weights(sp):
        for to, of in ((w_k, m.in_w_k), (w_v, m.in_w_v)):
            sp.dma_start(to[:, :, :], of.rearrange("(k p) n -> p k n", p=P)).then_inc(weights_loaded, 16)

    def free(sp, i, u):
        sp.wait_ge(tile_turned, 2 * i + (u + 1))

    def pe_begin(pe):
        pe.wait_ge(weights_loaded, 32)
        nc.tensor.matmul(total[:, :, :], m.ident[:, :], m.zeros[:, :].rearrange("p (k n) -> p k n", k=KD),
                         start=True, stop=False)

    def pe(pe, i, u, place):
        t = 2 * i + u
        if place == 0:
            pe.wait_ge(tile_loaded[u], 16 * i + 16)
            for h in range(KD):
                last = nc.tensor.transpose(turned[:, h, :], tile[:, u, h * P:(h + 1) * P], m.ident[:, :])
            last.then_inc(tile_turned, 1)
        if place == 1:
            pe.wait_ge(xt_ready, t + 1)
            for n, w in enumerate((w_k, w_v)):
                for k in range(KD):
                    last = nc.tensor.matmul(proj[n][:, 0, :], xt[:, k, :], w[:, k, :], start=(k == 0), stop=(k == KD - 1))
            last.then_inc(projected, 1)
        if place == 3:
            pe.wait_ge(keys_ready, t + 1)
            pe.wait_ge(values_ready, 2 * t + 2)
            for h in range(KD):
                nc.tensor.matmul(total[:, h, :], keys[:, h * P:(h + 1) * P], values[:, h, :], start=False, stop=False)

    def pe_end(pe):
        nc.tensor.matmul(total[:, :, :], m.ident[:, :], m.zeros[:, :].rearrange("p (k n) -> p k n", k=KD),
                         start=False, stop=True).then_inc(total_done, 1)

    def dve(dve, i, u, place):
        t = 2 * i + u
        if place == 1:
            dve.wait_ge(projected, t + 1)
            nc.vector.tensor_scalar(k_min[:, :], proj[0][:, 0, :], 0.0, None, ALU.min).then_inc(k_min_ready, 1)
        if place == 2:
            dve.wait_ge(k_exp_ready, t + 1)
            nc.vector.scalar_tensor_tensor(keys[:, :], proj[0][:, 0, :], 0.0, k_exp[:, :],
                                           ALU.max, ALU.add).then_inc(keys_ready, 1)

    def act(act, i, u):
        t = 2 * i + u
        act.dma_start(m.xe[bass.ds(t * (ZERO * P), ZERO * P), :].rearrange("(p n) f -> p n f", p=P),
                      m.zeros[:, 0:XW].rearrange("p (o f) -> p o f", o=1).to_broadcast([P, ZERO, XW])
                      ).then_inc(m.xe_zeroed, 16)
        act.wait_ge(tile_turned, t + 1)
        nc.scalar.copy(xt[:, :, :], turned[:, :, :]).then_inc(xt_ready, 1)
        act.wait_ge(projected, t + 1)
        nc.scalar.copy(values[:, :, 0:P], proj[1][:, 0, :].rearrange("p (k n) -> p k n", k=KD)).then_inc(values_ready, 1)
        nc.scalar.copy(values[:, :, P:KVS],
                       m.valid[:, bass.ds(t, 1)].rearrange("p (o n) -> p o n", o=1).to_broadcast([P, KD, 1])
                       ).then_inc(values_ready, 1)
        act.wait_ge(k_min_ready, t + 1)
        nc.scalar.activation(k_exp[:, :], k_min[:, :], ACT.Exp).then_inc(k_exp_ready, 1)

    def after():
        with nc.Block("kv") as block:
            @block.vector
            def _(dve):
                dve.wait_ge(total_done, 1)
                nc.vector.memset(m.kv[:, :, :], 0.0).then_inc(kv_zeroed, 1)
                dve.wait_ge(kv_zeroed, 1)
                for j in range(HC):
                    head = slice(j * HD, (j + 1) * HD)
                    nc.vector.tensor_scalar(m.kv[head, :, head], total[head, :, head], 1.0 / N, None, ALU.mult)
                    nc.vector.tensor_copy(m.kv[head, :, P + j:P + j + 1], total[head, :, P:KVS]).then_inc(kv_done, 1)
                dve.wait_ge(kv_done, HC)

    mix.load, mix.free, mix.pe_begin, mix.pe, mix.pe_end = load, free, pe_begin, pe, pe_end
    mix.dve, mix.act, mix.after = dve, act, after
    mix.store = lambda sp, i, u: None
    mix.load_weights = load_weights
    mix.load_past = mix.stored = mix.dve_begin = mix.act_begin = mix.dve_end = mix.act_end = lambda engine: None
    return mix


def attend(nc, m, sb, sem, ps):
    mix = Memory()
    tile = sb("tile", [P, 2, D])
    xt = sb("xt", [P, 2, KD, P])
    q_min = sb("q_min", [P, KD, P])
    queries = sb("queries", [P, KD, P])
    den = sb("den", [P, KD, HC])
    inv = sb("inv", [P, KD, HC])
    msg = sb("msg", [P, D])
    msg_t = sb("msg_t", [P, KD, P])
    norm_t = sb("norm_t", [P, KD, P])
    hidden = sb("hidden", [P, F1 // P, P])
    scaled = sb("scaled", [P, D])
    result = sb("result", [P, 2, D])
    stats = sb("stats", [P, 2, 6])
    mv = sb("mv", [P, 2, 2])
    var = sb("var", [P, 2, 1])
    ln_var = sb("ln_var", [P, 2, 1])
    guess = sb("guess", [P, 2, 1])
    square = sb("square", [P, 2, 1])
    inv_sd = sb("inv_sd", [P, 2, 1])

    tile_ps = ps("tile_ps", KD, P)
    query_ps = tile_ps
    num_ps = ps("num_ps", KD, KVW)
    turn_ps = ps("turn_ps", KD, P)
    row_ps = [ps(f"row_ps{n}_", 1, D)[:, 0, :] for n in range(2)]
    hidden_ps = ps("hidden_ps", F1 // P, P)

    tile_loaded = [sem(f"tile_loaded{u}_") for u in range(2)]
    tile_turned = sem("tile_turned")
    xt_ready = sem("xt_ready")
    query_projected = sem("query_projected")
    q_min_ready = sem("q_min_ready")
    q_exp_ready = sem("q_exp_ready")
    queries_ready = sem("queries_ready")
    num_ready = sem("num_ready")
    den_ready = sem("den_ready")
    inv_ready = sem("inv_ready")
    msg_ready = sem("msg_ready")
    msg_turned = sem("msg_turned")
    msg_t_ready = sem("msg_t_ready")
    msg_projected = sem("msg_projected")
    normed_ready = sem("normed_ready")
    norm_turned = sem("norm_turned")
    norm_t_ready = sem("norm_t_ready")
    hidden_done = sem("hidden_done")
    hidden_ready = sem("hidden_ready")
    mlp_done = sem("mlp_done")
    base_ready = sem("base_ready")
    scaled_ready = sem("scaled_ready")
    mixed = sem("mixed")
    stored = [sem(f"mix_stored{u}_") for u in range(2)]
    result_free = [sem(f"result_free{u}_") for u in range(2)]
    ln_step = [sem(f"ln_step{n}_") for n in range(2)]
    var_ready = [sem(f"var_ready{n}_") for n in range(2)]
    log_ready = [sem(f"log_ready{n}_") for n in range(2)]
    guess_ready = [sem(f"guess_ready{n}_") for n in range(2)]
    inv_sd_ready = [sem(f"inv_sd_ready{n}_") for n in range(2)]

    def load(sp, t, u):
        sp.dma_start(tile[:, u, :], m.xn[bass.ds(t * P, P), :]).then_inc(tile_loaded[u], 16)

    def free(sp, i, u):
        sp.wait_ge(base_ready, 2 * i + (u + 1))

    def store(sp, i, u):
        t = 2 * i + u
        sp.wait_ge(mixed, t + 1)
        sp.dma_start(m.mix[bass.ds(t * P, P), :], result[:, u, :]).then_inc(stored[u], 16)
        sp.wait_ge(stored[u], 16 * i + 16)
        sp.sem_inc(result_free[u], 1)

    def load_past(sp):
        free(sp, TURNS // 2 - 1, 0)
        load(sp, TURNS, 0)

    def all_stored(sp):
        for u in range(2):
            store(sp, TURNS // 2 - 1, u)

    def turn_tile(pe, t, u, i):
        pe.wait_ge(tile_loaded[u], 16 * i + 16)
        for h in range(KD):
            last = nc.tensor.transpose(tile_ps[:, h, :], tile[:, u, h * P:(h + 1) * P], m.ident[:, :])
        last.then_inc(tile_turned, 1)

    def project_queries(pe, t, u):
        pe.wait_ge(xt_ready, t + 1)
        for h in range(KD):
            for k in range(KD):
                last = nc.tensor.matmul(query_ps[:, h, :], m.w_q[:, k, h * P:(h + 1) * P], xt[:, u, k, :],
                                        start=(k == 0), stop=(k == KD - 1))
        last.then_inc(query_projected, 1)

    def mlp_output(pe, t):
        pe.wait_ge(hidden_ready, t + 1)
        for o in range(F1 // P):
            last = nc.tensor.matmul(row_ps[1], hidden[:, o, :], m.w_2[:, o, :], start=(o == 0),
                                    stop=(o == F1 // P - 1))
        last.then_inc(mlp_done, 1)

    def pe_begin(pe):
        turn_tile(pe, 0, 0, 0)
        project_queries(pe, 0, 0)

    def pe(pe, i, u, place):
        t = 2 * i + u
        if place == 1:
            pe.wait_ge(queries_ready, t + 1)
            for h in range(KD):
                last = nc.tensor.matmul(num_ps[:, h, :], queries[:, h, :], m.kv[:, h, :], start=True, stop=True)
            last.then_inc(num_ready, 1)
            if not before_first(i, u, 1):
                mlp_output(pe, t - 1)
        if place == 2:
            pe.wait_ge(msg_ready, t + 1)
            for h in range(KD):
                last = nc.tensor.transpose(turn_ps[:, h, :], msg[:, h * P:(h + 1) * P], m.ident[:, :])
            last.then_inc(msg_turned, 1)
            turn_tile(pe, t + 1, 1 - u, i + u)
            pe.wait_ge(msg_t_ready, t + 1)
            for k in range(KD):
                last = nc.tensor.matmul(row_ps[0], msg_t[:, k, :], m.w_m[:, k, :], start=(k == 0), stop=(k == KD - 1))
            last.then_inc(msg_projected, 1)
        if place == 4:
            pe.wait_ge(normed_ready, t + 1)
            for h in range(KD):
                last = nc.tensor.transpose(turn_ps[:, h, :], msg[:, h * P:(h + 1) * P], m.ident[:, :])
            last.then_inc(norm_turned, 1)
            project_queries(pe, t + 1, 1 - u)
            pe.wait_ge(norm_t_ready, 2 * t + 2)
            for o in range(F1 // P):
                for k in range(2 * KD):
                    of = xt[:, u, k, :] if k < KD else norm_t[:, k - KD, :]
                    last = nc.tensor.matmul(hidden_ps[:, o, :], m.w_1[:, k, o * P:(o + 1) * P], of,
                                            start=(k == 0), stop=(k == 2 * KD - 1))
            last.then_inc(hidden_done, 1)

    def pe_end(pe):
        mlp_output(pe, TURNS - 1)

    def variance(dve, t, n):
        nc.vector.bn_stats(stats[:, n, :], row_ps[n]).then_inc(ln_step[n], 1)
        wait_apart(dve, ln_step[n], 3 * t + 1, m.passed)
        nc.vector.bn_aggr(mv[:, n, :], stats[:, n, :]).then_inc(ln_step[n], 1)
        dve.wait_ge(ln_step[n], 3 * t + 2)
        nc.vector.tensor_scalar(var[:, n, :], mv[:, n, 1:2], LN_EPS, None, ALU.add).then_inc(var_ready[n], 1)

    def inverse_sd(dve, t, n):
        dve.wait_ge(guess_ready[n], t + 1)
        nc.vector.scalar_tensor_tensor(square[:, n, :], guess[:, n, :], var[:, n, :], guess[:, n, :],
                                       ALU.mult, ALU.mult).then_inc(ln_step[n], 1)
        dve.wait_ge(ln_step[n], 3 * t + 3)
        nc.vector.scalar_tensor_tensor(inv_sd[:, n, :], square[:, n, :], 3.0, guess[:, n, :],
                                       ALU.subtract, ALU.mult).then_inc(inv_sd_ready[n], 1)
        dve.wait_ge(inv_sd_ready[n], t + 1)

    def normalise(dve, to, n):
        return nc.vector.tensor_scalar(to, row_ps[n], mv[:, n, 0:1], inv_sd[:, n, :], ALU.subtract, ALU.mult)

    def guess_sd(act, t, n):
        act.wait_ge(var_ready[n], t + 1)
        nc.scalar.activation(ln_var[:, n, :], var[:, n, :], ACT.Ln).then_inc(log_ready[n], 1)
        act.wait_ge(log_ready[n], t + 1)
        nc.scalar.activation(guess[:, n, :], ln_var[:, n, :], ACT.Exp, scale=-0.5).then_inc(guess_ready[n], 1)

    def min_query(dve, t):
        dve.wait_ge(query_projected, t + 1)
        nc.vector.tensor_scalar(q_min[:, :, :], query_ps[:, :, :], 0.0, None, ALU.min).then_inc(q_min_ready, 1)

    def output_variance(dve, t):
        dve.wait_ge(mlp_done, t + 1)
        variance(dve, t, 1)

    def output(dve, t, u):
        inverse_sd(dve, t, 1)
        normalise(dve, scaled[:, :], 1).then_inc(scaled_ready, 1)
        dve.wait_ge(scaled_ready, 2 * t + 1)
        nc.vector.tensor_tensor(scaled[:, :], scaled[:, :], m.ln2_gh[:, :], ALU.mult).then_inc(scaled_ready, 1)
        dve.wait_ge(scaled_ready, 2 * t + 2)
        nc.vector.tensor_tensor(result[:, u, :], result[:, u, :], scaled[:, :], ALU.add).then_inc(mixed, 1)

    def dve_begin(dve):
        min_query(dve, 0)

    def dve(dve, i, u, place):
        t = 2 * i + u
        if place == 0:
            dve.wait_ge(q_exp_ready, t + 1)
            nc.vector.scalar_tensor_tensor(queries[:, :, :], query_ps[:, :, :], 0.0, q_min[:, :, :],
                                           ALU.max, ALU.add).then_inc(queries_ready, 1)
        if place == 1:
            dve.wait_ge(num_ready, t + 1)
            nc.vector.tensor_scalar(den[:, :, :], num_ps[:, :, P:KVW], ATT_EPS, 1.0 / N,
                                    ALU.add, ALU.mult).then_inc(den_ready, 1)
            dve.wait_ge(den_ready, t + 1)
            nc.vector.reciprocal(inv[:, :, :], den[:, :, :]).then_inc(inv_ready, 1)
            dve.wait_ge(inv_ready, t + 1)
            nc.vector.tensor_tensor(msg[:, :].rearrange("p (k h d) -> p k h d", k=KD, h=HC),
                                    num_ps[:, :, 0:P].rearrange("p k (h d) -> p k h d", h=HC),
                                    inv[:, :, :].rearrange("p k (h o) -> p k h o", o=1)
                                    .to_broadcast([P, KD, HC, HD]), ALU.mult).then_inc(msg_ready, 1)
            if not before_first(i, u, 1):
                output_variance(dve, t - 1)
        if place == 2:
            if not before_first(i, u, 1):
                output(dve, t - 1, 1 - u)
            dve.wait_ge(msg_projected, t + 1)
            variance(dve, t, 0)
            dve.wait_ge(result_free[u], i + 1)
            dve.sem_inc(m.passed, 1)
            nc.vector.tensor_tensor(result[:, u, :], tile[:, u, :], m.ln2_b[:, :], ALU.add).then_inc(base_ready, 1)
            inverse_sd(dve, t, 0)
            normalise(dve, msg[:, :], 0).then_inc(normed_ready, 1)
        if place == 3:
            min_query(dve, t + 1)

    def dve_end(dve):
        output_variance(dve, TURNS - 1)
        output(dve, TURNS - 1, 1)

    def copy_tile(act, t, u):
        act.wait_ge(tile_turned, t + 1)
        nc.scalar.copy(xt[:, u, :, :], tile_ps[:, :, :]).then_inc(xt_ready, 1)

    def exp_query(act, t):
        act.wait_ge(q_min_ready, t + 1)
        nc.scalar.activation(q_min[:, :, :], q_min[:, :, :], ACT.Exp).then_inc(q_exp_ready, 1)

    def act_begin(act):
        act.preload_act_table_set(TABLES)
        for u in range(2):
            act.sem_inc(result_free[u], 1)
        copy_tile(act, 0, 0)
        exp_query(act, 0)

    def act(act, i, u):
        t = 2 * i + u
        if not before_first(i, u, 1):
            guess_sd(act, t - 1, 1)
        act.wait_ge(msg_turned, t + 1)
        nc.scalar.copy(msg_t[:, :, :], turn_ps[:, :, :]).then_inc(msg_t_ready, 1)
        copy_tile(act, t + 1, 1 - u)
        guess_sd(act, t, 0)
        act.wait_ge(norm_turned, t + 1)
        for h in range(KD):
            nc.scalar.activation(norm_t[:, h, :], turn_ps[:, h, :], ACT.Identity, scale=m.ln1_gh[:, h:h + 1],
                                 bias=m.ln1_b[:, h:h + 1]).then_inc(norm_t_ready, 1)
        exp_query(act, t + 1)
        act.wait_ge(hidden_done, t + 1)
        nc.scalar.activation(hidden[:, :, :], hidden_ps[:, :, :], ACT.Relu).then_inc(hidden_ready, 1)

    def act_end(act):
        guess_sd(act, TURNS - 1, 1)

    mix.load, mix.free, mix.store, mix.stored = load, free, store, all_stored
    mix.pe_begin, mix.pe, mix.pe_end = pe_begin, pe, pe_end
    mix.dve_begin, mix.dve, mix.dve_end = dve_begin, dve, dve_end
    mix.act_begin, mix.act, mix.act_end, mix.load_past = act_begin, act, act_end, load_past
    mix.load_weights = lambda sp: None
    mix.after = lambda: None
    return mix


def dense_first(nc, m):
    with ExitStack() as ctx:
        def sb(name, shape, dt=F32):
            return ctx.enter_context(nc.sbuf_tensor(name, shape, dt))

        sem = semaphores(nc, ctx)

        w_g1 = sb("w_g1", [P, KD, D])
        b_g1 = sb("b_g1", [P, D])
        agg_now = sb("agg_now", [P, 2, KD, PAIR * P])
        pre = sb("pre", [P, 2, PAIR, D])
        exps = sb("exps", [P, 2, PAIR, D])
        positive = sb("positive", [P, 2, PAIR, D])
        h_one = sb("h_one", [P, 2, PAIR, D])
        h = sb("h", [P, 2, PAIR, D])
        z = [ctx.enter_context(nc.psum_tensor(f"z{u}", [P, BANK], F32))[:, :].rearrange("p (j f) -> p j f", j=PAIR)
             for u in range(2)]

        weights_loaded = sem("g1_weights_loaded")
        agg_ready = sem("agg_ready")
        z_ready = sem("z_ready")
        pre_ready = sem("pre_ready")
        parts_ready = sem("elu_parts_ready")
        h_one_ready = sem("h_one_ready")
        h_ready = sem("h_ready")
        h_stored = [sem(f"h_stored{u}") for u in range(2)]
        h_free = sem("h_free")
        loops = NT // PAIR // 2
        UNITS = 2 * loops
        h1_blocks = m.h1.rearrange("(b j p) f -> b p j f", p=P, j=PAIR)

        with nc.Block("dense1") as block:
            @block.gpsimd
            def _(pool):
                def copy(i, u):
                    q = 2 * i + u
                    wait_apart(pool, z_ready, q + 1, m.pool_passed)
                    nc.gpsimd.tensor_copy(agg_now[:, u, :, :], m.agg[:, :, bass.ds(q * (PAIR * P), PAIR * P)]
                                          ).then_inc(agg_ready, 1)
                two_by_two(pool, loops, copy)

            @block.tensor
            def _(pe):
                pe.sem_inc(z_ready, 2)
                pe.wait_ge(weights_loaded, 32)
                pe.sem_inc(m.pe_passed, 1)

                def product(i, u):
                    q = 2 * i + u
                    pe.wait_ge(agg_ready, q + 1)
                    pe.wait_ge(pre_ready, q + 1)
                    for j in range(PAIR):
                        for k in range(KD):
                            last = nc.tensor.matmul(z[u][:, j, :], agg_now[:, u, k, j * P:(j + 1) * P], w_g1[:, k, :],
                                                    start=(k == 0), stop=(k == KD - 1))
                    last.then_inc(z_ready, 1)
                two_by_two(pe, loops, product)

            @block.vector
            def _(dve):
                def sum_parts(q, u):
                    dve.wait_ge(parts_ready, q + 1)
                    nc.vector.scalar_tensor_tensor(h_one[:, u, :, :], exps[:, u, :, :], 1.0, positive[:, u, :, :],
                                                   ALU.min, ALU.add).then_inc(h_one_ready, 1)

                def unit(i, u):
                    q = 2 * i + u
                    dve.wait_ge(z_ready, q + 3)
                    nc.vector.tensor_tensor(pre[:, u, :, :], z[u], b_g1[:, :].rearrange("p (o f) -> p o f", o=1)
                                            .to_broadcast([P, PAIR, D]), ALU.add).then_inc(pre_ready, 1)
                    if not before_first(i, u, 1):
                        sum_parts(q - 1, 1 - u)

                dve.sem_inc(pre_ready, 2)
                dve.wait_ge(weights_loaded, 32)
                dve.sem_inc(m.passed, 1)
                two_by_two(dve, loops, unit)
                sum_parts(UNITS - 1, 1)

            @block.scalar
            def _(act):
                def less_one(q, u):
                    act.wait_ge(h_one_ready, q + 1)
                    act.wait_ge(h_free, q + 1)
                    act.sem_inc(m.act_passed, 1)
                    nc.scalar.activation(h[:, u, :, :], h_one[:, u, :, :], ACT.Copy, bias=-1.0).then_inc(h_ready, 1)

                def unit(i, u):
                    q = 2 * i + u
                    act.wait_ge(pre_ready, q + 3)
                    nc.scalar.activation(exps[:, u, :, :], pre[:, u, :, :], ACT.Exp)
                    nc.scalar.activation(positive[:, u, :, :], pre[:, u, :, :], ACT.Relu).then_inc(parts_ready, 1)
                    if not before_first(i, u, 1):
                        less_one(q - 1, 1 - u)

                two_by_two(act, loops, unit)
                less_one(UNITS - 1, 1)

            @block.sync
            def _(sp):
                sp.dma_start(w_g1[:, :, :], m.in_w_g1.rearrange("(k p) n -> p k n", p=P)).then_inc(weights_loaded, 16)
                sp.dma_start(b_g1[:, :], m.in_b_g1.rearrange("(o n) -> o n", o=1).to_broadcast([P, D])
                             ).then_inc(weights_loaded, 16)

                def store(i, u):
                    sp.wait_ge(h_ready, 2 * i + (u + 1))
                    sp.dma_start(h1_blocks[bass.ds(2 * i + u, 1)].rearrange("b p j f -> (b p) j f"),
                                 h[:, u, :, :]).then_inc(h_stored[u], 16)
                    if not before_first(i, u, 1):
                        sp.wait_ge(h_stored[1 - u], 16 * (i + u))
                        sp.sem_inc(h_free, 1)

                sp.sem_inc(h_free, 2)
                two_by_two(sp, loops, store)
                for u in range(2):
                    sp.wait_ge(h_stored[u], 16 * loops)


def dense_second(nc, m):
    with ExitStack() as ctx:
        def sb(name, shape, dt=F32):
            return ctx.enter_context(nc.sbuf_tensor(name, shape, dt))

        sem = semaphores(nc, ctx)

        x_in = sb("x_in", [P, 2, PAIR, D])
        x2 = sb("x2_now", [P, 2, PAIR, D])
        mix_in = sb("mix_in", [P, 2, PAIR, D])
        agg_now = sb("agg_now2", [P, 2, KD, PAIR * P])
        w_g2 = sb("w_g2", [P, KD, D])
        b_g2 = sb("b_g2", [P, D])
        pre = sb("pre2", [P, 2, PAIR, D])
        exps = sb("exps2", [P, PAIR, D])
        positive = sb("positive2", [P, PAIR, D])
        h_one = sb("h2_one", [P, PAIR, D])
        xf = sb("xf_rows", [P, 2, PAIR, D])
        xf_t = sb("xf_t", [P, PAIR * KD, P])
        stats = sb("x2_stats", [P, PAIR, 6])
        mv = sb("x2_mv", [P, 2, PAIR, 2])
        var = sb("x2_var", [P, PAIR])
        guess = sb("x2_guess", [P, PAIR])
        square = sb("x2_square", [P, PAIR])
        inv_sd = sb("x2_inv_sd", [P, PAIR])

        def ps(name, a, b):
            bank = ctx.enter_context(nc.psum_tensor(name, [P, BANK], F32))
            return bank[:, 0:a * b].rearrange("p (a b) -> p a b", a=a)

        z = [ps(f"z_second{u}", PAIR, D) for u in range(2)]
        xf_ps = ps("xf_ps", PAIR * KD, P)
        logit_ps = [ps(f"logit_ps{u}", PAIR, NE) for u in range(2)]

        weights_loaded = sem("g2_weights_loaded")
        x_loaded = [sem(f"x2_x_loaded{u}") for u in range(2)]
        mix_loaded = [sem(f"mix_loaded{u}") for u in range(2)]
        base_ready = sem("x2_base_ready")
        agg_ready = sem("agg2_ready")
        z_ready = sem("z2_ready")
        pre_ready = sem("pre2_ready")
        parts_ready = sem("elu2_parts_ready")
        h_one_ready = sem("h2_one_ready")
        x2_ready = sem("x2_ready")
        x2_stored = [sem(f"x2_stored{u}") for u in range(2)]
        xf_stored = [sem(f"xf_stored{u}") for u in range(2)]
        stored = sem("x2_and_xf_stored")
        var_ready = sem("x2_var_ready")
        log_ready = sem("x2_log_ready")
        guess_ready = sem("x2_guess_ready")
        xf_ready = sem("xf_ready")
        xf_turned = sem("xf_turned")
        xf_t_ready = sem("xf_t_ready")
        logits_done = sem("logits_done")
        logits_ready = sem("logits_ready")
        step = sem("dense2_step")
        loops = NT // PAIR // 2
        UNITS = 2 * loops
        STEPS = 4

        def blocks(of):
            return of.rearrange("(b j p) f -> b p j f", p=P, j=PAIR)

        with nc.Block("dense2") as block:
            @block.sync
            def _(sp):
                def load(q, u):
                    sp.dma_start(x_in[:, u, :, :], blocks(m.x)[bass.ds(q, 1)].rearrange("b p j f -> (b p) j f")
                                 ).then_inc(x_loaded[u], 16)
                    sp.dma_start(mix_in[:, u, :, :], blocks(m.mix)[bass.ds(q, 1)].rearrange("b p j f -> (b p) j f")
                                 ).then_inc(mix_loaded[u], 16)

                def store_x2(q, u):
                    sp.dma_start(blocks(m.x2)[bass.ds(q, 1)].rearrange("b p j f -> (b p) j f"),
                                 x2[:, u, :, :]).then_inc(x2_stored[u], 16)
                    sp.dma_start(blocks(m.out)[bass.ds(q, 1)].rearrange("b p j f -> (b p) j f"),
                                 x2[:, u, :, :]).then_inc(x2_stored[u], 16)

                def store_xf(q, u):
                    sp.wait_ge(xf_ready, q + 1)
                    sp.dma_start(blocks(m.xf)[bass.ds(q, 1)].rearrange("b p j f -> (b p) j f"),
                                 xf[:, u, :, :]).then_inc(xf_stored[u], 16)

                def unit(i, u):
                    q = 2 * i + u
                    if before_first(i, u, 2):
                        load(q, u)
                        return
                    sp.wait_ge(x2_ready, q - 1)
                    load(q, u)
                    if not before_first(i - 1, u, 1):
                        wait_apart(sp, x2_stored[1 - u], 32 * (i + (u - 1)), m.sp_passed)
                        sp.wait_ge(xf_stored[1 - u], 16 * (i + (u - 1)))
                        sp.sem_inc(stored, 1)
                    store_x2(q - 2, u)
                    store_xf(q - 2, u)

                sp.dma_start(w_g2[:, :, :], m.in_w_g2.rearrange("(k p) n -> p k n", p=P)).then_inc(weights_loaded, 16)
                sp.dma_start(b_g2[:, :], m.in_b_g2.rearrange("(o n) -> o n", o=1).to_broadcast([P, D])
                             ).then_inc(weights_loaded, 16)
                two_by_two(sp, loops, unit, peeled=2)
                for q in (UNITS - 2, UNITS - 1):
                    u = q % 2
                    count = 16 * ((q - 1) // 2 + 1)
                    sp.wait_ge(x2_stored[1 - u], 2 * count)
                    sp.wait_ge(xf_stored[1 - u], count)
                    sp.sem_inc(stored, 1)
                    sp.wait_ge(x2_ready, q + 1)
                    store_x2(q, u)
                    store_xf(q, u)
                for u in range(2):
                    sp.wait_ge(x2_stored[u], 32 * loops)
                    sp.wait_ge(xf_stored[u], 16 * loops)

            @block.gpsimd
            def _(pool):
                def add(i, u):
                    pool.wait_ge(x_loaded[u], 16 * i + 16)
                    pool.wait_ge(mix_loaded[u], 16 * i + 16)
                    pool.sem_inc(m.pool_passed, 1)
                    nc.gpsimd.tensor_tensor(x_in[:, u, :, :], x_in[:, u, :, :], mix_in[:, u, :, :],
                                            ALU.add).then_inc(base_ready, 1)
                two_by_two(pool, loops, add)

            @block.scalar
            def _(act):
                def copy_agg(q, u):
                    nc.scalar.copy(agg_now[:, u, :, :], m.agg[:, :, bass.ds(q * (PAIR * P), PAIR * P)]
                                   ).then_inc(agg_ready, 1)

                def copy_xf(q):
                    act.wait_ge(xf_turned, q + 1)
                    nc.scalar.copy(xf_t[:, :, :], xf_ps[:, :, :]).then_inc(xf_t_ready, 1)

                def unit(i, u, more=True):
                    q = 2 * i + u
                    if not before_first(i, u, 2):
                        copy_xf(q - 2)
                    act.wait_ge(pre_ready, q + 3)
                    nc.scalar.activation(exps[:, :, :], pre[:, u, :, :], ACT.Exp)
                    nc.scalar.activation(positive[:, :, :], pre[:, u, :, :], ACT.Relu).then_inc(parts_ready, 1)
                    if more:
                        copy_agg(q + 2, u)
                    act.wait_ge(var_ready, q + 1)
                    nc.scalar.activation(guess[:, :], var[:, :], ACT.Ln).then_inc(log_ready, 1)
                    act.wait_ge(log_ready, 2 * q + 1)
                    nc.scalar.activation(guess[:, :], guess[:, :], ACT.Exp, scale=-0.5).then_inc(log_ready, 1)
                    act.wait_ge(log_ready, 2 * q + 2)
                    nc.scalar.activation(square[:, :], guess[:, :], ACT.Square).then_inc(guess_ready, 1)

                act.preload_act_table_set(TABLES)
                for u in range(2):
                    copy_agg(u, u)
                for u in range(2):
                    unit(0, u)
                with act.Fori(1, loops - 1) as i:
                    for u in range(2):
                        unit(i, u)
                for u in range(2):
                    unit(loops - 1, u, more=False)
                for q in (UNITS - 2, UNITS - 1):
                    copy_xf(q)

            @block.tensor
            def _(pe):
                def turn_rows(q, u):
                    pe.wait_ge(xf_ready, q + 1)
                    for j in range(PAIR):
                        for h in range(KD):
                            last = nc.tensor.transpose(xf_ps[:, j * KD + h, :], xf[:, u, j, h * P:(h + 1) * P],
                                                       m.ident[:, :])
                    last.then_inc(xf_turned, 1)

                def gate_products(q, u):
                    pe.wait_ge(xf_t_ready, q + 1)
                    pe.wait_ge(logits_ready, q + 1)
                    for j in range(PAIR):
                        for k in range(KD):
                            last = nc.tensor.matmul(logit_ps[u][:, j, :], xf_t[:, j * KD + k, :], m.gate_w[:, k, :],
                                                    start=(k == 0), stop=(k == KD - 1))
                    last.then_inc(logits_done, 1)

                def unit(i, u):
                    q = 2 * i + u
                    pe.wait_ge(agg_ready, q + 1)
                    pe.wait_ge(pre_ready, q + 1)
                    for j in range(PAIR):
                        if j == PAIR - 1:
                            if not before_first(i, u, 3):
                                gate_products(q - 3, 1 - u)
                            if not before_first(i, u, 2):
                                turn_rows(q - 2, u)
                        for k in range(KD):
                            last = nc.tensor.matmul(z[u][:, j, :], agg_now[:, u, k, j * P:(j + 1) * P],
                                                    w_g2[:, k, :], start=(k == 0), stop=(k == KD - 1))
                    last.then_inc(z_ready, 1)

                pe.wait_ge(weights_loaded, 32)
                pe.sem_inc(m.pe_passed, 1)
                two_by_two(pe, loops, unit, peeled=2)
                gate_products(UNITS - 3, 1)
                for u in range(2):
                    turn_rows(UNITS - 2 + u, u)
                    gate_products(UNITS - 2 + u, u)

            @block.vector
            def _(dve):
                def normalise(q, u):
                    dve.wait_ge(guess_ready, q + 1)
                    nc.vector.scalar_tensor_tensor(square[:, :], square[:, :], -0.5, var[:, :],
                                                   ALU.mult, ALU.mult).then_inc(step, 1)
                    wait_apart(dve, step, q * STEPS + 3, m.passed)
                    nc.vector.scalar_tensor_tensor(inv_sd[:, :], square[:, :], 1.5, guess[:, :],
                                                   ALU.add, ALU.mult).then_inc(step, 1)
                    wait_apart(dve, step, q * STEPS + 4, m.passed)
                    for j in range(PAIR):
                        last = nc.vector.tensor_scalar(xf[:, u, j, :], x2[:, u, j, :], mv[:, u, j, 0:1],
                                                       inv_sd[:, j:j + 1], ALU.subtract, ALU.mult)
                    last.then_inc(xf_ready, 1)

                def take_logits(q, u):
                    dve.wait_ge(logits_done, q + 1)
                    nc.vector.tensor_tensor(m.logits[:, bass.ds(q * PAIR, PAIR), :], logit_ps[u][:, :, :],
                                            m.gate_b[:, :].rearrange("p (o e) -> p o e", o=1)
                                            .to_broadcast([P, PAIR, NE]), ALU.add).then_inc(logits_ready, 1)

                def unit(i, u):
                    q = 2 * i + u
                    dve.wait_ge(z_ready, q + 1)
                    nc.vector.tensor_tensor(pre[:, u, :, :], z[u][:, :, :],
                                            b_g2[:, :].rearrange("p (o f) -> p o f", o=1)
                                            .to_broadcast([P, PAIR, D]), ALU.add).then_inc(pre_ready, 1)
                    if not before_first(i, u, 1):
                        normalise(q - 1, 1 - u)
                    dve.wait_ge(parts_ready, q + 1)
                    nc.vector.scalar_tensor_tensor(h_one[:, :, :], exps[:, :, :], 1.0, positive[:, :, :],
                                                   ALU.min, ALU.add).then_inc(h_one_ready, 1)
                    dve.wait_ge(base_ready, q + 1)
                    dve.sem_inc(m.passed, 1)
                    dve.wait_ge(stored, q + 1)
                    dve.sem_inc(m.passed, 1)
                    dve.wait_ge(h_one_ready, q + 1)
                    nc.vector.scalar_tensor_tensor(x2[:, u, :, :], h_one[:, :, :], -1.0, x_in[:, u, :, :],
                                                   ALU.add, ALU.add).then_inc(x2_ready, 1)
                    if not before_first(i, u, 3):
                        take_logits(q - 3, 1 - u)
                    wait_apart(dve, x2_ready, q + 1, m.passed)
                    for j in range(PAIR):
                        last = nc.vector.bn_stats(stats[:, j, :], x2[:, u, j, :])
                    last.then_inc(step, 1)
                    wait_apart(dve, step, q * STEPS + 1, m.passed)
                    for j in range(PAIR):
                        last = nc.vector.bn_aggr(mv[:, u, j, :], stats[:, j, :])
                    last.then_inc(step, 1)
                    dve.wait_ge(step, q * STEPS + 2)
                    nc.vector.tensor_scalar(var[:, :], mv[:, u, :, 1], LN_EPS, None, ALU.add).then_inc(var_ready, 1)

                dve.sem_inc(pre_ready, 2)
                dve.sem_inc(stored, 2)
                dve.sem_inc(logits_ready, 2)
                dve.wait_ge(weights_loaded, 32)
                dve.sem_inc(m.passed, 1)
                two_by_two(dve, loops, unit, peeled=2)
                normalise(UNITS - 1, 1)
                for q in range(UNITS - 3, UNITS):
                    take_logits(q, q % 2)


def route(nc, m):
    with ExitStack() as ctx:
        def sb(name, shape, dt=F32):
            return ctx.enter_context(nc.sbuf_tensor(name, shape, dt))

        sem = semaphores(nc, ctx)

        def ps(name):
            bank = ctx.enter_context(nc.psum_tensor(name, [P, BANK], F32))
            return bank[:, 0:HALF * NE].rearrange("p (j e) -> p j e", e=NE)

        HALF = NT // 2
        probs = sb("probs", [P, NT, NE])
        most = sb("most", [P, NT])
        total = sb("total", [P, NT])
        top = m.prob
        marked = sb("marked", [P, NT, NE])
        first = sb("first", [P, NT])
        chosen = sb("chosen", [P, NT, NE])
        counts = sb("counts", [P, NT, NE])
        ends = sb("ends", [P, NT, NE])
        nth = sb("nth", [P, NT])
        expert_row = sb("expert_row", [P, NT])
        kept = sb("kept", [P, NT])
        row = sb("row", [P, NT])
        one = sb("route_one", [P, NT])
        left_i = sb("left_i", [P, NE], I32)
        left_f = sb("left_f", [P, NE])
        spare_i = sb("spare_i", [P, NT], I32)
        spare_f = sb("spare_f", [P, NT])
        blocks_i = sb("blocks_i", [1, NE], I32)
        blocks_f = sb("blocks_f", [1, NE])
        blocks_end = sb("blocks_end", [1, NE])
        nth_ps = [ps(f"nth_ps{k}") for k in range(2)]
        count_ps = [ps(f"count_ps{k}") for k in range(2)]

        iotas = sem("route_iotas")
        shifted = sem("route_shifted")
        exps_ready = sem("route_exps")
        chosen_ready = sem("chosen_ready")
        counted = sem("counted")
        step = sem("route_step")

        def by_tile(of):
            return of.rearrange("p (j o) -> p j o", o=1).to_broadcast([P, NT, NE])

        def by_expert(of):
            return of.rearrange("p (o e) -> p o e", o=1).to_broadcast([P, NT, NE])

        with nc.Block("route") as block:
            @block.gpsimd
            def _(pool):
                nc.gpsimd.iota(left_i[:, :], [[-1, NE]], base=NE, channel_multiplier=0).then_inc(iotas, 1)
                nc.gpsimd.iota(spare_i[:, :], [[P, NT]], base=TRASH, channel_multiplier=1).then_inc(iotas, 1)

            @block.scalar
            def _(act):
                act.wait_ge(shifted, 1)
                nc.scalar.activation(probs[:, :, :], m.logits[:, :, :], ACT.Exp).then_inc(exps_ready, 1)

            @block.tensor
            def _(pe):
                pe.wait_ge(chosen_ready, 1)
                for k in range(2):
                    half = chosen[:, k * HALF:(k + 1) * HALF, :]
                    nc.tensor.matmul(nth_ps[k], m.upto[:, :], half, start=True, stop=True)
                    nc.tensor.matmul(count_ps[k], m.ones[:, :], half, start=True, stop=True).then_inc(counted, 1)

            @block.vector
            def _(dve):
                count = [0]

                def link(instruction):
                    count[0] += 1
                    instruction.then_inc(step, 1)
                    dve.wait_ge(step, count[0])

                link(nc.vector.tensor_reduce(most[:, :], m.logits[:, :, :], AX.X, ALU.max))
                nc.vector.tensor_tensor(m.logits[:, :, :], m.logits[:, :, :], by_tile(most[:, :]),
                                        ALU.subtract).then_inc(shifted, 1)
                dve.wait_ge(iotas, 2)
                nc.vector.tensor_copy(left_f[:, :], left_i[:, :])
                nc.vector.tensor_copy(spare_f[:, :], spare_i[:, :])
                link(nc.vector.memset(one[:, :], 1.0))
                dve.wait_ge(exps_ready, 1)
                link(nc.vector.tensor_reduce(total[:, :], probs[:, :, :], AX.X, ALU.add))
                link(nc.vector.reciprocal(total[:, :], total[:, :]))
                link(nc.vector.tensor_tensor(probs[:, :, :], probs[:, :, :], by_tile(total[:, :]), ALU.mult))
                link(nc.vector.tensor_reduce(top[:, :], probs[:, :, :], AX.X, ALU.max))
                link(nc.vector.tensor_tensor(marked[:, :, :], probs[:, :, :], by_tile(top[:, :]), ALU.is_equal))
                link(nc.vector.tensor_tensor(marked[:, :, :], marked[:, :, :], by_expert(left_f[:, :]), ALU.mult))
                link(nc.vector.tensor_reduce(first[:, :], marked[:, :, :], AX.X, ALU.max))
                link(nc.vector.tensor_tensor(chosen[:, :, :], by_tile(first[:, :]), by_expert(left_f[:, :]),
                                             ALU.is_equal))
                nc.vector.tensor_tensor(chosen[:, :, :], chosen[:, :, :], by_tile(m.valid[:, :]),
                                        ALU.mult).then_inc(chosen_ready, 1)
                nc.vector.tensor_scalar(expert_row[:, :], first[:, :], float(-ROWS), float(NE * ROWS),
                                        ALU.mult, ALU.add)
                dve.wait_ge(counted, 2)
                for k in range(2):
                    last = nc.vector.tensor_copy(counts[:, k * HALF:(k + 1) * HALF, :], count_ps[k])
                link(last)
                for e in range(NE):
                    last = nc.vector.tensor_tensor_scan(ends[:, :, e], one[:, :], counts[:, :, e], 0.0,
                                                        ALU.mult, ALU.add)
                link(last)
                link(nc.vector.tensor_tensor(counts[:, :, :], ends[:, :, :], counts[:, :, :], ALU.subtract))
                for k in range(2):
                    half = counts[:, k * HALF:(k + 1) * HALF, :]
                    last = nc.vector.tensor_tensor(half, half, nth_ps[k], ALU.add)
                link(last)
                link(nc.vector.tensor_tensor(counts[:, :, :], counts[:, :, :], chosen[:, :, :], ALU.mult))
                link(nc.vector.tensor_reduce(nth[:, :], counts[:, :, :], AX.X, ALU.add))
                nc.vector.tensor_scalar(kept[:, :], nth[:, :], float(CAP), None, ALU.is_le)
                link(nc.vector.tensor_tensor(row[:, :], expert_row[:, :], nth[:, :], ALU.add))
                link(nc.vector.tensor_tensor(kept[:, :], kept[:, :], m.valid[:, :], ALU.mult))
                link(nc.vector.scalar_tensor_tensor(row[:, :], row[:, :], -1.0, spare_f[:, :],
                                                    ALU.add, ALU.subtract))
                link(nc.vector.tensor_tensor(row[:, :], row[:, :], kept[:, :], ALU.mult))
                nc.vector.tensor_tensor(m.row[:, :], row[:, :], spare_f[:, :], ALU.add)
                nc.vector.tensor_scalar(m.token[:, :], spare_f[:, :], float(1 - TRASH), None, ALU.add)
                link(nc.vector.tensor_scalar(blocks_i[:, :], ends[0:1, NT - 1, :], float(CAP), float(TB - 1),
                                             ALU.min, ALU.add))
                link(nc.vector.tensor_scalar(blocks_i[:, :], blocks_i[:, :], LOG_TB, None, ALU.arith_shift_right))
                link(nc.vector.tensor_scalar(blocks_f[:, :], blocks_i[:, :], 1.0, None, ALU.max))
                link(nc.vector.tensor_tensor_scan(blocks_end[:, :], one[0:1, 0:NE], blocks_f[:, :], 0.0,
                                                  ALU.mult, ALU.add))
                nc.vector.tensor_copy(m.blocks[0:1, :, 1], blocks_end[:, :])
                link(nc.vector.tensor_tensor(m.blocks[0:1, :, 0], blocks_end[:, :], blocks_f[:, :], ALU.subtract))


def scatter(nc, m):
    with ExitStack() as ctx:
        def sb(name, shape, dt=F32):
            return ctx.enter_context(nc.sbuf_tensor(name, shape, dt))

        sem = semaphores(nc, ctx)
        rows = sb("s_rows", [P, SETS, ST, XW])
        row_now = sb("row_now", [P, SETS, ST], I32)
        rows_loaded = [sem(f"s_rows_loaded{u}") for u in range(SETS)]
        row_ready = [sem(f"s_row_ready{u}") for u in range(SETS)]
        scattered = [sem(f"scattered{u}") for u in range(SETS)]
        loops = NT // (SETS * ST)
        xf_blocks = m.xf.rearrange("(b j p) f -> b p j f", p=P, j=ST)

        with nc.Block("scatter") as block:
            @block.sync
            def _(sp):
                for u in range(SETS):
                    sp.dma_start(rows[:, u, :, 0:D], xf_blocks[u]).then_inc(rows_loaded[u], 16)
                with sp.Fori(1, loops) as i:
                    for u in range(SETS):
                        sp.wait_ge(scattered[u], 16 * ST * i)
                        sp.dma_start(rows[:, u, :, 0:D],
                                     xf_blocks[bass.ds(SETS * i + u, 1)].rearrange("b p j f -> (b p) j f")
                                     ).then_inc(rows_loaded[u], 16)

            @block.vector
            def _(dve):
                def take(b, u):
                    nc.vector.tensor_copy(rows[:, u, :, D], m.token[:, bass.ds(b * ST, ST)])
                    nc.vector.tensor_copy(rows[:, u, :, D + 1], m.prob[:, bass.ds(b * ST, ST)])
                    nc.vector.tensor_copy(row_now[:, u, :], m.row[:, bass.ds(b * ST, ST)]).then_inc(row_ready[u], 1)

                for u in range(SETS):
                    take(u, u)
                with dve.Fori(1, loops) as i:
                    for u in range(SETS):
                        wait_apart(dve, scattered[u], 16 * ST * i, m.passed)
                        take(SETS * i + u, u)

            @block.gpsimd
            def _(pool):
                with pool.Fori(0, loops) as i:
                    for u in range(SETS):
                        pool.wait_ge(row_ready[u], i + 1)
                        pool.sem_inc(m.pool_passed, 1)
                        wait_apart(pool, rows_loaded[u], 16 * i + 16, m.pool_passed)
                        for j in range(ST):
                            nc.gpsimd.indirect_dma_start(
                                out=m.xe, out_offset=bass.IndirectOffsetOnAxis(ap=row_now[:, u, j:j + 1], axis=0),
                                in_=rows[:, u, j, :], in_offset=None).then_inc(scattered[u], 16)
                for u in range(SETS):
                    pool.wait_ge(scattered[u], 16 * ST * loops)
                    pool.sem_inc(m.pool_passed, 1)


def experts(nc, m):
    with ExitStack() as ctx:
        def sb(name, shape, dt=F32):
            return ctx.enter_context(nc.sbuf_tensor(name, shape, dt))

        sem = semaphores(nc, ctx)

        def ps(name, n):
            return ctx.enter_context(nc.psum_tensor(name, [P, BANK], F32))[:, 0:n]

        TT = TB // P
        w1 = [sb(f"w1_{u}", [P, KD, F]) for u in range(2)]
        w2 = [sb(f"w2_{u}", [P, FC, D]) for u in range(2)]
        b1 = [sb(f"b1_{u}", [P, FC]) for u in range(2)]
        b2 = [sb(f"b2_{u}", [P, D]) for u in range(2)]
        tokens = sb("tokens", [P, TT, XW])
        tokens_t = sb("tokens_t", [P, KD, TB])
        hidden = sb("e_hidden", [P, FC, TB])
        y = sb("y", [P, TT, D])
        scaled = sb("y_scaled", [P, TT, D])
        result = sb("y_result", [P, TT, D])
        x2 = sb("x2_of_tokens", [P, TT, D])
        finite = sb("finite", [P, TT, D], U8)
        nan = sb("nan", [P, TT, D], U8)
        zeros = sb("y_zeros", [P, TT, D])
        prob = sb("prob_now", [P, TT])
        none = sb("no_token", [P, TT])
        target = sb("target", [P, TT])
        target_i = sb("target_i", [P, TT], I32)
        spare_i = sb("spare_row_i", [P, TT], I32)
        spare_f = sb("spare_row_f", [P, TT])
        turn_ps = ps("e_turn_ps", KD * TB).rearrange("p (k n) -> p k n", k=KD)
        HB = 4
        hidden_ps = [ps(f"e_hidden_ps{f}", TB) for f in range(HB)]
        y_ps = [ps(f"y_ps{tt}", D) for tt in range(TT)]
        assert N + TB <= NP

        weights_loaded = [sem(f"weights_loaded{u}") for u in range(2)]
        tokens_loaded = sem("tokens_loaded")
        turned = sem("e_turned")
        tokens_t_ready = sem("tokens_t_ready")
        hidden_done = sem("e_hidden_done")
        by_act = sem("hidden_by_act")
        by_dve = sem("hidden_by_dve")
        y_done = sem("y_done")
        y_taken = sem("y_taken")
        ids_step = sem("ids_step")
        ids_taken = sem("ids_taken")
        target_ready = sem("target_ready")
        x2_gathered = sem("x2_gathered")
        y_scaled = sem("y_scaled_ready")
        masks = sem("masks")
        result_ready = sem("result_ready")
        out_scattered = sem("out_scattered")
        out_free = sem("out_free")
        setup = sem("experts_setup")

        def bounds(engine, e):
            return [engine.value_load(m.blocks[0:1, bass.ds(e, 1), k], min_val=0, max_val=NE * ROWS // TB)
                    for k in range(2)]

        def rows_of(of, e, n, first):
            at = (e * ROWS + (n - first) * TB).with_bounds(min_val=0, max_val=(NE * ROWS - TB))
            return of[bass.ds(at, TB), :].rearrange("(j p) f -> p j f", p=P)

        def blocks_of(engine, ii, u, body):
            e = 2 * ii + u
            first, end = bounds(engine, e)
            with engine.Fori(first, end) as n:
                body(e, u, ii, n, first)
            return end

        def each(engine, body):
            with engine.Fori(0, NE // 2) as ii:
                for u in range(2):
                    blocks_of(engine, ii, u, body)

        with nc.Block("experts") as block:
            @block.gpsimd
            def _(pool):
                def load(e, u):
                    one = bass.ds(e, 1)
                    pool.dma_start(w1[u][:, :, :], m.w_e1[one].rearrange("o (k p) f -> p (o k) f", p=P)
                                   ).then_inc(weights_loaded[u], 16)
                    pool.dma_start(w2[u][:, :, :], m.w_e2[one].rearrange("o (k p) f -> p (o k) f", p=P)
                                   ).then_inc(weights_loaded[u], 16)
                    pool.dma_start(b1[u][:, :], m.in_b_e1[:, one, :].rearrange("p o f -> p (o f)")
                                   ).then_inc(weights_loaded[u], 16)
                    pool.dma_start(b2[u][:, :], m.in_b_e2[one, :].to_broadcast([P, D])
                                   ).then_inc(weights_loaded[u], 16)

                def move(n):
                    wait_apart(pool, target_ready, n + 1, m.pool_passed)
                    for tt in range(TT):
                        nc.gpsimd.indirect_dma_start(
                            out=x2[:, tt, :], out_offset=None, in_=m.x2,
                            in_offset=bass.IndirectOffsetOnAxis(ap=target_i[:, tt:tt + 1], axis=0)
                        ).then_inc(x2_gathered, 16)
                    wait_apart(pool, result_ready, n + 1, m.pool_passed)
                    for tt in range(TT):
                        nc.gpsimd.indirect_dma_start(
                            out=m.out, out_offset=bass.IndirectOffsetOnAxis(ap=target_i[:, tt:tt + 1], axis=0),
                            in_=result[:, tt, :], in_offset=None).then_inc(out_scattered, 16)
                    pool.wait_ge(out_scattered, (n + 1) * (16 * TT))
                    pool.sem_inc(out_free, 1)

                for u in range(2):
                    load(u, u)
                nc.gpsimd.iota(spare_i[:, :], [[P, TT]], base=N + 1, channel_multiplier=1).then_inc(setup, 1)
                nc.gpsimd.memset(zeros[:, :, :], 0.0).then_inc(setup, 1)
                pool.sem_inc(out_free, 1)

                def move_all(ii, u):
                    return blocks_of(pool, ii, u, lambda e, u, ii, n, first: move(n))

                with pool.Fori(0, NE // 2 - 1) as ii:
                    for u in range(2):
                        end = move_all(ii, u)
                        wait_apart(pool, target_ready, end + 1, m.pool_passed)
                        load(2 * ii + (2 + u), u)
                for u in range(2):
                    end = move_all(NE // 2 - 1, u)
                move(end)

            @block.sync
            def _(sp):
                def load(e, u, ii, n, first):
                    sp.wait_ge(turned, n + 1)
                    wait_apart(sp, ids_taken, n + 1, m.sp_passed)
                    sp.dma_start(tokens[:, :, :], rows_of(m.xe, e, n, first)).then_inc(tokens_loaded, 16)

                each(sp, load)
                first, end = bounds(sp, NE - 1)
                sp.wait_ge(turned, end + 1)
                sp.wait_ge(ids_taken, end + 1)
                sp.dma_start(tokens[:, :, :], m.xe[0:TB, :].rearrange("(j p) f -> p j f", p=P)
                             ).then_inc(tokens_loaded, 16)
                wait_apart(sp, out_free, end + 2, m.sp_passed)

            @block.tensor
            def _(pe):
                def turn(n):
                    pe.wait_ge(tokens_loaded, 16 * n + 16)
                    for j in range(TT):
                        for h in range(KD):
                            last = nc.tensor.transpose(turn_ps[:, h, j * P:(j + 1) * P],
                                                       tokens[:, j, h * P:(h + 1) * P], m.ident[:, :])
                    last.then_inc(turned, 1)

                def block_of(e, u, ii, n, first):
                    pe.wait_ge(weights_loaded[u], 64 * ii + 64)
                    pe.wait_ge(tokens_t_ready, n + 1)
                    for f in range(FC):
                        if f >= HB:
                            pe.wait_ge(by_dve if f % 2 else by_act, n * (FC // 2) + ((f - HB) // 2 + 1))
                        for k in range(KD):
                            last = nc.tensor.matmul(hidden_ps[f % HB], w1[u][:, k, f * P:(f + 1) * P],
                                                    tokens_t[:, k, :], start=(k == 0), stop=(k == KD - 1))
                        last.then_inc(hidden_done, 1)
                    turn(n + 1)
                    pe.wait_ge(y_taken, n * TT + TT)
                    for tt in range(TT):
                        for f in range(FC):
                            if tt == 0 and f in (0, FC - 2):
                                have = (n * (FC // 2)) + (FC // 2 - 1 if f == 0 else FC // 2)
                                pe.wait_ge(by_act, have)
                                pe.wait_ge(by_dve, have)
                            last = nc.tensor.matmul(y_ps[tt], hidden[:, f, tt * P:(tt + 1) * P], w2[u][:, f, :],
                                                    start=(f == 0), stop=(f == FC - 1))
                        last.then_inc(y_done, 1)

                pe.sem_inc(turned, 1)
                turn(0)
                each(pe, block_of)

            @block.scalar
            def _(act):
                def copy(n):
                    act.wait_ge(turned, n + 2)
                    nc.scalar.copy(tokens_t[:, :, :], turn_ps[:, :, :]).then_inc(tokens_t_ready, 1)

                def block_of(e, u, ii, n, first):
                    for f in range(0, FC, 2):
                        act.wait_ge(hidden_done, n * FC + (f + 1))
                        nc.scalar.activation(hidden[:, f, :], hidden_ps[f % HB], ACT.Relu, bias=b1[u][:, f:f + 1]
                                             ).then_inc(by_act, 1)
                    copy(n + 1)

                copy(0)
                each(act, block_of)

            @block.vector
            def _(dve):
                def finish(n):
                    wait_apart(dve, y_scaled, (n + 1) * TT, m.passed)
                    now = result[:, :, :]
                    nc.vector.tensor_scalar(now, scaled[:, :, :], -1e4, 1e4, ALU.max, ALU.min)
                    nc.vector.tensor_scalar(finite[:, :, :], scaled[:, :, :], 0.0, 0.0, ALU.mult, ALU.is_equal)
                    nc.vector.tensor_tensor(nan[:, :, :], scaled[:, :, :], scaled[:, :, :],
                                            ALU.not_equal).then_inc(masks, 1)
                    wait_apart(dve, masks, 3 * n + 1, m.passed)
                    nc.vector.copy_predicated(now, finite[:, :, :], scaled[:, :, :]).then_inc(masks, 1)
                    wait_apart(dve, masks, 3 * n + 2, m.passed)
                    nc.vector.copy_predicated(now, nan[:, :, :], zeros[:, :, :]).then_inc(masks, 1)
                    dve.wait_ge(masks, 3 * n + 3)
                    dve.sem_inc(m.passed, 1)
                    dve.wait_ge(x2_gathered, 16 * TT * (n + 1))
                    nc.vector.tensor_tensor(now, now, x2[:, :, :], ALU.add).then_inc(result_ready, 1)

                def block_of(e, u, ii, n, first):
                    wait_apart(dve, tokens_loaded, 16 * n + 16, m.passed)
                    wait_apart(dve, y_scaled, (n + 1) * TT, m.passed)
                    nc.vector.scalar_tensor_tensor(none[:, :], tokens[:, :, D], 0.0, spare_f[:, :],
                                                   ALU.is_equal, ALU.mult).then_inc(ids_step, 1)
                    nc.vector.tensor_copy(prob[:, :], tokens[:, :, D + 1])
                    dve.wait_ge(ids_step, n + 1)
                    nc.vector.scalar_tensor_tensor(target[:, :], tokens[:, :, D], -1.0, none[:, :],
                                                   ALU.add, ALU.add).then_inc(ids_taken, 1)
                    for f in range(1, FC, 2):
                        dve.wait_ge(hidden_done, n * FC + (f + 1))
                        nc.vector.tensor_scalar(hidden[:, f, :], hidden_ps[f % HB], b1[u][:, f:f + 1], 0.0,
                                                ALU.add, ALU.max).then_inc(by_dve, 1)
                    finish(n)
                    for tt in range(TT):
                        dve.wait_ge(y_done, n * TT + (tt + 1))
                        nc.vector.tensor_tensor(y[:, tt, :], y_ps[tt], b2[u][:, :], ALU.add).then_inc(y_taken, 1)
                    for tt in range(TT):
                        dve.wait_ge(y_taken, (n + 1) * TT + (tt + 1))
                        last = nc.vector.tensor_scalar(scaled[:, tt, :], y[:, tt, :], prob[:, tt:tt + 1], None,
                                                       ALU.mult)
                        last.then_inc(y_scaled, 1)
                    wait_apart(dve, out_free, n + 2, m.passed)
                    wait_apart(dve, ids_taken, n + 2, m.passed)
                    nc.vector.tensor_copy(target_i[:, :], target[:, :]).then_inc(target_ready, 1)

                dve.sem_inc(y_taken, TT)
                dve.sem_inc(ids_taken, 1)
                dve.wait_ge(setup, 2)
                nc.vector.tensor_copy(spare_f[:, :], spare_i[:, :]).then_inc(setup, 1)
                nc.vector.memset(scaled[:, :, :], 0.0).then_inc(y_scaled, TT)
                dve.wait_ge(setup, 3)
                nc.vector.tensor_scalar(target_i[:, :], spare_f[:, :], -1.0, None, ALU.add).then_inc(target_ready, 1)
                each(dve, block_of)
                first, end = bounds(dve, NE - 1)
                finish(end)


def program(nc, ins, out, scratch):
    m = Memory()
    (m.x, m.in_src, m.in_dst, m.in_dst_rows, m.in_wgt, m.in_w_g1, m.in_b_g1, m.in_w_g2, m.in_b_g2,
     m.in_w_q, m.in_w_k, m.in_w_v, m.in_w_m, m.in_w_1, m.in_w_2, m.in_ln1_g, m.in_ln1_b, m.in_ln2_g, m.in_ln2_b,
     m.in_gate_w, m.in_gate_b, m.w_e1, m.in_b_e1, m.w_e2, m.in_b_e2) = ins
    m.out = out
    m.xn = scratch("xn", [NP + P, D], F32)
    m.h1 = scratch("h1", [NP, D], F32)
    m.mix = scratch("mix", [NP, D], F32)
    m.x2 = scratch("x2", [NP, D], F32)
    m.xe = scratch("xe", [TRASH + NP, XW], F32)
    m.xf = scratch("xf", [NP, D], F32)
    m.low_dram = scratch("low_dram", [TURNS, TURN], I32)
    m.more_dram = scratch("more_dram", [TURNS, 1], I32)

    with ExitStack() as ctx:
        def sb(name, shape, dt=F32):
            return ctx.enter_context(nc.sbuf_tensor(name, shape, dt))

        m.passed = ctx.enter_context(nc.semaphore("passed"))
        m.pool_passed = ctx.enter_context(nc.semaphore("pool_passed"))
        m.pe_passed = ctx.enter_context(nc.semaphore("pe_passed"))
        m.sp_passed = ctx.enter_context(nc.semaphore("sp_passed"))
        m.act_passed = ctx.enter_context(nc.semaphore("act_passed"))
        m.xe_zeroed = ctx.enter_context(nc.semaphore("xe_zeroed"))
        m.wgt = sb("wgt", [P, NCH + SLOTS])
        m.dst_rel = sb("dst_rel", [P, NCH + SLOTS])
        m.table = sb("table", [1, TURNS, TURN + 2], I32)
        m.cols = sb("cols", [P, WIN])
        m.eps = sb("eps", [P, 1])
        m.ident = sb("ident", [P, P])
        m.upto = sb("upto", [P, P])
        m.ones = sb("ones", [P, P])
        m.zeros = sb("zeros", [P, KD * KVS])
        m.valid = sb("valid", [P, NT])
        m.w_q = sb("w_q", [P, KD, D])
        m.w_m = sb("w_m", [P, KD, D])
        m.w_1 = sb("w_1", [P, 2 * KD, F1])
        m.w_2 = sb("w_2", [P, F1 // P, D])
        m.ln1_gh = sb("ln1_gh", [P, KD])
        m.ln2_gh = sb("ln2_gh", [P, D])
        m.ln1_b = sb("ln1_b", [P, KD])
        m.ln2_b = sb("ln2_b", [P, D])
        m.gate_w = sb("gate_w", [P, KD, NE])
        m.gate_b = sb("gate_b", [P, NE])
        m.blocks = sb("blocks", [1, NE, 2], I32)
        m.kv = sb("kv", [P, KD, KVW])
        m.logits = sb("logits", [P, NT, NE])
        m.row = sb("row_of", [P, NT], I32)
        m.token = sb("token", [P, NT])
        m.prob = sb("prob", [P, NT])
        prepare(nc, m)
        with ExitStack() as agg_ctx:
            m.agg = agg_ctx.enter_context(nc.sbuf_tensor("agg", [P, KD, AGG], F32))
            gather(nc, m, 1, m.xn, keys_values)
            dense_first(nc, m)
            gather(nc, m, 2, m.h1, attend)
            dense_second(nc, m)
        route(nc, m)
        scatter(nc, m)
        experts(nc, m)


def kernel(x, src, dst, edge_weight, L0_gnn_W1, L0_gnn_b1, L0_gnn_W2, L0_gnn_b2, L0_mix_Wq, L0_mix_Wk, L0_mix_Wv,
           L0_mix_Wm, L0_mix_W1, L0_mix_W2, L0_mix_g1, L0_mix_b1, L0_mix_g2, L0_mix_b2, L0_ffn_gate_w, L0_ffn_gate_b,
           L0_ffn_w1, L0_ffn_b1, L0_ffn_w2, L0_ffn_b2):
    import concourse.bacc as bacc
    from concourse.bass_utils import run_bass_kernel_spmd as run

    nc = bacc.Bacc("TRN2", target_bir_lowering=False, num_devices=1)

    def padded(a, n, value=0):
        a = np.asarray(a)
        return np.concatenate([a, np.full((n - a.shape[0],) + a.shape[1:], value, a.dtype)])

    def columns(a):
        return np.ascontiguousarray(a.reshape(NCH, P).T)

    dst_padded = padded(dst, NCH * P, N - 1)
    arrays = {
        "x": padded(x, NP),
        "src": padded(src, NCH * P).reshape(TURNS, SLOTS, P).transpose(0, 2, 1),
        "dst": columns(dst_padded),
        "dst_rows": dst_padded.reshape(TURNS, SLOTS * P),
        "edge_weight": columns(padded(edge_weight, NCH * P)),
        "gnn_W1": L0_gnn_W1, "gnn_b1": L0_gnn_b1, "gnn_W2": L0_gnn_W2, "gnn_b2": L0_gnn_b2,
        "mix_Wq": L0_mix_Wq, "mix_Wk": L0_mix_Wk, "mix_Wv": L0_mix_Wv, "mix_Wm": L0_mix_Wm,
        "mix_W1": L0_mix_W1, "mix_W2": L0_mix_W2,
        "mix_g1": np.asarray(L0_mix_g1).reshape(KD, P).T, "mix_b1": np.asarray(L0_mix_b1).reshape(KD, P).T,
        "mix_g2": L0_mix_g2, "mix_b2": L0_mix_b2,
        "gate_w": L0_ffn_gate_w, "gate_b": L0_ffn_gate_b,
        "ffn_w1": L0_ffn_w1, "ffn_b1": np.asarray(L0_ffn_b1).reshape(NE, FC, P).transpose(2, 0, 1),
        "ffn_w2": L0_ffn_w2, "ffn_b2": L0_ffn_b2,
    }
    arrays = {f"in_{k}": np.ascontiguousarray(v) for k, v in arrays.items()}
    ins = [nc.dram_tensor(k, v.shape, mybir.dt.from_np(v.dtype), kind="ExternalInput").ap() for k, v in arrays.items()]
    out = nc.dram_tensor("out", (NP, D), F32, kind="ExternalOutput").ap()

    def scratch(name, shape, dt):
        return nc.dram_tensor(name, shape, dt, kind=SCRATCH_KIND).ap()

    program(nc, ins, out, scratch)
    return run(nc, [arrays], core_ids=[0]).results[0]["out"][:N]


SCRATCH_KIND = "Internal"
```
